# Optimizing a Trainium2 kernel written in Bass

```python
import numpy as np
import jax
import jax.numpy as jnp

def _softmax(x, axis=-1):
    return jax.nn.softmax(x, axis=axis)

def _gelu(x):
    return jax.nn.gelu(x, approximate=True)

def _silu(x):
    return jax.nn.silu(x)

def _sigmoid(x):
    return jax.nn.sigmoid(x)

def _layernorm(x, axis=-1, eps=1e-05):
    m = jnp.mean(x, axis=axis, keepdims=True)
    v = jnp.var(x, axis=axis, keepdims=True)
    return (x - m) / jnp.sqrt(v + eps)

def _scatter_add(tgt, idx, src, axis=0):
    return tgt.at[idx].add(src)

def _segment_sum(src, seg, n):
    return jax.ops.segment_sum(src, seg, n)
kernel_name = 'mk_seq_postln_d1_jaxref_r8_736de9'

def setup_inputs(seed: int=0):
    np.random.seed(seed)
    _w = jnp.asarray

    def _L0_attn_setup():
        import math
        import jax, jax.numpy as jnp
        import numpy as np
        CHUNK = 32
        PROB_FLOOR = 0.02
        EPS = 1e-05

        def l2norm(x):
            return x * jax.lax.rsqrt(jnp.sum(x * x, -1, keepdims=True) + 1e-06)

        def causal_dwconv(x, w):
            B, L, C = x.shape
            K = w.shape[-1]
            y = jax.lax.conv_general_dilated(jnp.transpose(x, (0, 2, 1)), w[:, None, :], (1,), [(K - 1, 0)], feature_group_count=C)
            return jnp.transpose(y, (0, 2, 1))

        def delta_rule_chunkwise(q, k, v, beta, chunk=CHUNK):
            b, h, L, dk = q.shape
            dv = v.shape[-1]
            pad = -L % chunk
            if pad:
                q = jnp.pad(q, ((0, 0), (0, 0), (0, pad), (0, 0)))
                k = jnp.pad(k, ((0, 0), (0, 0), (0, pad), (0, 0)))
                v = jnp.pad(v, ((0, 0), (0, 0), (0, pad), (0, 0)))
                beta = jnp.pad(beta, ((0, 0), (0, 0), (0, pad)))
            Lp = L + pad
            n = Lp // chunk
            q = l2norm(q)
            k = l2norm(k)
            v = v * beta[..., None]
            kb = k * beta[..., None]
            r = lambda t: t.reshape(b, h, n, chunk, t.shape[-1])
            q, k, v, kb = (r(q), r(k), r(v), r(kb))
            i_ = jnp.arange(chunk)
            strict_lower = (i_[:, None] > i_[None, :]).astype(q.dtype)
            lower_incl = (i_[:, None] >= i_[None, :]).astype(q.dtype)
            inv = -(kb @ jnp.swapaxes(k, -1, -2)) * strict_lower
            for i in range(1, chunk):
                inv = inv.at[..., i, :].add(jnp.einsum('...j,...jk->...k', inv[..., i, :], inv))
            inv = inv + jnp.eye(chunk, dtype=q.dtype)
            u = inv @ v
            w = inv @ kb
            mv = lambda t: jnp.moveaxis(t, 2, 0)

            def step(S, xs):
                qi, ki, ui, wi = xs
                attn = qi @ jnp.swapaxes(ki, -1, -2) * lower_incl
                ui2 = ui - wi @ S
                oi = qi @ S + attn @ ui2
                return (S + jnp.swapaxes(ki, -1, -2) @ ui2, oi)
            S0 = jnp.zeros((b, h, dk, dv), q.dtype)
            S, outs = jax.lax.scan(step, S0, (mv(q), mv(k), mv(u), mv(w)))
            out = jnp.moveaxis(outs, 0, 2).reshape(b, h, Lp, dv)[:, :, :L]
            return (out, S)

        def head_stats(x):
            mean = x.mean(-1)
            var = ((x - mean[..., None]) ** 2).mean(-1)
            am = jnp.abs(x).mean(-1)
            l2 = jnp.sqrt((x * x).sum(-1))
            return jnp.stack([mean, var, am, l2], -1).mean(2)

        def rmsnorm(x, w):
            return x * jax.lax.rsqrt((x * x).mean(-1, keepdims=True) + EPS) * w
        key = jax.random.key(seed)
        ks = jax.random.split(key, 20)
        B, L, D, H = (2, 512, 128, 4)
        dv = D // H
        f32 = jnp.float32
        rn = lambda k, shape, s: (jax.random.normal(k, shape) * s).astype(f32)
        fir = lambda k, shape: rn(k, shape, 0.02).at[..., -1].add(1.0)
        return {'hidden_states': jax.random.normal(ks[0], (B, L, D), f32), 'Wq': rn(ks[1], (D, D), 0.02), 'Wk': rn(ks[2], (D, D), 0.02), 'Wv': rn(ks[3], (D, D), 0.02), 'Wb': rn(ks[4], (D, H), 0.02), 'wq_conv': fir(ks[5], (D, 4)), 'wk_conv': fir(ks[6], (D, 4)), 'wv_conv': fir(ks[7], (D, 4)), 'fir_long': fir(ks[8], (H, dv, 64)), 'fir_short': fir(ks[9], (H, dv, 5)), 'Wg1': rn(ks[10], (D + 16, D), 0.02), 'bg1': jnp.zeros((D,), f32), 'Wg2': rn(ks[11], (D, 4), 0.02), 'bg2': jnp.array([-0.5, -0.5, 1.0, 3.0], f32), 'logit_temp': jnp.array([math.log(math.expm1(0.7))], f32), 'conv_res_logit': jnp.full((H,), -1.0, f32), 'Wres': rn(ks[12], (D, H), 0.02), 'bres': jnp.full((H,), -1.0, f32), 'Wog1': rn(ks[13], (D + 8, D // 2), 0.02), 'bog1': jnp.zeros((D // 2,), f32), 'Wog2': rn(ks[14], (D // 2, 1), 0.02), 'bog2': jnp.full((1,), -1.0986122886681098, f32), 'norm_w': jnp.ones((dv,), f32), 'Wo': rn(ks[15], (D, D), 0.02)}
    _L0_attn_in = _L0_attn_setup()

    def _L0_ffn_setup():
        import jax, jax.numpy as jnp
        import numpy as np
        HIDDEN = 128
        NUM_EXPERTS = 8
        TOP_K = 2
        B, S = (2, 256)
        key = jax.random.key(seed)
        k1, k2, k3, k4, k5 = jax.random.split(key, 5)
        d, dff, E = (HIDDEN, 4 * HIDDEN, NUM_EXPERTS)
        x = jax.random.normal(k1, (B, S, d), dtype=jnp.float32)
        W1 = jax.random.normal(k2, (E, d, dff), dtype=jnp.float32) * (1.0 / np.sqrt(d))
        b1 = jax.random.normal(k3, (E, dff), dtype=jnp.float32) * 0.01
        W2 = jax.random.normal(k4, (E, dff, d), dtype=jnp.float32) * (1.0 / np.sqrt(dff))
        b2 = jax.random.normal(k5, (E, d), dtype=jnp.float32) * 0.01
        return {'x': x, 'W1': W1, 'b1': b1, 'W2': W2, 'b2': b2}
    _L0_ffn_in = _L0_ffn_setup()
    _d = {'L0_attn_hidden_states': _L0_attn_in['hidden_states'], 'L0_attn_Wq': _L0_attn_in['Wq'], 'L0_attn_Wk': _L0_attn_in['Wk'], 'L0_attn_Wv': _L0_attn_in['Wv'], 'L0_attn_Wb': _L0_attn_in['Wb'], 'L0_attn_wq_conv': _L0_attn_in['wq_conv'], 'L0_attn_wk_conv': _L0_attn_in['wk_conv'], 'L0_attn_wv_conv': _L0_attn_in['wv_conv'], 'L0_attn_fir_long': _L0_attn_in['fir_long'], 'L0_attn_fir_short': _L0_attn_in['fir_short'], 'L0_attn_Wg1': _L0_attn_in['Wg1'], 'L0_attn_bg1': _L0_attn_in['bg1'], 'L0_attn_Wg2': _L0_attn_in['Wg2'], 'L0_attn_bg2': _L0_attn_in['bg2'], 'L0_attn_logit_temp': _L0_attn_in['logit_temp'], 'L0_attn_conv_res_logit': _L0_attn_in['conv_res_logit'], 'L0_attn_Wres': _L0_attn_in['Wres'], 'L0_attn_bres': _L0_attn_in['bres'], 'L0_attn_Wog1': _L0_attn_in['Wog1'], 'L0_attn_bog1': _L0_attn_in['bog1'], 'L0_attn_Wog2': _L0_attn_in['Wog2'], 'L0_attn_bog2': _L0_attn_in['bog2'], 'L0_attn_norm_w': _L0_attn_in['norm_w'], 'L0_attn_Wo': _L0_attn_in['Wo'], 'L0_ffn_W1': _L0_ffn_in['W1'], 'L0_ffn_b1': _L0_ffn_in['b1'], 'L0_ffn_W2': _L0_ffn_in['W2'], 'L0_ffn_b2': _L0_ffn_in['b2']}
    _x0 = _d['L0_attn_hidden_states']
    _d['L0_attn_hidden_states'] = jax.random.normal(jax.random.fold_in(jax.random.key(seed), 1), (4, 512, 128), dtype=_x0.dtype)
    del _x0
    return _d

def reference(L0_attn_hidden_states, L0_attn_Wq, L0_attn_Wk, L0_attn_Wv, L0_attn_Wb, L0_attn_wq_conv, L0_attn_wk_conv, L0_attn_wv_conv, L0_attn_fir_long, L0_attn_fir_short, L0_attn_Wg1, L0_attn_bg1, L0_attn_Wg2, L0_attn_bg2, L0_attn_logit_temp, L0_attn_conv_res_logit, L0_attn_Wres, L0_attn_bres, L0_attn_Wog1, L0_attn_bog1, L0_attn_Wog2, L0_attn_bog2, L0_attn_norm_w, L0_attn_Wo, L0_ffn_W1, L0_ffn_b1, L0_ffn_W2, L0_ffn_b2):

    def _L0_attn_ref(hidden_states, Wq, Wk, Wv, Wb, wq_conv, wk_conv, wv_conv, fir_long, fir_short, Wg1, bg1, Wg2, bg2, logit_temp, conv_res_logit, Wres, bres, Wog1, bog1, Wog2, bog2, norm_w, Wo):
        import math
        import jax, jax.numpy as jnp
        import numpy as np
        CHUNK = 32
        PROB_FLOOR = 0.02
        EPS = 1e-05

        def l2norm(x):
            return x * jax.lax.rsqrt(jnp.sum(x * x, -1, keepdims=True) + 1e-06)

        def causal_dwconv(x, w):
            B, L, C = x.shape
            K = w.shape[-1]
            y = jax.lax.conv_general_dilated(jnp.transpose(x, (0, 2, 1)), w[:, None, :], (1,), [(K - 1, 0)], feature_group_count=C)
            return jnp.transpose(y, (0, 2, 1))

        def delta_rule_chunkwise(q, k, v, beta, chunk=CHUNK):
            b, h, L, dk = q.shape
            dv = v.shape[-1]
            pad = -L % chunk
            if pad:
                q = jnp.pad(q, ((0, 0), (0, 0), (0, pad), (0, 0)))
                k = jnp.pad(k, ((0, 0), (0, 0), (0, pad), (0, 0)))
                v = jnp.pad(v, ((0, 0), (0, 0), (0, pad), (0, 0)))
                beta = jnp.pad(beta, ((0, 0), (0, 0), (0, pad)))
            Lp = L + pad
            n = Lp // chunk
            q = l2norm(q)
            k = l2norm(k)
            v = v * beta[..., None]
            kb = k * beta[..., None]
            r = lambda t: t.reshape(b, h, n, chunk, t.shape[-1])
            q, k, v, kb = (r(q), r(k), r(v), r(kb))
            i_ = jnp.arange(chunk)
            strict_lower = (i_[:, None] > i_[None, :]).astype(q.dtype)
            lower_incl = (i_[:, None] >= i_[None, :]).astype(q.dtype)
            inv = -(kb @ jnp.swapaxes(k, -1, -2)) * strict_lower
            for i in range(1, chunk):
                inv = inv.at[..., i, :].add(jnp.einsum('...j,...jk->...k', inv[..., i, :], inv))
            inv = inv + jnp.eye(chunk, dtype=q.dtype)
            u = inv @ v
            w = inv @ kb
            mv = lambda t: jnp.moveaxis(t, 2, 0)

            def step(S, xs):
                qi, ki, ui, wi = xs
                attn = qi @ jnp.swapaxes(ki, -1, -2) * lower_incl
                ui2 = ui - wi @ S
                oi = qi @ S + attn @ ui2
                return (S + jnp.swapaxes(ki, -1, -2) @ ui2, oi)
            S0 = jnp.zeros((b, h, dk, dv), q.dtype)
            S, outs = jax.lax.scan(step, S0, (mv(q), mv(k), mv(u), mv(w)))
            out = jnp.moveaxis(outs, 0, 2).reshape(b, h, Lp, dv)[:, :, :L]
            return (out, S)

        def head_stats(x):
            mean = x.mean(-1)
            var = ((x - mean[..., None]) ** 2).mean(-1)
            am = jnp.abs(x).mean(-1)
            l2 = jnp.sqrt((x * x).sum(-1))
            return jnp.stack([mean, var, am, l2], -1).mean(2)

        def rmsnorm(x, w):
            return x * jax.lax.rsqrt((x * x).mean(-1, keepdims=True) + EPS) * w
        B, L, D = hidden_states.shape
        H = Wb.shape[-1]
        silu = jax.nn.silu
        q_in = silu(causal_dwconv(hidden_states @ Wq, wq_conv))
        k_in = silu(causal_dwconv(hidden_states @ Wk, wk_conv))
        v_in = silu(causal_dwconv(hidden_states @ Wv, wv_conv))
        dk = q_in.shape[-1] // H
        dv = v_in.shape[-1] // H
        q = q_in.reshape(B, L, H, dk)
        k = k_in.reshape(B, L, H, dk)
        v_direct = v_in.reshape(B, L, H, dv)
        beta = jax.nn.sigmoid(hidden_states @ Wb)
        do, S = delta_rule_chunkwise(jnp.transpose(q, (0, 2, 1, 3)), jnp.transpose(k, (0, 2, 1, 3)), jnp.transpose(v_direct, (0, 2, 1, 3)), jnp.transpose(beta, (0, 2, 1)))
        delta_out = jnp.transpose(do, (0, 2, 1, 3))
        local_long = causal_dwconv(v_in, fir_long.reshape(-1, fir_long.shape[-1])).reshape(B, L, H, dv)
        local_short = causal_dwconv(v_in, fir_short.reshape(-1, fir_short.shape[-1])).reshape(B, L, H, dv)
        stats = jnp.concatenate([head_stats(t) for t in (local_short, local_long, delta_out, v_direct)], -1)
        gate_in = jnp.concatenate([hidden_states, stats], -1)
        logits = (jax.nn.gelu(gate_in @ Wg1 + bg1, approximate=False) @ Wg2 + bg2) / jax.nn.softplus(logit_temp)
        p = jax.nn.softmax(logits, -1)
        p = jnp.clip(p, PROB_FLOOR, None)
        p = p / p.sum(-1, keepdims=True)
        pw = p[:, :, None, :]
        o = pw[..., 0:1] * local_short + pw[..., 1:2] * local_long + pw[..., 2:3] * delta_out + pw[..., 3:4] * v_direct
        res_gate = jax.nn.sigmoid(hidden_states @ Wres + bres)
        static = jax.nn.sigmoid(conv_res_logit)
        o = o + (static[None, None, :] * res_gate)[..., None] * local_short
        og_stats = jnp.concatenate([head_stats(o), head_stats(v_direct)], -1)
        og_in = jnp.concatenate([hidden_states, og_stats], -1)
        og = jax.nn.sigmoid(jax.nn.gelu(og_in @ Wog1 + bog1, approximate=False) @ Wog2 + bog2)
        o = o * og[:, :, :, None]
        o = rmsnorm(o, norm_w)
        return o.reshape(B, L, -1) @ Wo

    def _L0_ffn_ref(x, W1, b1, W2, b2):
        import jax, jax.numpy as jnp
        import numpy as np
        HIDDEN = 128
        NUM_EXPERTS = 8
        TOP_K = 2
        B, S = (2, 256)
        Bm, Sm, d = x.shape
        E = W1.shape[0]
        x_flat = x.reshape(-1, d)
        h = jnp.mod(x_flat[:, :TOP_K].sum(axis=1).astype(jnp.int32), E)
        sel = jnp.stack([h, jnp.mod(h + 1, E)], axis=1)

        def step(acc, params):
            e, W1e, b1e, W2e, b2e = params
            w = jnp.any(sel == e, axis=1).astype(x.dtype) / TOP_K
            y = jnp.maximum(x_flat @ W1e + b1e, 0.0) @ W2e + b2e
            return (acc + w[:, None] * y, None)
        init = jnp.zeros_like(x_flat)
        out_flat, _ = jax.lax.scan(step, init, (jnp.arange(E), W1, b1, W2, b2))
        return out_flat.reshape(Bm, Sm, d)
    x = L0_attn_hidden_states
    x = _layernorm(x + _L0_attn_ref(x, L0_attn_Wq, L0_attn_Wk, L0_attn_Wv, L0_attn_Wb, L0_attn_wq_conv, L0_attn_wk_conv, L0_attn_wv_conv, L0_attn_fir_long, L0_attn_fir_short, L0_attn_Wg1, L0_attn_bg1, L0_attn_Wg2, L0_attn_bg2, L0_attn_logit_temp, L0_attn_conv_res_logit, L0_attn_Wres, L0_attn_bres, L0_attn_Wog1, L0_attn_bog1, L0_attn_Wog2, L0_attn_bog2, L0_attn_norm_w, L0_attn_Wo), axis=-1)
    x = _layernorm(x + _L0_ffn_ref(x, L0_ffn_W1, L0_ffn_b1, L0_ffn_W2, L0_ffn_b2), axis=-1)
    return x

_drawn_inputs = setup_inputs


def setup_inputs(seed=0):
    import zlib

    import numpy as np

    out = dict(_drawn_inputs(seed))
    spreads = {'L0_attn_bg1': (0.0, 0.8),
     'L0_attn_conv_res_logit': (-1.0, 0.6),
     'L0_attn_bres': (-1.0, 0.6),
     'L0_attn_bog1': (0.0, 2.0),
     'L0_attn_norm_w': (1.0, 0.2)}
    factors = {'L0_attn_Wb': 8.0,
     'L0_attn_fir_long': 3.844,
     'L0_attn_Wg1': 8.0,
     'L0_attn_Wg2': 8.0,
     'L0_attn_Wres': 8.0,
     'L0_attn_Wog1': 21.555,
     'L0_attn_Wog2': 32.57,
     'L0_ffn_b1': 8.0,
     'L0_ffn_b2': 8.0}
    for name, (base, spread) in spreads.items():
        noise = np.random.default_rng([zlib.crc32(name.encode()), seed]).standard_normal(out[name].shape)
        drawn = base * np.exp(spread * noise) if base else spread * noise
        out[name] = jnp.asarray(drawn.astype(out[name].dtype))
    for name, factor in factors.items():
        out[name] = (out[name] * factor).astype(out[name].dtype)
    return out
```

```python
from contextlib import ExitStack

import numpy as np

import concourse.bass as bass
from concourse import mybir

F32 = mybir.dt.float32
I32 = mybir.dt.int32
ALU = mybir.AluOpType
ACT = mybir.ActivationFunctionType
AX = mybir.AxisListType

P = 128
B, L, D = 4, 512, 128
H = 4
Q = 32
C = L // Q
BC = B * C
TT = L // P
NT = B * TT
N = B * L
NE = 8
FF = 512
NF = FF // P
WIN = 3 * Q
EPS = 1e-5
L2_EPS = 1e-6
FLOOR = 0.02

C_ID, C_NSTRICT, C_UINCL, C_EYE, C_PAIR, C_STEP, C_VAL, C_TILE = 0, 128, 160, 192, 224, 256, 272, 304
C_ALL = C_TILE + NT
W_Q, W_K, W_V, W_G, W_O, W_OG, W_BR, W_G2, W_OG2, W_GS, W_OGS = 0, 128, 256, 384, 512, 640, 704, 832, 960, 1088, 1216
W_ALL = W_OGS + 64
V_CONV, V_BG1, V_BOG1, V_BG2, V_TEMP, V_BOG2, V_BRES, V_STATIC, V_NORM = 0, 12, 13, 14, 18, 19, 20, 21, 22
V_ALL = 23

PROJ = (2, 1, 0)
SRC_V, SRC_K, SRC_Q = 0, 1, 2
LEVELS = 4
ST_SHORT, ST_LONG, ST_V, ST_DELTA, ST_O = range(5)


def shape_constants():
    c = np.zeros((P, C_ALL), np.float32)
    i = np.arange(P)
    r, j = (i % Q)[:, None], np.arange(Q)[None, :]
    c[:, C_ID:C_ID + P] = np.eye(P)
    c[:, C_NSTRICT:C_NSTRICT + Q] = -(r > j).astype(np.float32)
    c[:, C_UINCL:C_UINCL + Q] = r <= j
    c[:, C_EYE:C_EYE + Q] = r == j
    c[:, C_PAIR:C_PAIR + Q] = (r // 2 == j // 2) & (r > j)
    c[:, C_STEP:C_STEP + 16] = np.arange(1, 17)
    c[:, C_VAL:C_VAL + 32] = np.arange(-16, 16)
    c[:, C_TILE:C_TILE + NT] = (i // NE)[:, None] == np.arange(NT)[None, :]
    m = np.zeros((P, LEVELS, Q), np.int32)
    for n in range(LEVELS):
        s = 2 << n
        m[:, n] = (r // (2 * s) == j // (2 * s)) & (r % (2 * s) >= s) & (j % (2 * s) < s)
    return c, m.reshape(P, LEVELS * Q)


def post_ln_block(nc, x, cst, lmask, wall, vecs, fir_l, fir_s, w1, b1, w2, b2, out):
    ctx = ExitStack()
    with ctx:
        def sb(name, shape, dt=F32):
            return ctx.enter_context(nc.sbuf_tensor(name, shape, dt))

        def sem(name):
            return ctx.enter_context(nc.semaphore(name))

        x_tok = sb("x_tok", [P, NT, D])
        xT = sb("xT", [P, N])
        qkT = sb("qkT", [P, 2, N])
        kT_raw = sb("kT_raw", [P, N])
        vT = sb("vT", [P, N])
        k_hc = sb("k_hc", [P, N])
        q_hc = sb("q_hc", [P, N])
        v_hc = sb("v_hc", [P, N])
        short = sb("short", [P, N])
        long = sb("long", [P, N])
        sqA = sb("sqA", [P, N])
        sqB = sb("sqB", [P, N])
        stats = sb("stats", [P, BC, Q])
        win = sb("win", [P, H, BC, Q])
        toep = sb("toep", [P, 2, Q * P])
        cst_s = sb("cst_s", [P, C_ALL])
        lmask_s = sb("lmask_s", [P, LEVELS, Q], I32)
        w_s = sb("w_s", [P, W_ALL])
        v_s = sb("v_s", [P, V_ALL])
        gate_hc = sb("gate_hc", [P, BC, Q])
        beta = sb("beta", [P, BC])
        sgate = sb("sgate", [P, BC])
        norm = sb("norm", [P, 2, BC])
        nrm1 = sb("nrm1", [P, 2, BC])
        raw = sb("raw", [P, 5, 3, BC])
        m1 = sb("m1", [P, 5, BC])
        m2 = sb("m2", [P, 5, BC])
        prob = sb("prob", [P, BC, 4])
        prob2 = sb("prob2", [P, BC, 4])
        row1 = sb("row1", [P, BC])
        row2 = sb("row2", [P, BC])
        row3 = sb("row3", [P, BC])
        coef = sb("coef", [P, BC])
        tmpv = sb("tmpv", [P, 8])
        epsv = sb("epsv", [P, 2])
        wexp = sb("wexp", [P, NT, NE])
        wcur = sb("wcur", [P, 2, NT])
        r_s = sb("r_s", [P, 6, NT])
        ge = sb("ge", [P, NT, 16])
        eq = sb("eq", [P, NT, 32])
        me = sb("me", [P, NT, NE])
        b2rep = sb("b2rep", [P, D])
        wT = sb("wT", [P, P])
        chain = sb("chain", [P, 2, 2 * Q])

        toep_flat = toep[:, :, :].rearrange("p a n -> p (a n)")
        win_flat = win[:, :, :, :].rearrange("p a b c -> p (a b c)")
        low = toep_flat[:, 0:N]
        lowT = toep_flat[:, N:2 * N]
        inv = toep_flat[:, 2 * N:3 * N]
        invT = toep_flat[:, 3 * N:4 * N]
        mid = win_flat[:, 0:N]
        attnT = win_flat[:, N:2 * N]
        state = win_flat[:, 2 * N:3 * N]
        delta = win_flat[:, 3 * N:4 * N]
        nbm = sqA[:, :]
        statsT = lowT
        hid = low
        o_hc = inv
        oT = invT
        mixA, mixB = mid, state
        x1 = v_hc[:, :].rearrange("p (n d) -> p n d", n=NT)
        dev = vT[:, :].rearrange("p (n d) -> p n d", n=NT)
        x1T = kT_raw
        hT = toep_flat.rearrange("p (k f n) -> p k f n", k=4, f=NF)
        wbuf1 = win_flat[:, 0:2 * FF].rearrange("p (k f) -> p k f", k=2)
        wbuf2 = win_flat[:, 2 * FF:4 * FF].rearrange("p (k c d) -> p k c d", k=2, c=NF)
        bbuf1 = sb("bbuf1", [P, 2, NF])
        b2big = k_hc[:, :].rearrange("p (n d) -> p n d", n=NT)

        ps = ctx.enter_context(nc.psum_tensor("ps", [P, 8, 512], F32))

        def hc(t):
            return t.rearrange("p (b c d) -> p b c d", b=B, c=C)

        def over(ap, shape):
            return ap.to_broadcast(shape)

        ident = cst_s[:, C_ID:C_ID + P]
        uincl = cst_s[:, C_UINCL:C_UINCL + Q].unsqueeze(1)
        nstrict = cst_s[:, C_NSTRICT:C_NSTRICT + Q].unsqueeze(1)
        eye = cst_s[:, C_EYE:C_EYE + Q].unsqueeze(1)
        pair = cst_s[:, C_PAIR:C_PAIR + Q].unsqueeze(1)
        FULL = [P, C, Q]

        x_in = [sem(f"x_in{b}") for b in range(B)]
        w_in, c_in, lm_in, v_in, f_in, b2_in = (
            sem(n) for n in ("w_in", "c_in", "lm_in", "v_in", "f_in", "b2_in"))
        w_even, w_odd = sem("w_even"), sem("w_odd")
        win_zero, win_in = sem("win_zero"), sem("win_in")
        eps_set, misc = sem("eps_set"), sem("misc")
        xt_psum, xt_done = sem("xt_psum"), sem("xt_done")
        proj_psum, tap3_done, taps_done, silu_done, hc_done = (
            sem(n) for n in ("proj_psum", "tap3_done", "taps_done", "silu_done", "hc_done"))
        tap2_done = sem("tap2_done")
        br_psum, br_hc, beta_done, res_done, sgate_done = (
            sem(n) for n in ("br_psum", "br_hc", "beta_done", "res_done", "sgate_done"))
        sq_done, ssq_done, nrm_sqrt, nrm_done, kn_done, knT_done = (
            sem(n) for n in ("sq_done", "ssq_done", "nrm_sqrt", "nrm_done", "kn_done", "knT_done"))
        nbm_done = sem("nbm_done")
        fir_psum, fir_done = sem("fir_psum"), sem("fir_done")
        gram_psum, low_done, attn_done, lowT_done = (sem(n) for n in ("gram_psum", "low_done", "attn_done", "lowT_done"))
        pair_done, inv_done, invT_done, tb_done = (sem(n) for n in ("pair_done", "inv_done", "invT_done", "tb_done"))
        lx_psum, lx_done, xlx_psum = sem("lx_psum"), sem("lx_done"), sem("xlx_psum")
        ks_psum, rhs_done, u_psum, u_done, ds_psum, s_done, o_psum = (
            sem(n) for n in ("ks_psum", "rhs_done", "u_psum", "u_done", "ds_psum", "s_done", "o_psum"))
        state0 = sem("state0")
        st_sq, st_red, st_small, st_m2, st_var, st_l2 = (
            sem(n) for n in ("st_sq", "st_red", "st_small", "st_m2", "st_var", "st_l2"))
        ws_scaled, wo_scaled = sem("ws_scaled"), sem("wo_scaled")
        soft_a, soft_b, soft_c = sem("soft_a"), sem("soft_b"), sem("soft_c")
        delta_done, stT_done, g_psum, g_done, lg_psum, lg_hc = (
            sem(n) for n in ("delta_done", "stT_done", "g_psum", "g_done", "lg_psum", "lg_hc"))
        sm, sm_exp = sem("sm"), sem("sm_exp")
        mix_d, mix_p = sem("mix_d"), sem("mix_p")
        og_sig, og_a, og_sqrt = sem("og_sig"), sem("og_a"), sem("og_sqrt")
        of_done, oT_done, wo_psum = sem("of_done"), sem("oT_done"), sem("wo_psum")
        ln_d, ln_sq, ln_sqrt = sem("ln_d"), sem("ln_sq"), sem("ln_sqrt")
        x1_done, x1t_psum, x1t_done = sem("x1_done"), sem("x1t_psum"), sem("x1t_done")
        rt, wexp_done, wt_psum, wt_done = sem("rt"), sem("wexp_done"), sem("wt_psum"), sem("wt_done")
        b2big_done, bias_psum = sem("b2big_done"), sem("bias_psum")
        wcur_done = sem("wcur_done")
        h_psum, h_done, y_psum, y_done = sem("h_psum"), sem("h_done"), sem("y_psum"), sem("y_done")
        fin_d, fin_sq, fin_sqrt, fin_done, out_done = (
            sem(n) for n in ("fin_d", "fin_sq", "fin_sqrt", "fin_done", "out_done"))

        block = ctx.enter_context(nc.Block())

        @block.sync
        def _(sp):
            xv = x.rearrange("(n p) d -> p n d", p=P)
            sp.dma_start(cst_s[:, :], cst).then_inc(c_in, 16)
            for b in range(B):
                sp.dma_start(x_tok[:, b * TT:(b + 1) * TT, :], xv[:, b * TT:(b + 1) * TT, :]).then_inc(x_in[b], 16)
                if b == 0:
                    sp.dma_start(w_s[:, :], wall).then_inc(w_in, 16)
                    sp.dma_start(v_s[:, :], vecs).then_inc(v_in, 16)
            sp.dma_start(lmask_s[:, :, :].rearrange("p a b -> p (a b)"), lmask).then_inc(lm_in, 16)
            for k, f in ((0, fir_l), (1, fir_s)):
                sp.dma_start(toep[0:WIN, k, :], f).then_inc(f_in, 16)
            sp.dma_start(b2rep[:, :], bass.AP(b2.tensor, 0, [[0, NT], [D, NE], [1, D]])).then_inc(b2_in, 16)
            sp.wait_ge(win_zero, 1)
            sp.wait_ge(hc_done, B)
            v4 = hc(v_hc[:, :])
            for h in range(H):
                for k in range(3):
                    dst = win[k * Q:(k + 1) * Q, h, :, :].rearrange("p (b c) d -> p b (c d)", b=B)
                    src = v4[h * Q:(h + 1) * Q, :, 0:C - 2 + k, :].rearrange("p b c d -> p b (c d)")
                    sp.dma_start(dst[:, :, (2 - k) * Q:C * Q], src).then_inc(win_in, 16)
            sp.wait_ge(of_done, B)
            sp.wait_ge(mix_d, 3 * B)
            with sp.Fori(0, NE // 2) as e2:
                for k, ready in ((0, w_even), (1, w_odd)):
                    sp.wait_ge(y_psum, 1 + e2 * (2 * B))
                    sp.dma_start(wbuf1[:, k, :], w1[bass.ds(e2 * 2 + k, 1), :, :].rearrange("e p f -> p (e f)")
                                 ).then_inc(ready, 16)
                    sp.dma_start(wbuf2[:, k, :, :], w2[bass.ds(e2 * 2 + k, 1), :, :].rearrange(
                        "e (c p) d -> p (e c) d", p=P)).then_inc(ready, 16)
                    sp.dma_start(bbuf1[:, k, :], b1[bass.ds(e2 * 2 + k, 1), :, :].rearrange("e p c -> p (e c)")
                                 ).then_inc(ready, 16)
            ov = out.rearrange("(n p) d -> p n d", p=P)
            for b in range(B):
                sp.wait_ge(fin_done, b + 1)
                sp.dma_start(ov[:, b * TT:(b + 1) * TT, :], x_tok[:, b * TT:(b + 1) * TT, :]).then_inc(out_done, 16)
            sp.wait_ge(out_done, 16 * B)

        @block.tensor
        def _(pe):
            k4, q4 = hc(qkT[:, 0, :]), hc(qkT[:, 1, :])
            kn4, low4, lowT4, inv4, invT4 = hc(k_hc[:, :]), hc(low), hc(lowT), hc(inv), hc(invT)
            mid4, attn4, state4 = hc(mid), hc(attnT), hc(state)

            def per_head(dst, lhsT, rhs, start=True, stop=True):
                for h in range(H):
                    s = slice(h * Q, (h + 1) * Q)
                    mm = nc.tensor.matmul(dst[s], lhsT[s], rhs[s], start=start, stop=stop)
                return mm

            pe.wait_ge(c_in, 16)
            for b in range(B):
                pe.wait_ge(x_in[b], 16)
                for t in range(TT):
                    mm = nc.tensor.transpose(ps[:, b, t * P:(t + 1) * P], x_tok[:, b * TT + t, :], ident)
                mm.then_inc(xt_psum, 1)
            pe.wait_ge(w_in, 16)
            for n in range(3 * B):
                s, b = divmod(n, B)
                if s == 0:
                    pe.wait_ge(xt_done, b + 1)
                else:
                    pe.wait_ge(taps_done, n - B + 1)
                w = (W_V, W_K, W_Q)[s]
                nc.tensor.matmul(ps[:, 4 + b, :], w_s[:, w:w + P], xT[:, b * L:(b + 1) * L],
                                 start=True, stop=True).then_inc(proj_psum, 1)
                if s == 0:
                    nc.tensor.matmul(ps[:, b, :], w_s[:, W_BR:W_BR + P], xT[:, b * L:(b + 1) * L],
                                     start=True, stop=True).then_inc(br_psum, 1)
            pe.wait_ge(f_in, 32)
            pe.wait_ge(win_in, 16 * 3 * H)
            pe.wait_ge(br_hc, B)
            for m in range(8):
                if m >= 4:
                    pe.wait_ge(fir_done, m - 3)
                for i in range(8):
                    d = (m % 4) * 8 + i
                    for h in range(H):
                        ch = h * Q + d
                        mm = nc.tensor.matmul(ps[h * Q:(h + 1) * Q, m % 4, i * BC:(i + 1) * BC],
                                              toep[0:WIN, m // 4, ch:Q * P:P], win[0:WIN, h, :, d],
                                              start=True, stop=True)
                mm.then_inc(fir_psum, 1)
            for b in range(B):
                pe.wait_ge(taps_done, 3 * B)
                pe.wait_ge(knT_done, b + 1)
                pe.wait_ge(silu_done, 2 * B + b + 1)
                if b >= 2:
                    pe.wait_ge(attn_done, b - 1)
                for c in range(C):
                    dst = ps[:, 4 + 2 * (b % 2) + c // 8, (c % 8) * 64:(c % 8) * 64 + 64]
                    both = qkT[:, :, (b * C + c) * Q:(b * C + c + 1) * Q]
                    mm = per_head(dst, k4[:, b, c, :], both)
                mm.then_inc(gram_psum, 1)
            for n in range(LEVELS):
                for b in range(B):
                    if n == 0:
                        pe.wait_ge(lowT_done, b + 1)
                        pe.wait_ge(pair_done, b + 1)
                        pe.wait_ge(fir_done, 8)
                    else:
                        pe.wait_ge(inv_done, n * B - B + b + 1)
                    for c in range(C):
                        mm = per_head(ps[:, b, c * Q:(c + 1) * Q], lowT4[:, b, c, :], inv4[:, b, c, :])
                    mm.then_inc(lx_psum, 1)
                for b in range(B):
                    pe.wait_ge(lx_done, n * B + b + 1)
                    pe.wait_ge(invT_done, n * B + b + 1)
                    if n == 0:
                        pe.wait_ge(attn_done, B)
                    for c in range(C):
                        mm = per_head(ps[:, 4 + b, c * Q:(c + 1) * Q], invT4[:, b, c, :], mid4[:, b, c, :])
                    mm.then_inc(xlx_psum, 1)
            pe.wait_ge(tb_done, B)
            pe.wait_ge(lx_done, LEVELS * B)

            def outputs(c, b):
                for h in range(H):
                    s = slice(h * Q, (h + 1) * Q)
                    dst = ps[s, 4 + b, c * Q:(c + 1) * Q]
                    if c > 0:
                        nc.tensor.matmul(dst, q4[s, b, c, :], state4[s, b, c, :], start=True, stop=False)
                    mm = nc.tensor.matmul(dst, attn4[s, b, c, :], mid4[s, b, c, :], start=(c == 0), stop=True)
                if c == C - 1:
                    mm.then_inc(o_psum, 1)

            for c in range(C):
                for g in range(2):
                    if c > 0:
                        pe.wait_ge(s_done, 2 * (c - 1) + g + 1)
                        for i in range(2):
                            b = 2 * g + i
                            mm = per_head(ps[:, g, i * Q:(i + 1) * Q], k4[:, b, c, :], state4[:, b, c, :])
                        mm.then_inc(ks_psum, 1)
                if c > 0:
                    outputs(c - 1, 0)
                    outputs(c - 1, 1)
                for g in range(2):
                    pe.wait_ge(rhs_done, 2 * c + g + 1)
                    for i in range(2):
                        b = 2 * g + i
                        mm = per_head(ps[:, g, 64 + i * Q:64 + (i + 1) * Q], invT4[:, b, c, :],
                                      chain[:, g, i * Q:(i + 1) * Q])
                    mm.then_inc(u_psum, 1)
                if c > 0:
                    outputs(c - 1, 2)
                    outputs(c - 1, 3)
                for g in range(2):
                    pe.wait_ge(u_done, 2 * c + g + 1)
                    if c < C - 1:
                        for i in range(2):
                            b = 2 * g + i
                            mm = per_head(ps[:, g, 128 + i * Q:128 + (i + 1) * Q], kn4[:, b, c, :],
                                          mid4[:, b, c, :])
                        mm.then_inc(ds_psum, 1)
            for b in range(B):
                outputs(C - 1, b)
            for r in range(2):
                wide = (P, 64)[r]
                wx, wst, w2_ = ((W_G, W_GS, W_G2), (W_OG, W_OGS, W_OG2))[r]
                pe.wait_ge(ws_scaled, 1)
                for b in range(B):
                    if r == 0:
                        pe.wait_ge(s_done, 2 * (C - 1))
                    pe.wait_ge(stT_done, r * B + b + 1)
                    if r == 1:
                        pe.wait_ge(g_done, b + 1)
                    nc.tensor.matmul(ps[0:wide, b, :], w_s[:, wx:wx + wide], xT[:, b * L:(b + 1) * L],
                                     start=True, stop=False)
                    nc.tensor.matmul(ps[0:wide, b, :], w_s[:, wst:wst + wide], statsT[:, b * L:(b + 1) * L],
                                     start=False, stop=True).then_inc(g_psum, 1)
                for b in range(B):
                    pe.wait_ge(g_done, r * B + b + 1)
                    if r == 0:
                        pe.wait_ge(delta_done, b + 1)
                    else:
                        pe.wait_ge(lg_hc, b + 1)
                    nc.tensor.matmul(ps[:, 4 + b, :], w_s[0:wide, w2_:w2_ + P], hid[0:wide, b * L:(b + 1) * L],
                                     start=True, stop=True).then_inc(lg_psum, 1)
            pe.wait_ge(wo_scaled, 1)
            for b in range(B):
                pe.wait_ge(oT_done, b + 1)
                pe.wait_ge(g_done, B + b + 1)
                for t in range(TT):
                    a = b * L + t * P
                    mm = nc.tensor.matmul(ps[:, b, t * P:(t + 1) * P], oT[:, a:a + P], w_s[:, W_O:W_O + P],
                                          start=True, stop=True)
                mm.then_inc(wo_psum, 1)
            pe.wait_ge(lg_hc, 2 * B)
            for b in range(B):
                pe.wait_ge(x1_done, b + 1)
                for t in range(TT):
                    mm = nc.tensor.transpose(ps[:, 4 + b, t * P:(t + 1) * P], x1[:, b * TT + t, :], ident)
                mm.then_inc(x1t_psum, 1)
            pe.wait_ge(wexp_done, 1)
            pe.wait_ge(ln_d, 4 * B)
            nc.tensor.transpose(ps[:, 3, 0:P], wexp[:, :, :].rearrange("p n e -> p (n e)"), ident).then_inc(wt_psum, 1)

            pe.wait_ge(wt_done, 1)
            pe.sem_inc(y_psum, 1)
            with pe.Fori(0, NE // 2) as e2:
                def down(k, b):
                    pe.wait_ge(h_done, 1 + e2 * (2 * B * NF) + (k * B + b + 1) * NF)
                    if k:
                        pe.wait_ge(y_done, 1 + e2 * (2 * B) + b + 1)
                    for t in range(TT):
                        for f in range(NF):
                            mm = nc.tensor.matmul(ps[:, 4 + b, t * P:(t + 1) * P], hT[:, b % 2, f, t * P:(t + 1) * P],
                                                  wbuf2[:, k, f, :], start=(f == 0), stop=(f == NF - 1))
                    mm.then_inc(y_psum, 1)

                pe.wait_ge(y_done, 1 + e2 * (2 * B))
                for k, ready in ((0, w_even), (1, w_odd)):
                    pe.wait_ge(ready, e2 * 48 + 48)
                    for b in range(B):
                        n = k * B + b
                        pe.wait_ge(x1t_done, b + 1)
                        for f in range(NF):
                            pe.wait_ge(h_done, 1 + e2 * (2 * B * NF) + ((n - 1) * NF + f + 1 if n else 0))
                            nc.tensor.matmul(ps[:, f, :], wbuf1[:, k, f * P:(f + 1) * P], x1T[:, b * L:(b + 1) * L],
                                             start=True, stop=True).then_inc(h_psum, 1)
                        if n >= 1:
                            down((n - 1) // B, (n - 1) % B)
                down(1, B - 1)
            pe.wait_ge(b2big_done, 1)
            pe.wait_ge(h_done, 1 + NE * B * NF)
            for b in range(B):
                nc.tensor.matmul(ps[:, b, :], wT[:, :], b2big[:, b * TT:(b + 1) * TT, :],
                                 start=True, stop=True).then_inc(bias_psum, 1)

        @block.scalar
        def _(act):
            srcs = (vT[:, :], kT_raw[:, :], qkT[:, 1, :])
            for b in range(B):
                act.wait_ge(xt_psum, b + 1)
                nc.scalar.copy(xT[:, b * L:(b + 1) * L], ps[:, b, :]).then_inc(xt_done, 1)
            act.wait_ge(v_in, 16)
            nc.scalar.activation(tmpv[:, 0:1], v_s[:, V_TEMP:V_TEMP + 1], ACT.Abs).then_inc(soft_a, 1)
            act.wait_ge(soft_a, 1)
            nc.scalar.activation(tmpv[:, 1:2], tmpv[:, 0:1], ACT.Exp, scale=-1.0).then_inc(soft_a, 1)
            act.wait_ge(soft_a, 2)
            nc.scalar.activation(tmpv[:, 2:3], tmpv[:, 1:2], ACT.Ln, bias=1.0).then_inc(soft_a, 1)
            for n in range(3 * B + 1):
                if n < 3 * B:
                    s, b = divmod(n, B)
                    act.wait_ge(proj_psum, n + 1)
                    c = V_CONV + 4 * s + 3
                    nc.scalar.activation(srcs[s][:, b * L:(b + 1) * L], ps[:, 4 + b, :], ACT.Copy,
                                         scale=v_s[:, c:c + 1]).then_inc(tap3_done, 1)
                if n >= 1:
                    s, b = divmod(n - 1, B)
                    act.wait_ge(taps_done, n)
                    y = srcs[s][:, b * L:(b + 1) * L]
                    nc.scalar.activation(y, y, ACT.Silu).then_inc(silu_done, 1)
            act.wait_ge(br_hc, B)
            nc.scalar.activation(beta[:, :], gate_hc[:, :, 0], ACT.Sigmoid).then_inc(beta_done, 1)
            nc.scalar.activation(row1[:, :], gate_hc[:, :, 1], ACT.Sigmoid,
                                 bias=v_s[:, V_BRES:V_BRES + 1]).then_inc(res_done, 1)
            nc.scalar.activation(tmpv[:, 3:4], v_s[:, V_STATIC:V_STATIC + 1], ACT.Sigmoid).then_inc(res_done, 1)
            act.wait_ge(ssq_done, 2 * B)
            act.wait_ge(eps_set, 2)
            nc.scalar.activation(nrm1[:, :, :], norm[:, :, :], ACT.Sqrt, bias=epsv[:, 0:1]).then_inc(nrm_sqrt, 1)
            for m in range(8):
                act.wait_ge(fir_psum, m + 1)
                dst = (long, short)[m // 4][:, :].rearrange("p (n d) -> p d n", d=Q)[:, (m % 4) * 8:(m % 4) * 8 + 8, :]
                nc.scalar.copy(dst, ps[:, m % 4, :].rearrange("p (d n) -> p d n", d=8)).then_inc(fir_done, 1)
            for n in range(LEVELS):
                for b in range(B):
                    act.wait_ge(lx_psum, n * B + b + 1)
                    nc.scalar.copy(mid[:, b * L:(b + 1) * L], ps[:, b, :]).then_inc(lx_done, 1)
                if n < 3:
                    if n == 0:
                        act.wait_ge(low_done, B)
                        act.wait_ge(fir_done, 8)
                    else:
                        act.wait_ge(st_red, 3 * n)
                    src = (short, long, v_hc)[n]
                    nc.scalar.activation(sqA[:, :], src[:, :], ACT.Square).then_inc(st_sq, 1)
            for c in range(C):
                for g in range(2):
                    act.wait_ge(u_psum, 2 * c + g + 1)
                    dst = hc(mid)[:, 2 * g:2 * g + 2, c, :]
                    nc.scalar.copy(dst, ps[:, g, 64:128].rearrange("p (b d) -> p b d", b=2)).then_inc(u_done, 1)
            act.wait_ge(st_red, 9)
            nc.scalar.activation(stats[:, :, 4 * 0 + 3:12:4].rearrange("p n s -> p s n"), raw[:, 0:3, 2, :],
                                 ACT.Sqrt).then_inc(st_l2, 1)
            for r in range(2):
                src = (delta, o_hc)[r]
                red = 9 + 3 * B * r
                for b in range(B):
                    act.wait_ge(delta_done, b + 1) if r == 0 else act.wait_ge(mix_d, 3 * (b + 1))
                    nc.scalar.activation(sqA[:, b * L:(b + 1) * L], src[:, b * L:(b + 1) * L],
                                         ACT.Square).then_inc(st_sq, 1)
                act.wait_ge(st_red, red + 3 * B)
                s = (ST_DELTA, ST_O)[r]
                nc.scalar.activation(stats[:, :, 4 * s + 3], raw[:, s, 2, :], ACT.Sqrt).then_inc(st_l2, 1)
                wide, col = ((P, V_BG1), (64, V_BOG1))[r]
                for b in range(B):
                    act.wait_ge(g_psum, r * B + b + 1)
                    if r == 1:
                        act.wait_ge(lg_psum, b + 1)
                    nc.scalar.activation(hid[0:wide, b * L:(b + 1) * L], ps[0:wide, b, :], ACT.Gelu,
                                         bias=v_s[0:wide, col:col + 1]).then_inc(g_done, 1)
                if r == 0:
                    act.wait_ge(sm, 3)
                    nc.scalar.activation(prob2[:, :, :], prob[:, :, :], ACT.Exp).then_inc(sm_exp, 1)
            act.wait_ge(lg_hc, 2 * B)
            nc.scalar.activation(row1[:, :], gate_hc[:, :, 0], ACT.Sigmoid,
                                 bias=v_s[:, V_BOG2:V_BOG2 + 1]).then_inc(og_sig, 1)
            act.wait_ge(og_a, 2)
            nc.scalar.activation(row3[:, :], row2[:, :], ACT.Sqrt, bias=epsv[:, 1:2]).then_inc(og_sqrt, 1)
            for b in range(B):
                act.wait_ge(ln_d, 4 * b + 3)
                t = slice(b * TT, (b + 1) * TT)
                nc.scalar.activation(sqA[:, b * L:(b + 1) * L].rearrange("p (n d) -> p n d", n=TT), dev[:, t, :],
                                     ACT.Square).then_inc(ln_sq, 1)
                act.wait_ge(ln_d, 4 * b + 4)
                nc.scalar.activation(r_s[:, 2, t], r_s[:, 1, t], ACT.Sqrt, bias=epsv[:, 1:2],
                                     scale=1.0 / D).then_inc(ln_sqrt, 1)
            for b in range(B):
                act.wait_ge(x1t_psum, b + 1)
                nc.scalar.copy(x1T[:, b * L:(b + 1) * L], ps[:, 4 + b, :]).then_inc(x1t_done, 1)
            act.wait_ge(wt_psum, 1)
            nc.scalar.copy(wT[:, :], ps[:, 3, 0:P]).then_inc(wt_done, 1)
            act.sem_inc(h_done, 1)
            with act.Fori(0, NE // 2) as e2:
                for k, ready in ((0, w_even), (1, w_odd)):
                    act.wait_ge(ready, e2 * 48 + 48)
                    for b in range(B):
                        n = k * B + b
                        if n >= 2:
                            act.wait_ge(y_psum, 1 + e2 * (2 * B) + n - 1)
                        else:
                            act.wait_ge(y_psum, 1 + e2 * (2 * B))
                        for f in range(NF):
                            act.wait_ge(h_psum, e2 * (2 * B * NF) + n * NF + f + 1)
                            nc.scalar.activation(hT[:, b % 2, f, :], ps[:, f, :], ACT.Relu,
                                                 bias=bbuf1[:, k, f:f + 1]).then_inc(h_done, 1)
            for b in range(B):
                act.wait_ge(fin_d, 3 * b + 2)
                t = slice(b * TT, (b + 1) * TT)
                nc.scalar.activation(sqA[:, b * L:(b + 1) * L].rearrange("p (n d) -> p n d", n=TT), dev[:, t, :],
                                     ACT.Square).then_inc(fin_sq, 1)
                act.wait_ge(fin_d, 3 * b + 3)
                nc.scalar.activation(r_s[:, 2, t], r_s[:, 1, t], ACT.Sqrt, bias=epsv[:, 1:2],
                                     scale=1.0 / D).then_inc(fin_sqrt, 1)

        @block.vector
        def _(dve):
            V = nc.vector
            srcs = (vT[:, :], kT_raw[:, :], qkT[:, 1, :])
            hcs = (v_hc, k_hc, q_hc)

            def to_hc(n):
                s, b = divmod(n, B)
                dve.wait_ge(silu_done, n + 1)
                V.transpose(hcs[s][:, b * L:(b + 1) * L], srcs[s][:, b * L:(b + 1) * L]).then_inc(hc_done, 1)

            dve.wait_ge(v_in, 16)
            for n in range(3 * B):
                s, b = divmod(n, B)
                dve.wait_ge(tap3_done, n + 1)
                for k in range(1, 4):
                    y = srcs[s][:, b * L + k:(b + 1) * L]
                    c = V_CONV + 4 * s + 3 - k
                    if k > 1:
                        dve.wait_ge(tap2_done, 2 * n + k - 1)
                    V.scalar_tensor_tensor(out=y, in0=ps[:, 4 + b, 0:L - k], scalar=v_s[:, c:c + 1], in1=y,
                                           op0=ALU.mult, op1=ALU.add).then_inc(taps_done if k == 3 else tap2_done, 1)
                if n >= 2:
                    to_hc(n - 2)
                if n == B:
                    for i in range(B):
                        dve.wait_ge(br_psum, i + 1)
                        V.transpose(gate_hc[:, i * C:(i + 1) * C, :].rearrange("p a b -> p (a b)"),
                                    ps[:, i, :]).then_inc(br_hc, 1)
            to_hc(3 * B - 2)
            to_hc(3 * B - 1)
            dve.wait_ge(soft_a, 3)
            V.tensor_scalar(tmpv[:, 4:5], v_s[:, V_TEMP:V_TEMP + 1], 0.0, tmpv[:, 2:3], ALU.max,
                            ALU.add).then_inc(soft_b, 1)
            dve.wait_ge(soft_b, 1)
            V.reciprocal(tmpv[:, 5:6], tmpv[:, 4:5]).then_inc(soft_c, 1)
            dve.wait_ge(res_done, 2)
            V.tensor_scalar(sgate[:, :], row1[:, :], tmpv[:, 3:4], None, ALU.mult).then_inc(sgate_done, 1)
            for i in range(2 * B):
                s, b = divmod(i, B)
                dve.wait_ge(sq_done, i + 1)
                V.tensor_reduce(norm[:, s, b * C:(b + 1) * C], hc((sqA, sqB)[s][:, :])[:, b, :, :], AX.X,
                                ALU.add).then_inc(ssq_done, 1)
            dve.wait_ge(nrm_sqrt, 1)
            V.reciprocal(norm[:, :, :], nrm1[:, :, :]).then_inc(nrm_done, 1)
            dve.wait_ge(nrm_done, 1)
            dve.wait_ge(hc_done, 3 * B)
            for b in range(B):
                k = hc(k_hc[:, :])[:, b, :, :]
                V.tensor_tensor(k, k, over(norm[:, 0, b * C:(b + 1) * C].unsqueeze(2), FULL),
                                ALU.mult).then_inc(kn_done, 1)
                dve.wait_ge(kn_done, b + 1)
                V.transpose(qkT[:, 0, b * L:(b + 1) * L], k_hc[:, b * L:(b + 1) * L]).then_inc(knT_done, 1)
            dve.wait_ge(fir_psum, 8)
            for b in range(B):
                dve.wait_ge(gram_psum, b + 1)
                dve.wait_ge(nbm_done, b + 1)
                g = ps[:, 4 + 2 * (b % 2):6 + 2 * (b % 2), :].rearrange("p k (c x) -> p (k c) x", x=2 * Q)
                V.tensor_tensor(hc(low)[:, b, :, :], g[:, :, 0:Q], hc(nbm)[:, b, :, :], ALU.mult).then_inc(low_done, 1)
                V.tensor_tensor(hc(attnT)[:, b, :, :], g[:, :, Q:2 * Q], over(uincl, FULL),
                                ALU.mult).then_inc(attn_done, 1)
                dve.wait_ge(low_done, b + 1)
                V.transpose(lowT[:, b * L:(b + 1) * L], low[:, b * L:(b + 1) * L]).then_inc(lowT_done, 1)
            for b in range(B):
                dve.wait_ge(pair_done, b + 1)
                V.transpose(invT[:, b * L:(b + 1) * L], inv[:, b * L:(b + 1) * L]).then_inc(invT_done, 1)

            def sums(src, squares, s, b0, b1, count):
                cs = slice(b0 * C, b1 * C)
                v = src.rearrange("p (n d) -> p n d", d=Q)[:, cs, :]
                V.tensor_reduce(raw[:, s, 0, cs], v, AX.X, ALU.add).then_inc(st_red, 1)
                V.tensor_reduce(raw[:, s, 1, cs], v, AX.X, ALU.add, apply_absolute_value=True).then_inc(st_red, 1)
                dve.wait_ge(st_sq, count)
                V.tensor_reduce(raw[:, s, 2, cs], squares.rearrange("p (n d) -> p n d", d=Q)[:, cs, :], AX.X,
                                ALU.add).then_inc(st_red, 1)

            dve.wait_ge(lm_in, 16)
            for n in range(LEVELS):
                for b in range(B):
                    dve.wait_ge(xlx_psum, n * B + b + 1)
                    x_ = hc(inv)[:, b, :, :]
                    V.copy_predicated(x_, over(lmask_s[:, n, :].unsqueeze(1), FULL),
                                      ps[:, 4 + b, :].rearrange("p (c d) -> p c d", c=C)).then_inc(inv_done, 1)
                    dve.wait_ge(inv_done, n * B + b + 1)
                    V.transpose(invT[:, b * L:(b + 1) * L], inv[:, b * L:(b + 1) * L]).then_inc(invT_done, 1)
                    if n == LEVELS - 1:
                        dve.wait_ge(invT_done, (n + 1) * B + b + 1)
                        t = hc(invT)[:, b, :, :]
                        V.tensor_tensor(t, t, over(beta[:, b * C:(b + 1) * C].unsqueeze(2), FULL),
                                        ALU.mult).then_inc(tb_done, 1)
                if n < 3:
                    sums((short, long, v_hc)[n][:, :], sqA[:, :], n, 0, B, n + 1)
            st4, v4 = hc(state), hc(v_hc[:, :])
            for c in range(C):
                for g in range(2):
                    bs = slice(2 * g, 2 * g + 2)
                    r_ = chain[:, g, :].rearrange("p (b d) -> p b d", b=2)
                    if c == 0:
                        V.tensor_copy(r_, v4[:, bs, c, :]).then_inc(rhs_done, 1)
                    else:
                        dve.wait_ge(ks_psum, 2 * (c - 1) + g + 1)
                        V.tensor_tensor(r_, v4[:, bs, c, :], ps[:, g, 0:64].rearrange("p (b d) -> p b d", b=2),
                                        ALU.subtract).then_inc(rhs_done, 1)
                if c < C - 1:
                    for g in range(2):
                        bs = slice(2 * g, 2 * g + 2)
                        dve.wait_ge(ds_psum, 2 * c + g + 1)
                        d_ = ps[:, g, 128:192].rearrange("p (b d) -> p b d", b=2)
                        if c == 0:
                            V.tensor_copy(st4[:, bs, 1, :], d_).then_inc(s_done, 1)
                        else:
                            dve.wait_ge(s_done, 2 * (c - 1) + g + 1)
                            V.tensor_tensor(st4[:, bs, c + 1, :], st4[:, bs, c, :], d_, ALU.add).then_inc(s_done, 1)

            def small_stats(s0, s1, k):
                n = s1 - s0
                slot = stats[:, :, 4 * s0:4 * s1].rearrange("p n (s k) -> p k s n", k=4)
                V.tensor_scalar(slot[:, 0], raw[:, s0:s1, 0, :], 1.0 / Q, None, ALU.mult).then_inc(st_small, 1)
                V.tensor_scalar(slot[:, 2], raw[:, s0:s1, 1, :], 1.0 / Q, None, ALU.mult).then_inc(st_small, 1)
                V.tensor_scalar(m1[:, s0:s1, :], raw[:, s0:s1, 0, :], 1.0 / Q, None, ALU.mult).then_inc(st_small, 1)
                dve.wait_ge(st_small, 3 * k + 3)
                V.tensor_tensor(m2[:, s0:s1, :], m1[:, s0:s1, :], m1[:, s0:s1, :], ALU.mult).then_inc(st_m2, 1)
                dve.wait_ge(st_m2, k + 1)
                for s in range(s0, s1):
                    V.scalar_tensor_tensor(out=stats[:, :, 4 * s + 1], in0=raw[:, s, 2, :], scalar=1.0 / Q,
                                           in1=m2[:, s, :], op0=ALU.mult, op1=ALU.subtract).then_inc(st_var, 1)

            dve.wait_ge(st_red, 9)
            dve.wait_ge(misc, 1)
            small_stats(0, 3, 0)

            def gate_round(r):
                s = (ST_DELTA, ST_O)[r]
                dve.wait_ge(st_red, 9 + 3 * B * (r + 1))
                small_stats(s, s + 1, r + 1)
                dve.wait_ge(st_var, 4 + r)
                dve.wait_ge(st_l2, 2 + r)
                for b in range(B):
                    if r == 1:
                        dve.wait_ge(g_psum, b + 1)
                    V.transpose(statsT[:, b * L:(b + 1) * L], stats[:, b * C:(b + 1) * C, :].rearrange(
                        "p a b -> p (a b)")).then_inc(stT_done, 1)
                for b in range(B):
                    dve.wait_ge(lg_psum, r * B + b + 1)
                    V.transpose(gate_hc[:, b * C:(b + 1) * C, :].rearrange("p a b -> p (a b)"),
                                ps[:, 4 + b, :]).then_inc(lg_hc, 1)

            for b in range(B):
                dve.wait_ge(o_psum, b + 1)
                V.tensor_tensor(hc(delta)[:, b, :, :], ps[:, 4 + b, :].rearrange("p (c d) -> p c d", c=C),
                                over(norm[:, 1, b * C:(b + 1) * C].unsqueeze(2), FULL), ALU.mult).then_inc(delta_done, 1)
            for b in range(B):
                dve.wait_ge(delta_done, b + 1)
                sums(delta, sqA[:, :], ST_DELTA, b, b + 1, 3 + b + 1)
            gate_round(0)
            count = [0]

            def step(i):
                count[0] += 1
                i.then_inc(sm, 1)
                dve.wait_ge(sm, count[0])

            W4 = [P, BC, 4]
            dve.wait_ge(lg_hc, B)
            dve.wait_ge(soft_c, 1)
            step(V.tensor_tensor(prob2[:, :, :], gate_hc[:, :, 0:4],
                                 over(v_s[:, V_BG2:V_BG2 + 4].unsqueeze(1), W4), ALU.add))
            step(V.tensor_reduce(row1[:, :], prob2[:, :, :], AX.X, ALU.max))
            V.tensor_tensor(prob2[:, :, :], prob2[:, :, :], over(row1[:, :].unsqueeze(2), W4),
                            ALU.subtract).then_inc(soft_c, 1)
            dve.wait_ge(soft_c, 2)
            step(V.tensor_scalar(prob[:, :, :], prob2[:, :, :], tmpv[:, 5:6], None, ALU.mult))
            dve.wait_ge(sm_exp, 1)
            step(V.tensor_reduce(row1[:, :], prob2[:, :, :], AX.X, ALU.add))
            step(V.reciprocal(row2[:, :], row1[:, :]))
            step(V.tensor_tensor(prob[:, :, :], prob2[:, :, :], over(row2[:, :].unsqueeze(2), W4), ALU.mult))
            step(V.tensor_scalar(prob2[:, :, :], prob[:, :, :], FLOOR, None, ALU.max))
            step(V.tensor_reduce(row1[:, :], prob2[:, :, :], AX.X, ALU.add))
            step(V.reciprocal(row2[:, :], row1[:, :]))
            step(V.tensor_tensor(prob[:, :, :], prob2[:, :, :], over(row2[:, :].unsqueeze(2), W4), ALU.mult))
            dve.wait_ge(sgate_done, 1)
            step(V.tensor_tensor(coef[:, :], prob[:, :, 0], sgate[:, :], ALU.add))
            for b in range(B):
                cs = slice(b * C, (b + 1) * C)
                V.tensor_tensor(hc(o_hc)[:, b, :, :], hc(short[:, :])[:, b, :, :],
                                over(coef[:, cs].unsqueeze(2), FULL), ALU.mult).then_inc(mix_d, 1)
                V.tensor_tensor(hc(delta)[:, b, :, :], hc(delta)[:, b, :, :],
                                over(prob[:, cs, 2].unsqueeze(2), FULL), ALU.mult).then_inc(soft_b, 1)
                dve.wait_ge(mix_d, 3 * b + 1)
                dve.wait_ge(soft_b, b + 2)
                V.tensor_tensor(o_hc[:, b * L:(b + 1) * L], o_hc[:, b * L:(b + 1) * L],
                                delta[:, b * L:(b + 1) * L], ALU.add).then_inc(mix_d, 1)
                dve.wait_ge(mix_d, 3 * b + 2)
                dve.wait_ge(mix_p, 3 * (b + 1))
                V.tensor_tensor(o_hc[:, b * L:(b + 1) * L], o_hc[:, b * L:(b + 1) * L],
                                mixA[:, b * L:(b + 1) * L], ALU.add).then_inc(mix_d, 1)
                dve.wait_ge(mix_d, 3 * b + 3)
                sums(o_hc, sqA[:, :], ST_O, b, b + 1, 3 + B + b + 1)
            gate_round(1)
            dve.wait_ge(og_sig, 1)
            V.tensor_tensor(row3[:, :], row1[:, :], row1[:, :], ALU.mult).then_inc(og_a, 1)
            dve.wait_ge(og_a, 1)
            V.scalar_tensor_tensor(out=row2[:, :], in0=raw[:, ST_O, 2, :], scalar=1.0 / Q, in1=row3[:, :],
                                   op0=ALU.mult, op1=ALU.mult).then_inc(og_a, 1)
            dve.wait_ge(og_sqrt, 1)
            V.reciprocal(row2[:, :], row3[:, :]).then_inc(og_a, 1)
            dve.wait_ge(og_a, 3)
            V.tensor_tensor(coef[:, :], row1[:, :], row2[:, :], ALU.mult).then_inc(og_a, 1)
            dve.wait_ge(og_a, 4)
            for b in range(B):
                o = hc(o_hc)[:, b, :, :]
                V.tensor_tensor(o, o, over(coef[:, b * C:(b + 1) * C].unsqueeze(2), FULL), ALU.mult).then_inc(of_done, 1)
                dve.wait_ge(of_done, b + 1)
                V.transpose(oT[:, b * L:(b + 1) * L], o_hc[:, b * L:(b + 1) * L]).then_inc(oT_done, 1)

            T4 = [P, TT, D]
            for b in range(B):
                t = slice(b * TT, (b + 1) * TT)
                dve.wait_ge(wo_psum, b + 1)
                V.tensor_tensor(x_tok[:, t, :], x_tok[:, t, :], ps[:, b, :].rearrange("p (n d) -> p n d", n=TT),
                                ALU.add).then_inc(ln_d, 1)
                dve.wait_ge(ln_d, 4 * b + 1)
                V.tensor_reduce(r_s[:, 0, t], x_tok[:, t, :], AX.X, ALU.add).then_inc(ln_d, 1)
                dve.wait_ge(ln_d, 4 * b + 2)
                V.tensor_scalar(r_s[:, 0, t], r_s[:, 0, t], 1.0 / D, None, ALU.mult).then_inc(rt, 1)
                dve.wait_ge(rt, 2 * b + 1)
                V.tensor_tensor(dev[:, t, :], x_tok[:, t, :], over(r_s[:, 0, t].unsqueeze(2), T4),
                                ALU.subtract).then_inc(ln_d, 1)
                dve.wait_ge(ln_sq, b + 1)
                V.tensor_reduce(r_s[:, 1, t], sqA[:, b * L:(b + 1) * L].rearrange("p (n d) -> p n d", n=TT), AX.X,
                                ALU.add).then_inc(ln_d, 1)
                dve.wait_ge(ln_sqrt, b + 1)
                V.reciprocal(r_s[:, 3, t], r_s[:, 2, t]).then_inc(rt, 1)
                dve.wait_ge(rt, 2 * b + 2)
                V.tensor_tensor(x1[:, t, :], dev[:, t, :], over(r_s[:, 3, t].unsqueeze(2), T4),
                                ALU.mult).then_inc(x1_done, 1)
            count[0] = 2 * B

            def hop(i):
                count[0] += 1
                i.then_inc(rt, 1)
                dve.wait_ge(rt, count[0])

            dve.wait_ge(x1_done, B)
            hop(V.tensor_tensor(r_s[:, 0, :], x1[:, :, 0], x1[:, :, 1], ALU.add))
            hop(V.tensor_scalar(r_s[:, 1, :], r_s[:, 0, :], -1.0, None, ALU.mult))
            hop(V.tensor_tensor(r_s[:, 2, :], r_s[:, 0, :], r_s[:, 1, :], ALU.max))
            hop(V.tensor_tensor(ge[:, :, :], over(r_s[:, 2, :].unsqueeze(2), [P, NT, 16]),
                                over(cst_s[:, C_STEP:C_STEP + 16].unsqueeze(1), [P, NT, 16]), ALU.is_ge))
            hop(V.tensor_reduce(r_s[:, 3, :], ge[:, :, :], AX.X, ALU.add))
            hop(V.tensor_scalar(r_s[:, 4, :], r_s[:, 0, :], 0.0, 2.0, ALU.is_ge, ALU.mult))
            hop(V.tensor_scalar(r_s[:, 5, :], r_s[:, 4, :], -1.0, None, ALU.add))
            hop(V.tensor_tensor(r_s[:, 4, :], r_s[:, 3, :], r_s[:, 5, :], ALU.mult))
            hop(V.tensor_tensor(eq[:, :, :], over(r_s[:, 4, :].unsqueeze(2), [P, NT, 32]),
                                over(cst_s[:, C_VAL:C_VAL + 32].unsqueeze(1), [P, NT, 32]), ALU.is_equal))
            hop(V.tensor_reduce(me[:, :, :], eq[:, :, :].rearrange("p n (g e) -> p n e g", e=NE), AX.X, ALU.add))
            hop(V.tensor_tensor(wexp[:, :, 1:NE], me[:, :, 1:NE], me[:, :, 0:NE - 1], ALU.add))
            hop(V.tensor_tensor(wexp[:, :, 0:1], me[:, :, 0:1], me[:, :, NE - 1:NE], ALU.add))
            V.tensor_scalar(wexp[:, :, :], wexp[:, :, :], 0.5, None, ALU.mult).then_inc(wexp_done, 1)
            dve.wait_ge(wexp_done, 1)
            dve.sem_inc(y_done, 1)
            with dve.Fori(0, NE // 2) as e2:
                for k in range(2):
                    V.tensor_copy(wcur[:, k, :], wexp[:, :, bass.ds(e2 * 2 + k, 1)].rearrange(
                        "p n e -> p (n e)")).then_inc(wcur_done, 1)
                    dve.wait_ge(wcur_done, e2 * 2 + k + 1)
                    for b in range(B):
                        n = k * B + b
                        dve.wait_ge(y_psum, 1 + e2 * (2 * B) + n + 1)
                        for t in range(TT):
                            y = V.scalar_tensor_tensor(
                                out=x1[:, b * TT + t, :], in0=ps[:, 4 + b, t * P:(t + 1) * P],
                                scalar=wcur[:, k, b * TT + t:b * TT + t + 1], in1=x1[:, b * TT + t, :],
                                op0=ALU.mult, op1=ALU.add)
                        y.then_inc(y_done, 1)
            dve.wait_ge(y_done, 1 + NE * B)
            base = count[0]
            for b in range(B):
                t = slice(b * TT, (b + 1) * TT)
                dve.wait_ge(bias_psum, b + 1)
                V.tensor_tensor(x1[:, t, :], x1[:, t, :], ps[:, b, :].rearrange("p (n d) -> p n d", n=TT),
                                ALU.add).then_inc(fin_d, 1)
                dve.wait_ge(fin_d, 3 * b + 1)
                hop(V.tensor_reduce(r_s[:, 0, t], x1[:, t, :], AX.X, ALU.add))
                hop(V.tensor_scalar(r_s[:, 3, t], r_s[:, 0, t], 1.0 / D, None, ALU.mult))
                V.tensor_tensor(dev[:, t, :], x1[:, t, :], over(r_s[:, 3, t].unsqueeze(2), T4),
                                ALU.subtract).then_inc(fin_d, 1)
                dve.wait_ge(fin_sq, b + 1)
                V.tensor_reduce(r_s[:, 1, t], sqA[:, b * L:(b + 1) * L].rearrange("p (n d) -> p n d", n=TT), AX.X,
                                ALU.add).then_inc(fin_d, 1)
                dve.wait_ge(fin_sqrt, b + 1)
                hop(V.reciprocal(r_s[:, 4, t], r_s[:, 2, t]))
                V.tensor_tensor(x_tok[:, t, :], dev[:, t, :], over(r_s[:, 4, t].unsqueeze(2), T4),
                                ALU.mult).then_inc(fin_done, 1)

        @block.gpsimd
        def _(pool):
            G = nc.gpsimd
            G.memset(win[:, :, :, :], 0.0).then_inc(win_zero, 1)
            G.memset(epsv[:, 0:1], L2_EPS).then_inc(eps_set, 1)
            G.memset(epsv[:, 1:2], EPS).then_inc(eps_set, 1)
            G.memset(stats[:, :, :], 0.0).then_inc(misc, 1)
            pool.wait_ge(w_in, 16)
            pool.wait_ge(v_in, 16)
            G.tensor_scalar(w_s[:, W_GS:W_ALL], w_s[:, W_GS:W_ALL], 1.0 / H, None, ALU.mult).then_inc(ws_scaled, 1)
            G.tensor_scalar(w_s[:, W_O:W_O + P], w_s[:, W_O:W_O + P], v_s[:, V_NORM:V_NORM + 1], None,
                            ALU.mult).then_inc(wo_scaled, 1)
            for i in range(2 * B):
                s, b = divmod(i, B)
                src = (k_hc, q_hc)[s][:, b * L:(b + 1) * L]
                pool.wait_ge(hc_done, B + i + 1)
                G.tensor_tensor((sqA, sqB)[s][:, b * L:(b + 1) * L], src, src, ALU.mult).then_inc(sq_done, 1)
            pool.wait_ge(beta_done, 1)
            pool.wait_ge(ssq_done, 2 * B)
            pool.wait_ge(c_in, 16)
            for b in range(B):
                G.tensor_tensor(hc(nbm)[:, b, :, :], over(nstrict, FULL),
                                over(beta[:, b * C:(b + 1) * C].unsqueeze(2), FULL), ALU.mult).then_inc(nbm_done, 1)
            for b in range(B):
                pool.wait_ge(low_done, b + 1)
                x_ = hc(inv)[:, b, :, :]
                G.tensor_tensor(x_, hc(low)[:, b, :, :], over(pair, FULL), ALU.mult).then_inc(state0, 1)
                pool.wait_ge(state0, b + 1)
                G.tensor_tensor(x_, x_, over(eye, FULL), ALU.add).then_inc(pair_done, 1)
            pool.wait_ge(sm, 10)
            pool.wait_ge(o_psum, B)
            for b in range(B):
                cs = slice(b * C, (b + 1) * C)
                G.tensor_tensor(hc(mixA)[:, b, :, :], hc(v_hc[:, :])[:, b, :, :],
                                over(prob[:, cs, 3].unsqueeze(2), FULL), ALU.mult).then_inc(mix_p, 1)
                G.tensor_tensor(hc(mixB)[:, b, :, :], hc(long[:, :])[:, b, :, :],
                                over(prob[:, cs, 1].unsqueeze(2), FULL), ALU.mult).then_inc(mix_p, 1)
                pool.wait_ge(mix_p, 3 * b + 2)
                G.tensor_tensor(mixA[:, b * L:(b + 1) * L], mixA[:, b * L:(b + 1) * L],
                                mixB[:, b * L:(b + 1) * L], ALU.add).then_inc(mix_p, 1)
            pool.wait_ge(b2_in, 16)
            pool.wait_ge(ds_psum, 2 * (C - 1))
            G.tensor_tensor(b2big, over(b2rep[:, :].unsqueeze(1), [P, NT, D]),
                            over(cst_s[:, C_TILE:C_TILE + NT].unsqueeze(2), [P, NT, D]), ALU.mult).then_inc(b2big_done, 1)


def toeplitz(taps):
    n = taps.shape[1]
    block = np.zeros((WIN, Q, P), taps.dtype)
    for i in range(Q):
        block[2 * Q + i - n + 1:2 * Q + i + 1, i, :] = taps.T
    return block.reshape(WIN, Q * P)


def laid_out(a):
    f = {k.replace("L0_attn_", "").replace("L0_ffn_", "f_"): np.asarray(v) for k, v in a.items()}
    z = np.float32
    wall = np.zeros((P, W_ALL), z)
    for at, name in ((W_Q, "Wq"), (W_K, "Wk"), (W_V, "Wv"), (W_O, "Wo")):
        wall[:, at:at + P] = f[name]
    wall[:, W_G:W_G + P] = f["Wg1"][:D]
    wall[:, W_OG:W_OG + 64] = f["Wog1"][:D]
    given = (0, 1, 3, 2)
    for h in range(H):
        wall[:, W_BR + h * Q] = f["Wb"][:, h]
        wall[:, W_BR + h * Q + 1] = f["Wres"][:, h]
        wall[:, W_G2 + h * Q:W_G2 + h * Q + 4] = f["Wg2"]
        wall[:64, W_OG2 + h * Q] = f["Wog2"][:, 0]
        for s in range(4):
            r = h * Q + 4 * s
            wall[r:r + 4, W_GS:W_GS + P] = f["Wg1"][D + 4 * given[s]:D + 4 * given[s] + 4]
        wall[h * Q + 4 * ST_O:h * Q + 4 * ST_O + 4, W_OGS:W_OGS + 64] = f["Wog1"][D:D + 4]
        wall[h * Q + 4 * ST_V:h * Q + 4 * ST_V + 4, W_OGS:W_OGS + 64] = f["Wog1"][D + 4:D + 8]
    vecs = np.zeros((P, V_ALL), z)
    for s, name in enumerate(("wv_conv", "wk_conv", "wq_conv")):
        vecs[:, V_CONV + 4 * s:V_CONV + 4 * s + 4] = f[name]
    vecs[:, V_BG1] = f["bg1"]
    vecs[:64, V_BOG1] = f["bog1"]
    vecs[:, V_BG2:V_BG2 + 4] = f["bg2"]
    vecs[:, V_TEMP] = f["logit_temp"][0]
    vecs[:, V_BOG2] = f["bog2"][0]
    vecs[:, V_BRES] = np.repeat(f["bres"], Q)
    vecs[:, V_STATIC] = np.repeat(f["conv_res_logit"], Q)
    vecs[:, V_NORM] = np.tile(f["norm_w"], H)
    fir_l, fir_s = toeplitz(f["fir_long"].reshape(P, 64)), toeplitz(f["fir_short"].reshape(P, 5))
    cst, lmask = shape_constants()
    return {
        "x": f["hidden_states"].reshape(N, D), "cst": cst, "lmask": lmask, "wall": wall, "vecs": vecs,
        "fir_l": fir_l, "fir_s": fir_s, "w1": f["f_W1"],
        "b1": f["f_b1"].reshape(NE, NF, P).transpose(0, 2, 1), "w2": f["f_W2"], "b2": f["f_b2"],
    }


def kernel(**inputs):
    import concourse.bacc as _bacc
    from concourse.bass_utils import run_bass_kernel_spmd as _run

    nc = _bacc.Bacc("TRN2", target_bir_lowering=False, num_devices=1)
    arrays, args = {}, []
    for name, a in laid_out(inputs).items():
        a = np.ascontiguousarray(a)
        arrays[f"in_{name}_dram"] = a
        args.append(nc.dram_tensor(f"in_{name}_dram", a.shape, mybir.dt.from_np(a.dtype), kind="ExternalInput").ap())
    args.append(nc.dram_tensor("out_0_dram", (N, D), F32, kind="ExternalOutput").ap())
    post_ln_block(nc, *args)
    r = _run(nc, [arrays], core_ids=[0])
    return r.results[0]["out_0_dram"].reshape(B, L, D)
```

```python
from contextlib import ExitStack

import numpy as np

import concourse.bass as bass
from concourse import mybir

F32 = mybir.dt.float32
I32 = mybir.dt.int32
ALU = mybir.AluOpType
ACT = mybir.ActivationFunctionType
AX = mybir.AxisListType

P = 128
B, L, D = 4, 512, 128
H = 4
Q = 32
C = L // Q
BC = B * C
TT = L // P
NT = B * TT
N = B * L
NE = 8
FF = 512
NF = FF // P
WIN = 3 * Q
EPS = 1e-5
L2_EPS = 1e-6
FLOOR = 0.02

C_ID, C_NSTRICT, C_UINCL, C_EYE, C_PAIR, C_STEP, C_VAL, C_TILE = 0, 128, 160, 192, 224, 256, 272, 304
C_LESS, C_ONE, C_FULL, C_BEFORE = C_TILE, C_TILE + P, C_TILE + 2 * P, C_TILE + 2 * P + NE
C_ALL = C_BEFORE + NE * NE
W_Q, W_K, W_V, W_G, W_O, W_OG, W_BR, W_G2, W_OG2, W_GS, W_OGS = 0, 128, 256, 384, 512, 640, 704, 832, 960, 1088, 1216
W_ALL = W_OGS + 64
V_CONV, V_BG1, V_BOG1, V_BG2, V_TEMP, V_BOG2, V_BRES, V_STATIC, V_NORM = 0, 12, 13, 14, 18, 19, 20, 21, 22
V_ALL = 23

G = 2
TAPS = [(0, 0), (0, 1), (0, 2), (0, 3), (1, 0), (1, 1), (2, 0), (2, 1), (1, 2), (1, 3), (2, 2), (2, 3)]
TAP_BANK = [4, 5, 6, 7, 4, 5, 6, 7, 2, 3, 6, 7]
GT = G * TT
SLOTS = (GT * P + NE * (P - 1)) // P
STEPS = 2 * SLOTS
SM_STEPS = 11
T_GATE, T_SOFT, T_STAT, T_OGATE, T_FACT, T_PROJ, T_NORM = 0, 2, 4, 6, 8, 9, 10
LEVELS = 4
ST_SHORT, ST_LONG, ST_V, ST_DELTA, ST_O = range(5)


def shape_constants():
    c = np.zeros((P, C_ALL), np.float32)
    i = np.arange(P)
    r, j = (i % Q)[:, None], np.arange(Q)[None, :]
    c[:, C_ID:C_ID + P] = np.eye(P)
    c[:, C_NSTRICT:C_NSTRICT + Q] = -(r > j).astype(np.float32)
    c[:, C_UINCL:C_UINCL + Q] = r <= j
    c[:, C_EYE:C_EYE + Q] = r == j
    c[:, C_PAIR:C_PAIR + Q] = (r // 2 == j // 2) & (r > j)
    c[:, C_STEP:C_STEP + 16] = np.arange(1, 17)
    c[:, C_VAL:C_VAL + 32] = np.arange(-16, 16)
    c[:, C_LESS:C_LESS + P] = i[:, None] < i[None, :]
    c[:, C_ONE:C_ONE + P] = 1.0
    c[:, C_FULL:C_FULL + NE] = P * np.arange(NE) + 1
    c[:, C_BEFORE:C_BEFORE + NE * NE] = (np.arange(NE)[None, :] < np.arange(NE)[:, None]).reshape(1, NE * NE)
    m = np.zeros((P, LEVELS, Q), np.int32)
    for n in range(LEVELS):
        s = 2 << n
        m[:, n] = (r // (2 * s) == j // (2 * s)) & (r % (2 * s) >= s) & (j % (2 * s) < s)
    return c, m.reshape(P, LEVELS * Q)


def post_ln_block(nc, x, cst, lmask, wall, vecs, fir_l, fir_s, w1, b1, w2, b2, sorted_in, sorted_out, out):
    ctx = ExitStack()
    with ctx:
        def sb(name, shape, dt=F32):
            return ctx.enter_context(nc.sbuf_tensor(name, shape, dt))

        def sem(name):
            return ctx.enter_context(nc.semaphore(name))

        x_tok = sb("x_tok", [P, NT, D])
        xT = sb("xT", [P, N])
        qkT = sb("qkT", [P, 2, N])
        kT_raw = sb("kT_raw", [P, N])
        vT = sb("vT", [P, N])
        k_hc = sb("k_hc", [P, N])
        q_hc = sb("q_hc", [P, N])
        v_hc = sb("v_hc", [P, N])
        short = sb("short", [P, N])
        long = sb("long", [P, N])
        sqA = sb("sqA", [P, N])
        sqB = sb("sqB", [P, N])
        stats = sb("stats", [P, BC, Q])
        arena = sb("arena", [P, NE, N])
        cst_s = sb("cst_s", [P, C_ALL])
        lmask_s = sb("lmask_s", [P, LEVELS, Q], I32)
        w_s = sb("w_s", [P, W_ALL])
        v_s = sb("v_s", [P, V_ALL])
        gate_hc = sb("gate_hc", [P, BC, Q])
        beta = sb("beta", [P, BC])
        sgate = sb("sgate", [P, BC])
        norm = sb("norm", [P, 2, BC])
        nrm1 = sb("nrm1", [P, 2, BC])
        raw = sb("raw", [P, 5, 3, BC])
        m1 = sb("m1", [P, 5, BC])
        m2 = sb("m2", [P, 5, BC])
        prob = sb("prob", [P, BC, 4])
        prob2 = sb("prob2", [P, BC, 4])
        row1 = sb("row1", [P, BC])
        row2 = sb("row2", [P, BC])
        row3 = sb("row3", [P, BC])
        coef = sb("coef", [P, BC])
        tmpv = sb("tmpv", [P, 8])
        epsv = sb("epsv", [P, 2])
        r_s = sb("r_s", [P, 6, NT])
        ge = sb("ge", [P, GT, 16])
        eq = sb("eq", [P, GT, 32])
        me = sb("me", [P, G, GT + 1, NE])
        rank = sb("rank", [P, GT + 1, NE])
        cnt = sb("cnt", [P, 4, NE])
        place = sb("place", [P, NT])
        place_i = sb("place_i", [P, NT], I32)
        tile_e = sb("tile_e", [P, 3, SLOTS])
        tile_i = sb("tile_i", [P, G, 2, SLOTS], I32)
        zero = sb("zero", [P, D])
        fit = eq[:, :, :].rearrange("p a b -> p (a b)")[:, 0:SLOTS * NE].rearrange("p (j e) -> p j e", e=NE)
        chain = sb("chain", [P, B, Q])

        toep_flat = arena[:, 0:4, :].rearrange("p a n -> p (a n)")
        win_flat = arena[:, 4:8, :].rearrange("p a n -> p (a n)")
        toep = toep_flat.rearrange("p (a n) -> p a n", a=2)
        win = win_flat.rearrange("p (h n d) -> p h n d", h=H, n=BC)
        low = toep_flat[:, 0:N]
        lowT = toep_flat[:, N:2 * N]
        inv = toep_flat[:, 2 * N:3 * N]
        invT = toep_flat[:, 3 * N:4 * N]
        mid = win_flat[:, 0:N]
        attnT = win_flat[:, N:2 * N]
        state = win_flat[:, 2 * N:3 * N]
        delta = win_flat[:, 3 * N:4 * N]
        nbm = sqA[:, :]
        statsT = lowT
        hid = low
        o_hc = inv
        oT = invT
        mixA, mixB = mid, state
        x1 = v_hc[:, :].rearrange("p (n d) -> p n d", n=NT)
        dev = vT[:, :].rearrange("p (n d) -> p n d", n=NT)
        xs = kT_raw[:, 0:SLOTS * P].rearrange("p (n d) -> p n d", d=D)
        ys = xs
        xsT = q_hc[:, 0:SLOTS * P]
        hT = k_hc[:, :].rearrange("p (k f n) -> p k f n", k=4, f=NF)
        wbuf = qkT[:, :, :].rearrange("p k (a n) -> p (k a) n", a=2)
        bbuf = sb("bbuf", [P, 4, NF])
        b1tab = xT[:, 0:NE * NF].rearrange("p (e f) -> p e f", e=NE)
        b2buf = long[:, 0:2 * D].rearrange("p (k d) -> p k d", k=2)
        b2in = long[:, 0:NE * D].rearrange("p (e d) -> p e d", e=NE)
        b2pair = short[:, 0:NE * D].rearrange("p (e d) -> p e d", e=NE)
        y_tok = sqA[:, :].rearrange("p (n d) -> p n d", n=NT)

        ps = ctx.enter_context(nc.psum_tensor("ps", [P, 8, 512], F32))

        def hc(t):
            return t.rearrange("p (b c d) -> p b c d", b=B, c=C)

        def over(ap, shape):
            return ap.to_broadcast(shape)

        ident = cst_s[:, C_ID:C_ID + P]
        uincl = cst_s[:, C_UINCL:C_UINCL + Q].unsqueeze(1)
        nstrict = cst_s[:, C_NSTRICT:C_NSTRICT + Q].unsqueeze(1)
        eye = cst_s[:, C_EYE:C_EYE + Q].unsqueeze(1)
        pair = cst_s[:, C_PAIR:C_PAIR + Q].unsqueeze(1)
        FULL = [P, C, Q]

        x_in = [sem(f"x_in{b}") for b in range(B)]
        w_in, c_in, lm_in, v_in, f_in, b2_in = (
            sem(n) for n in ("w_in", "c_in", "lm_in", "v_in", "f_in", "b2_in"))
        w_all, filled = sem("w_all"), sem("filled")
        scattered = [sem(f"scattered{g}") for g in range(2)]
        xs_in = [sem(f"xs_in{g}") for g in range(2)]
        ys_out = [sem(f"ys_out{g}") for g in range(2)]
        y_in = [sem(f"y_in{g}") for g in range(2)]
        zero_set, me_done, rank_psum, place_done = sem("zero_set"), sem("me_done"), sem("rank_psum"), sem("place_done")
        xs_psum, xs_done, wb_done = sem("xs_psum"), sem("xs_done"), sem("wb_done")
        pair_sum, bias_done = sem("pair_sum"), sem("bias_done")
        win_zero, win_in = sem("win_zero"), sem("win_in")
        eps_set, misc = sem("eps_set"), sem("misc")
        xt_psum, xt_done = sem("xt_psum"), sem("xt_done")
        proj_psum, tap3_done, taps_done, silu_done, hc_done = (
            sem(n) for n in ("proj_psum", "tap3_done", "taps_done", "silu_done", "hc_done"))
        tap2_done = sem("tap2_done")
        br_psum, br_hc, beta_done, res_done, sgate_done = (
            sem(n) for n in ("br_psum", "br_hc", "beta_done", "res_done", "sgate_done"))
        sq_done, ssq_done, nrm_sqrt, nrm_done, kn_done, knT_done = (
            sem(n) for n in ("sq_done", "ssq_done", "nrm_sqrt", "nrm_done", "kn_done", "knT_done"))
        nbm_done = sem("nbm_done")
        fir_psum, fir_done = sem("fir_psum"), sem("fir_done")
        gram_psum, low_done, attn_done, lowT_done = (sem(n) for n in ("gram_psum", "low_done", "attn_done", "lowT_done"))
        pair_done, inv_done, invT_done, tb_done = (sem(n) for n in ("pair_done", "inv_done", "invT_done", "tb_done"))
        lx_psum, lx_done, xlx_psum = sem("lx_psum"), sem("lx_done"), sem("xlx_psum")
        ks_psum, rhs_done, u_psum, u_done, ds_psum, s_done, o_psum = (
            sem(n) for n in ("ks_psum", "rhs_done", "u_psum", "u_done", "ds_psum", "s_done", "o_psum"))
        state0 = sem("state0")
        st_sq, st_red, st_small, st_m2, st_var, st_l2 = (
            sem(n) for n in ("st_sq", "st_red", "st_small", "st_m2", "st_var", "st_l2"))
        ws_scaled, wo_scaled = sem("ws_scaled"), sem("wo_scaled")
        soft_a, soft_b, soft_c = sem("soft_a"), sem("soft_b"), sem("soft_c")
        delta_done, stT_done, g_psum, g_done, lg_psum, lg_hc = (
            sem(n) for n in ("delta_done", "stT_done", "g_psum", "g_done", "lg_psum", "lg_hc"))
        sm, sm_exp = sem("sm"), sem("sm_exp")
        mix_d, mix_p = sem("mix_d"), sem("mix_p")
        og_sig, og_a, og_sqrt = sem("og_sig"), sem("og_a"), sem("og_sqrt")
        of_done, oT_done, wo_psum = sem("of_done"), sem("oT_done"), sem("wo_psum")
        ln_d, ln_sq, ln_sqrt = sem("ln_d"), sem("ln_sq"), sem("ln_sqrt")
        x1_done, rt, b2_done = sem("x1_done"), sem("rt"), sem("b2_done")
        h_psum, h_done, dn_psum, y_done = sem("h_psum"), sem("h_done"), sem("dn_psum"), sem("y_done")
        fin_d, fin_sq, fin_sqrt, fin_done, out_done = (
            sem(n) for n in ("fin_d", "fin_sq", "fin_sqrt", "fin_done", "out_done"))

        block = ctx.enter_context(nc.Block())

        def lv(n, b):
            return (b // G) * G * LEVELS + G * n + b % G + 1

        def sc(c, b):
            return (b // G) * G * C + G * c + b % G + 1

        def sl(c, b):
            return (b // G) * G * (C - 1) + G * c + b % G + 1

        def gt(r, b):
            return (b // G) * 2 * G + r * G + b % G + 1

        def ivt(n, b):
            return (b // G) * G * (LEVELS + 1) + G * n + b % G + 1

        def red(g, r):
            return 9 + (2 * g + r) * 3 * G

        def group(g):
            return range(g * G, (g + 1) * G)

        @block.sync
        def _(sp):
            xv = x.rearrange("(n p) d -> p n d", p=P)
            sp.dma_start(cst_s[:, :], cst).then_inc(c_in, 16)
            for b in range(B):
                sp.dma_start(x_tok[:, b * TT:(b + 1) * TT, :], xv[:, b * TT:(b + 1) * TT, :]).then_inc(x_in[b], 16)
                if b == 0:
                    sp.dma_start(w_s[:, :], wall).then_inc(w_in, 16)
                    sp.dma_start(v_s[:, :], vecs).then_inc(v_in, 16)
            for k, f in ((0, fir_l), (1, fir_s)):
                sp.dma_start(toep[0:WIN, k, :], f).then_inc(f_in, 16)
            sp.dma_start(lmask_s[:, :, :].rearrange("p a b -> p (a b)"), lmask).then_inc(lm_in, 16)
            sp.wait_ge(zero_set, 1)
            for g in range(2):
                sp.dma_start(sorted_in[g].rearrange("(n p) d -> p n d", p=P),
                             zero[:, :].unsqueeze(1).to_broadcast([P, SLOTS, D])).then_inc(filled, 16)
            sp.wait_ge(win_zero, 1)
            sp.wait_ge(hc_done, B)
            v4 = hc(v_hc[:, :])
            for h in range(H):
                for k in range(3):
                    dst = win[k * Q:(k + 1) * Q, h, :, :].rearrange("p (b c) d -> p b (c d)", b=B)
                    src = v4[h * Q:(h + 1) * Q, :, 0:C - 2 + k, :].rearrange("p b c d -> p b (c d)")
                    sp.dma_start(dst[:, :, (2 - k) * Q:C * Q], src).then_inc(win_in, 16)
            sp.wait_ge(x1_done, G)
            sp.wait_ge(mix_p, 3 * G)
            sp.dma_start(b2in, bass.AP(b2.tensor, 0, [[0, P], [D, NE], [1, D]])).then_inc(b2_in, 16)
            sp.dma_start(b1tab, b1.rearrange("e p c -> p e c")).then_inc(w_all, 16)
            for e in range(NE):
                sp.dma_start(arena[:, e, 0:FF], w1[e]).then_inc(w_all, 16)
                sp.dma_start(arena[:, e, FF:2 * FF].rearrange("p (c d) -> p c d", c=NF),
                             w2[e].rearrange("(c p) d -> p c d", p=P)).then_inc(w_all, 16)
            ov = out.rearrange("(n p) d -> p n d", p=P)

            def sorted_rows(t, a, b):
                return t.rearrange("(n p) d -> p n d", p=P)[:, a:b, :]

            for g in range(2):
                if g == 1:
                    sp.wait_ge(ys_out[0], 16 * 3)
                sp.wait_ge(scattered[g], 16 * GT)
                sp.dma_start(xs, sorted_rows(sorted_in[g], 0, SLOTS)).then_inc(xs_in[g], 16)
                if g == 1:
                    for b in group(0):
                        sp.wait_ge(fin_done, b + 1)
                        sp.dma_start(ov[:, b * TT:(b + 1) * TT, :], x_tok[:, b * TT:(b + 1) * TT, :]).then_inc(out_done, 16)
                third = SLOTS // 3
                for a in range(0, SLOTS, third):
                    sp.wait_ge(y_done, g * SLOTS + a + third)
                    sp.dma_start(sorted_rows(sorted_out[g], a, a + third), ys[:, a:a + third, :]).then_inc(ys_out[g], 16)
            for b in group(1):
                sp.wait_ge(fin_done, b + 1)
                sp.dma_start(ov[:, b * TT:(b + 1) * TT, :], x_tok[:, b * TT:(b + 1) * TT, :]).then_inc(out_done, 16)
            sp.wait_ge(out_done, 16 * B)

        @block.tensor
        def _(pe):
            k4, q4 = hc(qkT[:, 0, :]), hc(qkT[:, 1, :])
            kn4, lowT4, inv4, invT4 = hc(k_hc[:, :]), hc(lowT), hc(inv), hc(invT)
            mid4, attn4, state4 = hc(mid), hc(attnT), hc(state)

            def per_head(dst, lhsT, rhs, start=True, stop=True):
                for h in range(H):
                    s = slice(h * Q, (h + 1) * Q)
                    mm = nc.tensor.matmul(dst[s], lhsT[s], rhs[s], start=start, stop=stop)
                return mm

            def project(n):
                s, b = TAPS[n]
                w = (W_V, W_K, W_Q)[s]
                nc.tensor.matmul(ps[:, TAP_BANK[n], :], w_s[:, w:w + P], xT[:, b * L:(b + 1) * L],
                                 start=True, stop=True).then_inc(proj_psum, 1)

            pe.wait_ge(c_in, 16)
            for b in range(B):
                pe.wait_ge(x_in[b], 16)
                for t in range(TT):
                    mm = nc.tensor.transpose(ps[:, b, t * P:(t + 1) * P], x_tok[:, b * TT + t, :], ident)
                mm.then_inc(xt_psum, 1)
                pe.wait_ge(w_in, 16)
                pe.wait_ge(xt_done, b + 1)
                project(b)
            for b in range(B):
                nc.tensor.matmul(ps[:, b, :], w_s[:, W_BR:W_BR + P], xT[:, b * L:(b + 1) * L],
                                 start=True, stop=True).then_inc(br_psum, 1)
            for n in range(B, 2 * B):
                pe.wait_ge(taps_done, n - B + 1)
                project(n)
            pe.wait_ge(f_in, 32)
            pe.wait_ge(win_in, 16 * 3 * H)
            pe.wait_ge(br_hc, B)
            for m in range(8):
                if m >= 4:
                    pe.wait_ge(fir_done, m - 3)
                for i in range(8):
                    for h in range(H):
                        ch = h * Q + (m % 4) * 8 + i
                        mm = nc.tensor.matmul(ps[h * Q:(h + 1) * Q, m % 4, i * BC:(i + 1) * BC],
                                              toep[0:WIN, m // 4, ch:Q * P:P], win[0:WIN, h, :, ch % Q],
                                              start=True, stop=True)
                mm.then_inc(fir_psum, 1)
            pe.wait_ge(taps_done, 2 * B)
            pe.wait_ge(fir_done, 8)
            for n in range(2 * B, 3 * B):
                project(n)

            def gram(b):
                pe.wait_ge(knT_done, b + 1)
                for c in range(C):
                    mm = per_head(ps[:, b + 4 * (c // 8), (c % 8) * 64:(c % 8) * 64 + 64], k4[:, b, c, :],
                                  qkT[:, :, (b * C + c) * Q:(b * C + c + 1) * Q])
                mm.then_inc(gram_psum, 1)

            def low_x(n, b):
                if n == 0:
                    pe.wait_ge(lowT_done, b + 1)
                    pe.wait_ge(pair_done, b + 1)
                    pe.wait_ge(attn_done, b + 1)
                else:
                    pe.wait_ge(inv_done, lv(n - 1, b))
                for c in range(C):
                    mm = per_head(ps[:, b, c * Q:(c + 1) * Q], lowT4[:, b, c, :], inv4[:, b, c, :])
                mm.then_inc(lx_psum, 1)

            def x_low_x(n, b):
                pe.wait_ge(lx_done, lv(n, b))
                pe.wait_ge(invT_done, ivt(n, b))
                for c in range(C):
                    mm = per_head(ps[:, 4 + b, c * Q:(c + 1) * Q], invT4[:, b, c, :], mid4[:, b, c, :])
                mm.then_inc(xlx_psum, 1)

            def outputs(c, b):
                for h in range(H):
                    s = slice(h * Q, (h + 1) * Q)
                    dst = ps[s, 4 + b, c * Q:(c + 1) * Q]
                    if c > 0:
                        nc.tensor.matmul(dst, q4[s, b, c, :], state4[s, b, c, :], start=True, stop=False)
                    mm = nc.tensor.matmul(dst, attn4[s, b, c, :], mid4[s, b, c, :], start=(c == 0), stop=True)
                if c == C - 1:
                    mm.then_inc(o_psum, 1)

            def scan_step(g, c):
                if c > 0:
                    for b in group(g):
                        pe.wait_ge(s_done, sl(c - 1, b))
                        per_head(ps[:, b, 0:Q], k4[:, b, c, :], state4[:, b, c, :]).then_inc(ks_psum, 1)
                    outputs(c - 1, g * G)
                for b in group(g):
                    pe.wait_ge(rhs_done, sc(c, b))
                    per_head(ps[:, b, 64:64 + Q], invT4[:, b, c, :], chain[:, b, :]).then_inc(u_psum, 1)
                if c > 0:
                    outputs(c - 1, g * G + 1)
                for b in group(g):
                    pe.wait_ge(u_done, sc(c, b))
                    if c < C - 1:
                        per_head(ps[:, b, 128:128 + Q], kn4[:, b, c, :], mid4[:, b, c, :]).then_inc(ds_psum, 1)
                if c == C - 1:
                    for b in group(g):
                        outputs(c, b)

            def gate_hidden(g, r):
                wide = (P, 64)[r]
                wx, wst = ((W_G, W_GS), (W_OG, W_OGS))[r]
                pe.wait_ge(ws_scaled, 1)
                for b in group(g):
                    pe.wait_ge(stT_done, gt(r, b))
                    nc.tensor.matmul(ps[0:wide, b, :], w_s[:, wx:wx + wide], xT[:, b * L:(b + 1) * L],
                                     start=True, stop=False)
                    nc.tensor.matmul(ps[0:wide, b, :], w_s[:, wst:wst + wide], statsT[:, b * L:(b + 1) * L],
                                     start=False, stop=True).then_inc(g_psum, 1)

            def gate_out(g, r):
                wide, w = ((P, W_G2), (64, W_OG2))[r]
                for b in group(g):
                    pe.wait_ge(g_done, gt(r, b))
                    pe.wait_ge(delta_done, b + 1) if r == 0 else pe.wait_ge(lg_hc, gt(0, b))
                    nc.tensor.matmul(ps[:, 4 + b, :], w_s[0:wide, w:w + P], hid[0:wide, b * L:(b + 1) * L],
                                     start=True, stop=True).then_inc(lg_psum, 1)

            def project_out(g):
                pe.wait_ge(wo_scaled, 1)
                for b in group(g):
                    pe.wait_ge(oT_done, b + 1)
                    for t in range(TT):
                        a = b * L + t * P
                        mm = nc.tensor.matmul(ps[:, b, t * P:(t + 1) * P], oT[:, a:a + P], w_s[:, W_O:W_O + P],
                                              start=True, stop=True)
                    mm.then_inc(wo_psum, 1)

            def ranks(g):
                out_ = ps[:, 4, 0:(GT + 1) * NE]
                pe.wait_ge(me_done, g + 1)
                if g == 1:
                    pe.wait_ge(y_done, SLOTS)
                m_ = me[:, g, :, :].rearrange("p n e -> p (n e)")
                nc.tensor.matmul(out_, cst_s[:, C_LESS:C_LESS + P], m_, start=True, stop=False)
                for k in range(1, GT + 1):
                    mm = nc.tensor.matmul(ps[:, 4, k * NE:(GT + 1) * NE], cst_s[:, C_ONE:C_ONE + P],
                                          m_[:, 0:(GT + 1 - k) * NE], start=False, stop=(k == GT))
                mm.then_inc(rank_psum, 1)

            def turn_sorted(g):
                pe.wait_ge(xs_in[g], 16)
                pe.wait_ge(place_done, g + 1)
                if g == 1:
                    pe.wait_ge(h_done, STEPS)
                for j in range(SLOTS):
                    mm = nc.tensor.transpose(ps[:, (4, 5, 0, 1)[j // 4], j % 4 * P:(j % 4 + 1) * P], xs[:, j, :], ident)
                    if j % 4 == 3 or j == SLOTS - 1:
                        mm.then_inc(xs_psum, 1)

            def up(u, i, tile, base):
                pe.wait_ge(wb_done, i + (base + 1))
                if not (base == 0 and u < 2 and i is u):
                    pe.wait_ge(h_done, i + (base - 1))
                for f in range(NF):
                    mm = nc.tensor.matmul(ps[:, u % 2, f * P:(f + 1) * P], wbuf[:, u, f * P:(f + 1) * P], tile,
                                          start=True, stop=True)
                mm.then_inc(h_psum, 1)

            def down(u, i, j, base):
                pe.wait_ge(h_done, i + (base + 1))
                if u % 2 == 0 and not (base == 0 and i is u):
                    pe.wait_ge(y_done, j + (base // 2 - 1))
                for f in range(NF):
                    mm = nc.tensor.matmul(ps[:, 4 + u // 2, 0:P], hT[:, u, f, :], wbuf[:, u, FF + f * P:FF + (f + 1) * P],
                                          start=(u % 2 == 0 and f == 0), stop=(u % 2 == 1 and f == NF - 1))
                mm.then_inc(dn_psum, 1)

            for b in group(0):
                gram(b)
            for n in range(LEVELS):
                for b in group(0):
                    low_x(n, b)
                for b in group(0):
                    x_low_x(n, b)
            for b in group(0):
                pe.wait_ge(tb_done, b + 1)
            for c in range(C):
                scan_step(0, c)
            for b in group(1):
                gram(b)
            for n in range(LEVELS):
                for b in group(1):
                    low_x(n, b)
                if n == 0:
                    gate_hidden(0, 0)
                if n == 2:
                    gate_hidden(0, 1)
                if n == 3:
                    project_out(0)
                for b in group(1):
                    x_low_x(n, b)
                if n == 0:
                    gate_out(0, 0)
                if n == 2:
                    gate_out(0, 1)
            for b in group(1):
                pe.wait_ge(tb_done, b + 1)
            ranks(0)
            for c in range(C):
                scan_step(1, c)
            turn_sorted(0)
            between = {T_GATE: lambda: gate_hidden(1, 0), T_GATE + 1: lambda: gate_out(1, 0),
                       T_OGATE: lambda: gate_hidden(1, 1), T_OGATE + 1: lambda: gate_out(1, 1),
                       T_PROJ: lambda: project_out(1)}

            def sorted_tile(j):
                return xsT[:, j * P:(j + 1) * P]

            pe.wait_ge(xs_done, 4)
            for i in range(STEPS + 2):
                if i < STEPS:
                    up(i % 4, i, sorted_tile(i // 2), 0)
                if i >= 2:
                    down((i - 2) % 4, i - 2, (i - 2) // 2, 0)
                if i % 2 == 1 and i // 2 in between:
                    between[i // 2]()
            ranks(1)
            turn_sorted(1)
            pe.wait_ge(xs_done, 8)
            up(0, 0, sorted_tile(0), STEPS)
            up(1, 1, sorted_tile(0), STEPS)
            with pe.Fori(0, (STEPS - 2) // 4) as r:
                for u in range(4):
                    down(u, r * 4 + u, r * 2 + u // 2, STEPS)
                    up((u + 2) % 4, r * 4 + (u + 2), xsT[:, bass.ds((r * 2 + (u + 2) // 2) * P, P)], STEPS)
            for u in range(2):
                down(u, STEPS - 2 + u, SLOTS - 1, STEPS)

        @block.scalar
        def _(act):
            srcs = (vT[:, :], kT_raw[:, :], qkT[:, 1, :])
            for b in range(B):
                act.wait_ge(xt_psum, b + 1)
                nc.scalar.copy(xT[:, b * L:(b + 1) * L], ps[:, b, :]).then_inc(xt_done, 1)
            act.wait_ge(v_in, 16)

            def newest_tap(n):
                s, b = TAPS[n]
                act.wait_ge(proj_psum, n + 1)
                c = V_CONV + 4 * s + 3
                nc.scalar.activation(srcs[s][:, b * L:(b + 1) * L], ps[:, TAP_BANK[n], :], ACT.Copy,
                                     scale=v_s[:, c:c + 1]).then_inc(tap3_done, 1)

            def silu(n):
                s, b = TAPS[n]
                act.wait_ge(taps_done, n + 1)
                y = srcs[s][:, b * L:(b + 1) * L]
                nc.scalar.activation(y, y, ACT.Silu).then_inc(silu_done, 1)

            def norms(g):
                cs = slice(g * G * C, (g + 1) * G * C)
                act.wait_ge(ssq_done, 2 * G * (g + 1))
                nc.scalar.activation(nrm1[:, :, cs], norm[:, :, cs], ACT.Sqrt, bias=epsv[:, 0:1]).then_inc(nrm_sqrt, 1)

            for n in range(2 * B + 1):
                if n < 2 * B:
                    newest_tap(n)
                if n >= 1:
                    silu(n - 1)
            act.wait_ge(eps_set, 2)
            norms(0)
            nc.scalar.activation(tmpv[:, 0:1], v_s[:, V_TEMP:V_TEMP + 1], ACT.Abs).then_inc(soft_a, 1)
            act.wait_ge(soft_a, 1)
            nc.scalar.activation(tmpv[:, 1:2], tmpv[:, 0:1], ACT.Exp, scale=-1.0).then_inc(soft_a, 1)
            act.wait_ge(soft_a, 2)
            nc.scalar.activation(tmpv[:, 2:3], tmpv[:, 1:2], ACT.Ln, bias=1.0).then_inc(soft_a, 1)
            act.wait_ge(br_hc, B)
            nc.scalar.activation(beta[:, :], gate_hc[:, :, 0], ACT.Sigmoid).then_inc(beta_done, 1)
            nc.scalar.activation(row1[:, :], gate_hc[:, :, 1], ACT.Sigmoid,
                                 bias=v_s[:, V_BRES:V_BRES + 1]).then_inc(res_done, 1)
            nc.scalar.activation(tmpv[:, 3:4], v_s[:, V_STATIC:V_STATIC + 1], ACT.Sigmoid).then_inc(res_done, 1)
            for m in range(8):
                act.wait_ge(fir_psum, m + 1)
                dst = (long, short)[m // 4][:, :].rearrange("p (n d) -> p d n", d=Q)[:, (m % 4) * 8:(m % 4) * 8 + 8, :]
                nc.scalar.copy(dst, ps[:, m % 4, :].rearrange("p (d n) -> p d n", d=8)).then_inc(fir_done, 1)
            for n in range(2 * B, 3 * B):
                newest_tap(n)

            def low_x_out(n, b):
                act.wait_ge(lx_psum, lv(n, b))
                nc.scalar.copy(mid[:, b * L:(b + 1) * L], ps[:, b, :]).then_inc(lx_done, 1)

            def first_squares(s):
                if s:
                    act.wait_ge(st_red, 3 * s)
                nc.scalar.activation(delta[:, :], (short, long, v_hc)[s][:, :], ACT.Square).then_inc(st_sq, 1)

            def scan_out(g):
                for c in range(C):
                    for b in group(g):
                        act.wait_ge(u_psum, sc(c, b))
                        nc.scalar.copy(hc(mid)[:, b, c, :], ps[:, b, 64:64 + Q]).then_inc(u_done, 1)

            def gate_squares(g, r):
                for b in group(g):
                    act.wait_ge(delta_done, b + 1) if r == 0 else act.wait_ge(mix_d, 3 * G * g + 2 * G + b % G + 1)
                    nc.scalar.activation(sqB[:, b * L:(b + 1) * L], (delta, o_hc)[r][:, b * L:(b + 1) * L],
                                         ACT.Square).then_inc(st_sq, 1)
                act.wait_ge(st_red, red(g, r) + 3 * G)
                cs, s = slice(g * G * C, (g + 1) * G * C), (ST_DELTA, ST_O)[r]
                nc.scalar.activation(stats[:, cs, 4 * s + 3], raw[:, s, 2, cs], ACT.Sqrt).then_inc(st_l2, 1)

            def gate_gelu(g, r):
                wide, col = ((P, V_BG1), (64, V_BOG1))[r]
                for b in group(g):
                    act.wait_ge(g_psum, gt(r, b))
                    if r == 1:
                        act.wait_ge(lg_psum, gt(0, b))
                    nc.scalar.activation(hid[0:wide, b * L:(b + 1) * L], ps[0:wide, b, :], ACT.Gelu,
                                         bias=v_s[0:wide, col:col + 1]).then_inc(g_done, 1)

            def soft_exp(g):
                cs = slice(g * G * C, (g + 1) * G * C)
                act.wait_ge(sm, SM_STEPS * g + 3)
                nc.scalar.activation(prob2[:, cs, :], prob[:, cs, :], ACT.Exp).then_inc(sm_exp, 1)

            def out_gate(g):
                cs = slice(g * G * C, (g + 1) * G * C)
                act.wait_ge(lg_hc, gt(1, (g + 1) * G - 1))
                nc.scalar.activation(row1[:, cs], gate_hc[:, cs, 0], ACT.Sigmoid,
                                     bias=v_s[:, V_BOG2:V_BOG2 + 1]).then_inc(og_sig, 1)
                act.wait_ge(og_a, 4 * g + 2)
                nc.scalar.activation(row3[:, cs], row2[:, cs], ACT.Sqrt, bias=epsv[:, 1:2]).then_inc(og_sqrt, 1)

            def first_norm(g):
                for b in group(g):
                    act.wait_ge(ln_d, 4 * b + 3)
                    t = slice(b * TT, (b + 1) * TT)
                    nc.scalar.activation(sqB[:, b * L:(b + 1) * L].rearrange("p (n d) -> p n d", n=TT), dev[:, t, :],
                                         ACT.Square).then_inc(ln_sq, 1)
                    act.wait_ge(ln_d, 4 * b + 4)
                    nc.scalar.activation(r_s[:, 2, t], r_s[:, 1, t], ACT.Sqrt, bias=epsv[:, 1:2],
                                         scale=1.0 / D).then_inc(ln_sqrt, 1)

            def sorted_out_T(g):
                for k in range(4):
                    n = min(4, SLOTS - 4 * k) * P
                    act.wait_ge(xs_psum, 4 * g + k + 1)
                    nc.scalar.copy(xsT[:, 4 * k * P:4 * k * P + n], ps[:, (4, 5, 0, 1)[k], 0:n]).then_inc(xs_done, 1)

            def relus(u, i, base):
                act.wait_ge(h_psum, i + (base + 1))
                if not (base == 0 and i is u):
                    act.wait_ge(dn_psum, i + (base - 3))
                for f in range(NF):
                    a = nc.scalar.activation(hT[:, u, f, :], ps[:, u % 2, f * P:(f + 1) * P], ACT.Relu,
                                             bias=bbuf[:, u, f:f + 1])
                a.then_inc(h_done, 1)

            def second_norm(g):
                for b in group(g):
                    act.wait_ge(fin_d, 3 * b + 2)
                    t = slice(b * TT, (b + 1) * TT)
                    nc.scalar.activation(sqB[:, b * L:(b + 1) * L].rearrange("p (n d) -> p n d", n=TT), dev[:, t, :],
                                         ACT.Square).then_inc(fin_sq, 1)
                    act.wait_ge(fin_d, 3 * b + 3)
                    nc.scalar.activation(r_s[:, 2, t], r_s[:, 1, t], ACT.Sqrt, bias=epsv[:, 1:2],
                                         scale=1.0 / D).then_inc(fin_sqrt, 1)

            for n in range(LEVELS):
                for b in group(0):
                    low_x_out(n, b)
                if n == 0:
                    silu(2 * B)
                    silu(2 * B + 1)
                if n == 1:
                    silu(2 * B + 2)
                    silu(2 * B + 3)
                if n == 2:
                    norms(1)
                    first_squares(0)
                if n == 3:
                    first_squares(1)
            scan_out(0)
            first_squares(2)
            act.wait_ge(st_red, 9)
            nc.scalar.activation(stats[:, :, 3:12:4].rearrange("p n s -> p s n"), raw[:, 0:3, 2, :],
                                 ACT.Sqrt).then_inc(st_l2, 1)
            gate_squares(0, 0)
            for n in range(LEVELS):
                for b in group(1):
                    low_x_out(n, b)
                if n == 0:
                    gate_gelu(0, 0)
                    soft_exp(0)
                if n == 1:
                    gate_squares(0, 1)
                if n == 2:
                    gate_gelu(0, 1)
                    out_gate(0)
            first_norm(0)
            for c in range(C):
                for b in group(1):
                    act.wait_ge(u_psum, sc(c, b))
                    nc.scalar.copy(hc(mid)[:, b, c, :], ps[:, b, 64:64 + Q]).then_inc(u_done, 1)
            sorted_out_T(0)
            gate_squares(1, 0)
            between = {T_GATE: lambda: gate_gelu(1, 0), T_SOFT: lambda: soft_exp(1),
                       T_STAT: lambda: gate_squares(1, 1), T_OGATE: lambda: gate_gelu(1, 1),
                       T_FACT: lambda: out_gate(1), T_NORM: lambda: first_norm(1)}
            for i in range(STEPS):
                relus(i % 4, i, 0)
                if i % 2 == 1 and i // 2 in between:
                    between[i // 2]()
            second_norm(0)
            sorted_out_T(1)
            with act.Fori(0, (STEPS - 2) // 4) as r:
                for u in range(4):
                    relus(u, r * 4 + u, STEPS)
            for u in range(2):
                relus(u, STEPS - 2 + u, STEPS)
            second_norm(1)

        @block.vector
        def _(dve):
            V = nc.vector
            srcs = (vT[:, :], kT_raw[:, :], qkT[:, 1, :])
            hcs = (v_hc, k_hc, q_hc)
            st4, v4 = hc(state), hc(v_hc[:, :])
            T4 = [P, TT, D]
            softmax_steps, small_steps = [0], [0]

            def step(i):
                softmax_steps[0] += 1
                i.then_inc(sm, 1)
                dve.wait_ge(sm, softmax_steps[0])

            def hop(i):
                small_steps[0] += 1
                i.then_inc(rt, 1)
                dve.wait_ge(rt, small_steps[0])

            def chunks(g):
                return slice(g * G * C, (g + 1) * G * C)

            def older_taps(n):
                s, b = TAPS[n]
                dve.wait_ge(tap3_done, n + 1)
                for k in range(1, 4):
                    y = srcs[s][:, b * L + k:(b + 1) * L]
                    c = V_CONV + 4 * s + 3 - k
                    if k > 1:
                        dve.wait_ge(tap2_done, 2 * n + k - 1)
                    V.scalar_tensor_tensor(out=y, in0=ps[:, TAP_BANK[n], 0:L - k], scalar=v_s[:, c:c + 1], in1=y,
                                           op0=ALU.mult, op1=ALU.add).then_inc(taps_done if k == 3 else tap2_done, 1)

            def to_hc(n):
                s, b = TAPS[n]
                dve.wait_ge(silu_done, n + 1)
                V.transpose(hcs[s][:, b * L:(b + 1) * L], srcs[s][:, b * L:(b + 1) * L]).then_inc(hc_done, 1)

            def norms(g):
                for n in range(B + 2 * G * g, B + 2 * G * (g + 1)):
                    s, b = TAPS[n]
                    dve.wait_ge(sq_done, n - B + 1)
                    V.tensor_reduce(norm[:, s - 1, b * C:(b + 1) * C], hc((sqA, sqB)[s - 1][:, :])[:, b, :, :], AX.X,
                                    ALU.add).then_inc(ssq_done, 1)

            def unit_k(g):
                dve.wait_ge(nrm_sqrt, g + 1)
                V.reciprocal(norm[:, :, chunks(g)], nrm1[:, :, chunks(g)]).then_inc(nrm_done, 1)
                dve.wait_ge(nrm_done, g + 1)
                for b in group(g):
                    k = hc(k_hc[:, :])[:, b, :, :]
                    V.tensor_tensor(k, k, over(norm[:, 0, b * C:(b + 1) * C].unsqueeze(2), FULL),
                                    ALU.mult).then_inc(kn_done, 1)
                    dve.wait_ge(kn_done, b + 1)
                    V.transpose(qkT[:, 0, b * L:(b + 1) * L], k_hc[:, b * L:(b + 1) * L]).then_inc(knT_done, 1)

            def triangles(g):
                for b in group(g):
                    dve.wait_ge(gram_psum, b + 1)
                    dve.wait_ge(nbm_done, b + 1)
                    for half in range(2):
                        gram = ps[:, b + 4 * half, :].rearrange("p (c x) -> p c x", x=2 * Q)
                        cs = slice(half * 8, half * 8 + 8)
                        V.tensor_tensor(hc(low)[:, b, cs, :], gram[:, :, 0:Q], hc(nbm)[:, b, cs, :],
                                        ALU.mult).then_inc(low_done, 1)
                    dve.wait_ge(low_done, 2 * b + 2)
                    V.transpose(lowT[:, b * L:(b + 1) * L], low[:, b * L:(b + 1) * L]).then_inc(lowT_done, 1)
                    for half in range(2):
                        gram = ps[:, b + 4 * half, :].rearrange("p (c x) -> p c x", x=2 * Q)
                        cs = slice(half * 8, half * 8 + 8)
                        a = V.tensor_tensor(hc(attnT)[:, b, cs, :], gram[:, :, Q:2 * Q], over(uincl, [P, 8, Q]),
                                            ALU.mult)
                    a.then_inc(attn_done, 1)
                for b in group(g):
                    dve.wait_ge(pair_done, b + 1)
                    V.transpose(invT[:, b * L:(b + 1) * L], inv[:, b * L:(b + 1) * L]).then_inc(invT_done, 1)

            def level(g, n):
                for b in group(g):
                    dve.wait_ge(xlx_psum, lv(n, b))
                    V.copy_predicated(hc(inv)[:, b, :, :], over(lmask_s[:, n, :].unsqueeze(1), FULL),
                                      ps[:, 4 + b, :].rearrange("p (c d) -> p c d", c=C)).then_inc(inv_done, 1)
                    dve.wait_ge(inv_done, lv(n, b))
                    V.transpose(invT[:, b * L:(b + 1) * L], inv[:, b * L:(b + 1) * L]).then_inc(invT_done, 1)
                    if n == LEVELS - 1:
                        dve.wait_ge(invT_done, ivt(n + 1, b))
                        t = hc(invT)[:, b, :, :]
                        V.tensor_tensor(t, t, over(beta[:, b * C:(b + 1) * C].unsqueeze(2), FULL),
                                        ALU.mult).then_inc(tb_done, 1)

            def scan_step(g, c):
                for b in group(g):
                    if c == 0:
                        V.tensor_copy(chain[:, b, :], v4[:, b, c, :]).then_inc(rhs_done, 1)
                    else:
                        dve.wait_ge(ks_psum, sl(c - 1, b))
                        V.tensor_tensor(chain[:, b, :], v4[:, b, c, :], ps[:, b, 0:Q], ALU.subtract).then_inc(rhs_done, 1)
                if c < C - 1:
                    for b in group(g):
                        dve.wait_ge(ds_psum, sl(c, b))
                        d_ = ps[:, b, 128:128 + Q]
                        if c == 0:
                            V.tensor_copy(st4[:, b, 1, :], d_).then_inc(s_done, 1)
                        else:
                            dve.wait_ge(s_done, sl(c - 1, b))
                            V.tensor_tensor(st4[:, b, c + 1, :], st4[:, b, c, :], d_, ALU.add).then_inc(s_done, 1)

            def sums(src, squares, s, b0, b1, count):
                cs = slice(b0 * C, b1 * C)
                v = src.rearrange("p (n d) -> p n d", d=Q)[:, cs, :]
                V.tensor_reduce(raw[:, s, 0, cs], v, AX.X, ALU.add).then_inc(st_red, 1)
                V.tensor_reduce(raw[:, s, 1, cs], v, AX.X, ALU.add, apply_absolute_value=True).then_inc(st_red, 1)
                dve.wait_ge(st_sq, count)
                V.tensor_reduce(raw[:, s, 2, cs], squares.rearrange("p (n d) -> p n d", d=Q)[:, cs, :], AX.X,
                                ALU.add).then_inc(st_red, 1)

            def small_stats(s0, s1, cs, k):
                slot = stats[:, cs, 4 * s0:4 * s1].rearrange("p n (s k) -> p k s n", k=4)
                V.tensor_scalar(slot[:, 0], raw[:, s0:s1, 0, cs], 1.0 / Q, None, ALU.mult).then_inc(st_small, 1)
                V.tensor_scalar(slot[:, 2], raw[:, s0:s1, 1, cs], 1.0 / Q, None, ALU.mult).then_inc(st_small, 1)
                V.tensor_scalar(m1[:, s0:s1, cs], raw[:, s0:s1, 0, cs], 1.0 / Q, None, ALU.mult).then_inc(st_small, 1)
                dve.wait_ge(st_small, 3 * k + 3)
                V.tensor_tensor(m2[:, s0:s1, cs], m1[:, s0:s1, cs], m1[:, s0:s1, cs], ALU.mult).then_inc(st_m2, 1)
                dve.wait_ge(st_m2, k + 1)
                for s in range(s0, s1):
                    V.scalar_tensor_tensor(out=stats[:, cs, 4 * s + 1], in0=raw[:, s, 2, cs], scalar=1.0 / Q,
                                           in1=m2[:, s, cs], op0=ALU.mult, op1=ALU.subtract).then_inc(st_var, 1)

            def scan_result(g):
                for b in group(g):
                    dve.wait_ge(o_psum, b + 1)
                    V.tensor_tensor(hc(delta)[:, b, :, :], ps[:, 4 + b, :].rearrange("p (c d) -> p c d", c=C),
                                    over(norm[:, 1, b * C:(b + 1) * C].unsqueeze(2), FULL),
                                    ALU.mult).then_inc(delta_done, 1)

            def gate_stats(g, r):
                s, src = ((ST_DELTA, delta), (ST_O, o_hc))[r]
                for b in group(g):
                    dve.wait_ge(delta_done, b + 1) if r == 0 else dve.wait_ge(mix_d, 3 * G * g + 2 * G + b % G + 1)
                    sums(src, sqB[:, :], s, b, b + 1, 3 + gt(r, b))
                dve.wait_ge(st_red, red(g, r) + 3 * G)
                small_stats(s, s + 1, chunks(g), 1 + 2 * g + r)
                dve.wait_ge(st_var, 4 + 2 * g + r)
                dve.wait_ge(st_l2, 2 + 2 * g + r)
                for b in group(g):
                    if r == 1:
                        dve.wait_ge(g_psum, gt(0, b))
                    V.transpose(statsT[:, b * L:(b + 1) * L], stats[:, b * C:(b + 1) * C, :].rearrange(
                        "p a b -> p (a b)")).then_inc(stT_done, 1)

            def logits_hc(g, r):
                for b in group(g):
                    dve.wait_ge(lg_psum, gt(r, b))
                    V.transpose(gate_hc[:, b * C:(b + 1) * C, :].rearrange("p a b -> p (a b)"),
                                ps[:, 4 + b, :]).then_inc(lg_hc, 1)

            def softmax(g):
                logits_hc(g, 0)
                cs, n = chunks(g), G * C
                W4 = [P, n, 4]
                dve.wait_ge(lg_hc, gt(0, (g + 1) * G - 1))
                dve.wait_ge(soft_c, 1)
                step(V.tensor_tensor(prob2[:, cs, :], gate_hc[:, cs, 0:4],
                                     over(v_s[:, V_BG2:V_BG2 + 4].unsqueeze(1), W4), ALU.add))
                step(V.tensor_reduce(row1[:, cs], prob2[:, cs, :], AX.X, ALU.max))
                V.tensor_tensor(prob2[:, cs, :], prob2[:, cs, :], over(row1[:, cs].unsqueeze(2), W4),
                                ALU.subtract).then_inc(soft_c, 1)
                dve.wait_ge(soft_c, 2 + g)
                step(V.tensor_scalar(prob[:, cs, :], prob2[:, cs, :], tmpv[:, 5:6], None, ALU.mult))
                dve.wait_ge(sm_exp, g + 1)
                step(V.tensor_reduce(row1[:, cs], prob2[:, cs, :], AX.X, ALU.add))
                step(V.reciprocal(row2[:, cs], row1[:, cs]))
                step(V.tensor_tensor(prob[:, cs, :], prob2[:, cs, :], over(row2[:, cs].unsqueeze(2), W4), ALU.mult))
                step(V.tensor_scalar(prob2[:, cs, :], prob[:, cs, :], FLOOR, None, ALU.max))
                step(V.tensor_reduce(row1[:, cs], prob2[:, cs, :], AX.X, ALU.add))
                step(V.reciprocal(row2[:, cs], row1[:, cs]))
                step(V.tensor_tensor(prob[:, cs, :], prob2[:, cs, :], over(row2[:, cs].unsqueeze(2), W4), ALU.mult))
                step(V.tensor_tensor(coef[:, cs], prob[:, cs, 0], sgate[:, cs], ALU.add))

            def mix(g):
                for b in group(g):
                    cs, ls = slice(b * C, (b + 1) * C), slice(b * L, (b + 1) * L)
                    V.tensor_tensor(hc(o_hc)[:, b, :, :], hc(short[:, :])[:, b, :, :],
                                    over(coef[:, cs].unsqueeze(2), FULL), ALU.mult).then_inc(mix_d, 1)
                    V.tensor_tensor(hc(delta)[:, b, :, :], hc(delta)[:, b, :, :],
                                    over(prob[:, cs, 2].unsqueeze(2), FULL), ALU.mult).then_inc(soft_b, 1)
                    dve.wait_ge(mix_d, 3 * G * g + 2 * (b % G) + 1)
                    dve.wait_ge(soft_b, b + 2)
                    V.tensor_tensor(o_hc[:, ls], o_hc[:, ls], delta[:, ls], ALU.add).then_inc(mix_d, 1)
                for b in group(g):
                    ls = slice(b * L, (b + 1) * L)
                    dve.wait_ge(mix_d, 3 * G * g + 2 * G)
                    dve.wait_ge(mix_p, 3 * (b + 1))
                    V.tensor_tensor(o_hc[:, ls], o_hc[:, ls], mixA[:, ls], ALU.add).then_inc(mix_d, 1)

            def factor(g):
                logits_hc(g, 1)
                cs = chunks(g)
                dve.wait_ge(og_sig, g + 1)
                V.tensor_tensor(row3[:, cs], row1[:, cs], row1[:, cs], ALU.mult).then_inc(og_a, 1)
                dve.wait_ge(og_a, 4 * g + 1)
                V.scalar_tensor_tensor(out=row2[:, cs], in0=raw[:, ST_O, 2, cs], scalar=1.0 / Q, in1=row3[:, cs],
                                       op0=ALU.mult, op1=ALU.mult).then_inc(og_a, 1)
                dve.wait_ge(og_sqrt, g + 1)
                V.reciprocal(row2[:, cs], row3[:, cs]).then_inc(og_a, 1)
                dve.wait_ge(og_a, 4 * g + 3)
                V.tensor_tensor(coef[:, cs], row1[:, cs], row2[:, cs], ALU.mult).then_inc(og_a, 1)
                dve.wait_ge(og_a, 4 * g + 4)
                for b in group(g):
                    o = hc(o_hc)[:, b, :, :]
                    V.tensor_tensor(o, o, over(coef[:, b * C:(b + 1) * C].unsqueeze(2), FULL),
                                    ALU.mult).then_inc(of_done, 1)
                    dve.wait_ge(of_done, b + 1)
                    V.transpose(oT[:, b * L:(b + 1) * L], o_hc[:, b * L:(b + 1) * L]).then_inc(oT_done, 1)

            def first_norm(g):
                for b in group(g):
                    t = slice(b * TT, (b + 1) * TT)
                    dve.wait_ge(wo_psum, b + 1)
                    V.tensor_tensor(x_tok[:, t, :], x_tok[:, t, :], ps[:, b, :].rearrange("p (n d) -> p n d", n=TT),
                                    ALU.add).then_inc(ln_d, 1)
                    dve.wait_ge(ln_d, 4 * b + 1)
                    V.tensor_reduce(r_s[:, 0, t], x_tok[:, t, :], AX.X, ALU.add).then_inc(ln_d, 1)
                    dve.wait_ge(ln_d, 4 * b + 2)
                    hop(V.tensor_scalar(r_s[:, 0, t], r_s[:, 0, t], 1.0 / D, None, ALU.mult))
                    V.tensor_tensor(dev[:, t, :], x_tok[:, t, :], over(r_s[:, 0, t].unsqueeze(2), T4),
                                    ALU.subtract).then_inc(ln_d, 1)
                    dve.wait_ge(ln_sq, b + 1)
                    V.tensor_reduce(r_s[:, 1, t], sqB[:, b * L:(b + 1) * L].rearrange("p (n d) -> p n d", n=TT), AX.X,
                                    ALU.add).then_inc(ln_d, 1)
                    dve.wait_ge(ln_sqrt, b + 1)
                    hop(V.reciprocal(r_s[:, 3, t], r_s[:, 2, t]))
                    V.tensor_tensor(x1[:, t, :], dev[:, t, :], over(r_s[:, 3, t].unsqueeze(2), T4),
                                    ALU.mult).then_inc(x1_done, 1)

            def first_experts(g):
                t, n = slice(g * GT, (g + 1) * GT), GT
                dve.wait_ge(x1_done, (g + 1) * G)
                hop(V.tensor_tensor(r_s[:, 0, t], x1[:, t, 0], x1[:, t, 1], ALU.add))
                hop(V.tensor_scalar(r_s[:, 1, t], r_s[:, 0, t], -1.0, None, ALU.mult))
                hop(V.tensor_tensor(r_s[:, 2, t], r_s[:, 0, t], r_s[:, 1, t], ALU.max))
                hop(V.tensor_tensor(ge[:, :, :], over(r_s[:, 2, t].unsqueeze(2), [P, n, 16]),
                                    over(cst_s[:, C_STEP:C_STEP + 16].unsqueeze(1), [P, n, 16]), ALU.is_ge))
                hop(V.tensor_reduce(r_s[:, 3, t], ge[:, :, :], AX.X, ALU.add))
                hop(V.tensor_scalar(r_s[:, 4, t], r_s[:, 0, t], 0.0, 2.0, ALU.is_ge, ALU.mult))
                hop(V.tensor_scalar(r_s[:, 5, t], r_s[:, 4, t], -1.0, None, ALU.add))
                hop(V.tensor_tensor(r_s[:, 4, t], r_s[:, 3, t], r_s[:, 5, t], ALU.mult))
                hop(V.tensor_tensor(eq[:, :, :], over(r_s[:, 4, t].unsqueeze(2), [P, n, 32]),
                                    over(cst_s[:, C_VAL:C_VAL + 32].unsqueeze(1), [P, n, 32]), ALU.is_equal))
                V.tensor_reduce(me[:, g, 0:GT, :], eq[:, :, :].rearrange("p n (g e) -> p n e g", e=NE), AX.X,
                                ALU.add).then_inc(me_done, 1)

            def places(g):
                t = slice(g * GT, (g + 1) * GT)
                EE, SE = [P, NE, NE], [P, SLOTS, NE]
                dve.wait_ge(rank_psum, g + 1)
                hop(V.tensor_copy(rank[:, :, :].rearrange("p n e -> p (n e)"), ps[:, 4, 0:(GT + 1) * NE]))
                hop(V.tensor_tensor(fit[:, 0:NE, :], over(rank[:, GT, :].unsqueeze(2), EE),
                                    over(cst_s[:, C_FULL:C_FULL + NE].unsqueeze(1), EE), ALU.is_ge))
                hop(V.tensor_reduce(cnt[:, 0, :], fit[:, 0:NE, :], AX.X, ALU.add))
                hop(V.tensor_tensor(fit[:, 0:NE, :], over(cnt[:, 0, :].unsqueeze(1), EE),
                                    cst_s[:, C_BEFORE:C_BEFORE + NE * NE].rearrange("p (a b) -> p a b", a=NE), ALU.mult))
                hop(V.tensor_reduce(cnt[:, 1, :], fit[:, 0:NE, :], AX.X, ALU.add))
                hop(V.scalar_tensor_tensor(out=rank[:, 0:GT, :], in0=over(cnt[:, 1, :].unsqueeze(1), [P, GT, NE]),
                                           scalar=float(P), in1=rank[:, 0:GT, :], op0=ALU.mult, op1=ALU.add))
                hop(V.tensor_tensor(rank[:, 0:GT, :], rank[:, 0:GT, :], me[:, g, 0:GT, :], ALU.mult))
                hop(V.tensor_reduce(place[:, t], rank[:, 0:GT, :], AX.X, ALU.add))
                V.tensor_copy(place_i[:, t], place[:, t]).then_inc(place_done, 1)
                hop(V.tensor_tensor(cnt[:, 2, :], cnt[:, 1, :], cnt[:, 0, :], ALU.add))
                hop(V.scalar_tensor_tensor(out=fit[:, :, :],
                                           in0=over(cst_s[:, C_STEP:C_STEP + SLOTS].unsqueeze(2), SE), scalar=-1.0,
                                           in1=over(cnt[:, 2, :].unsqueeze(1), SE), op0=ALU.add, op1=ALU.is_ge))
                hop(V.tensor_reduce(tile_e[:, 0, :], fit[:, :, :], AX.X, ALU.add))
                hop(V.tensor_scalar(tile_e[:, 0, :], tile_e[:, 0, :], NE - 1.0, None, ALU.min))
                hop(V.tensor_scalar(tile_e[:, 1, :], tile_e[:, 0, :], NE - 1.0, float(-NE), ALU.is_ge, ALU.mult))
                hop(V.scalar_tensor_tensor(out=tile_e[:, 2, :], in0=tile_e[:, 0, :], scalar=1.0, in1=tile_e[:, 1, :],
                                           op0=ALU.add, op1=ALU.add))
                hop(V.tensor_copy(tile_i[:, g, :, :], tile_e[:, 0:3:2, :]))

            def expert(g, k, j):
                return nc.values_load(tile_i[0:1, g, k, j], engines=(mybir.EngineType.DVE,), min_val=0,
                                      max_val=NE - 1, skip_runtime_bounds_check_because="the counts are cut to NE - 1")

            def fetch(g, u, i, j, base):
                for k in range(2):
                    if not (base == 0 and i is u):
                        dve.wait_ge(dn_psum, i + (base - 3 + k))
                    e = expert(g, k, j)
                    if k == 0:
                        first = e
                    V.tensor_copy(wbuf[:, u + k, :], arena[:, bass.ds(e, 1), 0:2 * FF].rearrange("p a n -> p (a n)"))
                    V.tensor_copy(bbuf[:, u + k, :], b1tab[:, bass.ds(e, 1), :].rearrange("p a f -> p (a f)")
                                  ).then_inc(wb_done, 1)
                return first

            def fetch_bias(u, e, taken=0):
                if not (isinstance(taken, int) and taken == 0):
                    dve.wait_ge(y_done, taken)
                V.tensor_copy(b2buf[:, u // 2, :], b2pair[:, bass.ds(e, 1), :].rearrange("p a d -> p (a d)")
                              ).then_inc(bias_done, 1)

            def take(u, j, y, base):
                dve.wait_ge(dn_psum, j * 2 + (base + 2))
                dve.wait_ge(bias_done, j + (base // 2 + 1))
                V.scalar_tensor_tensor(out=y, in0=ps[:, 4 + u // 2, 0:P], scalar=0.5, in1=b2buf[:, u // 2, :],
                                       op0=ALU.mult, op1=ALU.add).then_inc(y_done, 1)

            def second_norm(g):
                for b in group(g):
                    t = slice(b * TT, (b + 1) * TT)
                    dve.wait_ge(y_in[g], 16 * GT)
                    V.tensor_tensor(x1[:, t, :], x1[:, t, :], y_tok[:, t, :], ALU.add).then_inc(fin_d, 1)
                    dve.wait_ge(fin_d, 3 * b + 1)
                    hop(V.tensor_reduce(r_s[:, 0, t], x1[:, t, :], AX.X, ALU.add))
                    hop(V.tensor_scalar(r_s[:, 3, t], r_s[:, 0, t], 1.0 / D, None, ALU.mult))
                    V.tensor_tensor(dev[:, t, :], x1[:, t, :], over(r_s[:, 3, t].unsqueeze(2), T4),
                                    ALU.subtract).then_inc(fin_d, 1)
                    dve.wait_ge(fin_sq, b + 1)
                    V.tensor_reduce(r_s[:, 1, t], sqB[:, b * L:(b + 1) * L].rearrange("p (n d) -> p n d", n=TT), AX.X,
                                    ALU.add).then_inc(fin_d, 1)
                    dve.wait_ge(fin_sqrt, b + 1)
                    hop(V.reciprocal(r_s[:, 4, t], r_s[:, 2, t]))
                    V.tensor_tensor(x_tok[:, t, :], dev[:, t, :], over(r_s[:, 4, t].unsqueeze(2), T4),
                                    ALU.mult).then_inc(fin_done, 1)

            dve.wait_ge(v_in, 16)
            for n in range(2 * B):
                older_taps(n)
                if n >= 2:
                    to_hc(n - 2)
                if n == B + 1:
                    for i in range(B):
                        dve.wait_ge(br_psum, i + 1)
                        V.transpose(gate_hc[:, i * C:(i + 1) * C, :].rearrange("p a b -> p (a b)"),
                                    ps[:, i, :]).then_inc(br_hc, 1)
            to_hc(2 * B - 2)
            to_hc(2 * B - 1)
            norms(0)
            unit_k(0)
            dve.wait_ge(soft_a, 3)
            V.tensor_scalar(tmpv[:, 4:5], v_s[:, V_TEMP:V_TEMP + 1], 0.0, tmpv[:, 2:3], ALU.max,
                            ALU.add).then_inc(soft_b, 1)
            dve.wait_ge(soft_b, 1)
            V.reciprocal(tmpv[:, 5:6], tmpv[:, 4:5]).then_inc(soft_c, 1)
            dve.wait_ge(res_done, 2)
            V.tensor_scalar(sgate[:, :], row1[:, :], tmpv[:, 3:4], None, ALU.mult).then_inc(sgate_done, 1)
            dve.wait_ge(fir_psum, 8)
            triangles(0)
            older_taps(2 * B)
            older_taps(2 * B + 1)
            dve.wait_ge(lm_in, 16)
            for n in range(LEVELS):
                level(0, n)
                if n == 0:
                    to_hc(2 * B)
                    to_hc(2 * B + 1)
                    older_taps(2 * B + 2)
                    older_taps(2 * B + 3)
                if n == 1:
                    to_hc(2 * B + 2)
                    to_hc(2 * B + 3)
                    norms(1)
                if n == 2:
                    unit_k(1)
                    sums(short[:, :], delta, ST_SHORT, 0, B, 1)
            for c in range(C):
                scan_step(0, c)
            sums(long[:, :], delta, ST_LONG, 0, B, 2)
            sums(v_hc[:, :], delta, ST_V, 0, B, 3)
            dve.wait_ge(st_red, 9)
            dve.wait_ge(misc, 1)
            small_stats(0, 3, slice(0, BC), 0)
            scan_result(0)
            triangles(1)
            gate_stats(0, 0)
            level(1, 0)
            softmax(0)
            mix(0)
            level(1, 1)
            gate_stats(0, 1)
            level(1, 2)
            factor(0)
            first_norm(0)
            dve.wait_ge(zero_set, 1)
            first_experts(0)
            level(1, 3)
            for c in range(C):
                scan_step(1, c)
                if c == 1:
                    places(0)
            scan_result(1)
            gate_stats(1, 0)
            dve.wait_ge(w_all, 16 * (2 * NE + 1))
            dve.wait_ge(b2_done, 1)
            between = {T_SOFT - 1: lambda: (softmax(1), mix(1)), T_STAT - 1: lambda: gate_stats(1, 1),
                       T_FACT - 1: lambda: factor(1), T_NORM - 1: lambda: first_norm(1)}
            fetch_bias(0, fetch(0, 0, 0, slice(0, 1), 0))
            fetch_bias(2, fetch(0, 2, 2, slice(1, 2), 0))
            for j in range(SLOTS):
                if j + 2 < SLOTS:
                    e = fetch(0, 2 * j % 4, 2 * j + 4, slice(j + 2, j + 3), 0)
                take(2 * j % 4, j, ys[:, j, :], 0)
                if j + 2 < SLOTS:
                    fetch_bias(2 * j % 4, e, j + 1)
                if j in between:
                    between[j]()
            first_experts(1)
            places(1)
            fetch_bias(0, fetch(1, 0, 0, slice(0, 1), STEPS), SLOTS)
            fetch_bias(2, fetch(1, 2, 2, slice(1, 2), STEPS), SLOTS)
            second_norm(0)
            with dve.Fori(0, (SLOTS - 3) // 2) as r:
                for k in range(2):
                    e = fetch(1, 2 * k, r * 4 + (2 * k + 4), bass.ds(r * 2 + (k + 2), 1), STEPS)
                    take(2 * k, r * 2 + k, ys[:, bass.ds(r * 2 + k, 1), :].rearrange("p a d -> p (a d)"), STEPS)
                    fetch_bias(2 * k, e, r * 2 + (SLOTS + k + 1))
            for j in range(SLOTS - 3, SLOTS):
                if j + 2 < SLOTS:
                    e = fetch(1, 2 * j % 4, 2 * j + 4, slice(j + 2, j + 3), STEPS)
                take(2 * j % 4, j, ys[:, j, :], STEPS)
                if j + 2 < SLOTS:
                    fetch_bias(2 * j % 4, e, SLOTS + j + 1)
            second_norm(1)

        @block.gpsimd
        def _(pool):
            gp = nc.gpsimd
            w5 = win[:, :, :, :].rearrange("p h (b c) d -> p h b (c d)", b=B)
            for h in range(H):
                z = gp.memset(w5[:, h, :, 0:2 * Q], 0.0)
            z.then_inc(win_zero, 1)
            gp.memset(zero[:, :], 0.0)
            gp.memset(me[:, :, :, :], 0.0).then_inc(zero_set, 1)
            gp.memset(epsv[:, 0:1], L2_EPS).then_inc(eps_set, 1)
            gp.memset(epsv[:, 1:2], EPS).then_inc(eps_set, 1)
            pool.wait_ge(w_in, 16)
            pool.wait_ge(v_in, 16)
            gp.tensor_scalar(w_s[:, W_GS:W_ALL], w_s[:, W_GS:W_ALL], 1.0 / H, None, ALU.mult).then_inc(ws_scaled, 1)
            gp.tensor_scalar(w_s[:, W_O:W_O + P], w_s[:, W_O:W_O + P], v_s[:, V_NORM:V_NORM + 1], None,
                             ALU.mult).then_inc(wo_scaled, 1)

            def squares(n):
                s, b = TAPS[n]
                src = (k_hc, q_hc)[s - 1][:, b * L:(b + 1) * L]
                pool.wait_ge(hc_done, n + 1)
                gp.tensor_tensor((sqA, sqB)[s - 1][:, b * L:(b + 1) * L], src, src, ALU.mult).then_inc(sq_done, 1)

            def beta_masks(g):
                pool.wait_ge(ssq_done, 2 * G * (g + 1))
                for b in group(g):
                    gp.tensor_tensor(hc(nbm)[:, b, :, :], over(nstrict, FULL),
                                     over(beta[:, b * C:(b + 1) * C].unsqueeze(2), FULL), ALU.mult).then_inc(nbm_done, 1)

            def pairs(g):
                for b in group(g):
                    pool.wait_ge(low_done, 2 * b + 2)
                    x_ = hc(inv)[:, b, :, :]
                    gp.tensor_tensor(x_, hc(low)[:, b, :, :], over(pair, FULL), ALU.mult).then_inc(state0, 1)
                    pool.wait_ge(state0, b + 1)
                    gp.tensor_tensor(x_, x_, over(eye, FULL), ALU.add).then_inc(pair_done, 1)

            def mix(g):
                pool.wait_ge(sm, SM_STEPS * g + SM_STEPS - 1)
                pool.wait_ge(o_psum, (g + 1) * G)
                for b in group(g):
                    cs, ls = slice(b * C, (b + 1) * C), slice(b * L, (b + 1) * L)
                    gp.tensor_tensor(hc(mixA)[:, b, :, :], hc(v_hc[:, :])[:, b, :, :],
                                     over(prob[:, cs, 3].unsqueeze(2), FULL), ALU.mult).then_inc(mix_p, 1)
                    gp.tensor_tensor(hc(mixB)[:, b, :, :], hc(long[:, :])[:, b, :, :],
                                     over(prob[:, cs, 1].unsqueeze(2), FULL), ALU.mult).then_inc(mix_p, 1)
                    pool.wait_ge(mix_p, 3 * b + 2)
                    gp.tensor_tensor(mixA[:, ls], mixA[:, ls], mixB[:, ls], ALU.add).then_inc(mix_p, 1)

            for n in range(B, 2 * B):
                squares(n)
            gp.memset(stats[:, :, :], 0.0).then_inc(misc, 1)
            pool.wait_ge(beta_done, 1)
            pool.wait_ge(c_in, 16)
            beta_masks(0)
            pairs(0)
            for n in range(2 * B, 3 * B):
                squares(n)
            beta_masks(1)
            pairs(1)
            mix(0)
            pool.wait_ge(b2_in, 16)
            gp.tensor_tensor(b2pair[:, 0:NE - 1, :], b2in[:, 0:NE - 1, :], b2in[:, 1:NE, :], ALU.add)
            gp.tensor_tensor(b2pair[:, NE - 1, :], b2in[:, NE - 1, :], b2in[:, 0, :], ALU.add).then_inc(pair_sum, 1)
            pool.wait_ge(pair_sum, 1)
            gp.tensor_scalar(b2pair, b2pair, 0.5, None, ALU.mult).then_inc(b2_done, 1)

            def scatter(g):
                pool.wait_ge(place_done, g + 1)
                pool.wait_ge(filled, 32)
                for n in range(g * GT, (g + 1) * GT):
                    gp.indirect_dma_start(sorted_in[g], bass.IndirectOffsetOnAxis(place_i[:, n:n + 1], 0),
                                          x1[:, n, :], None).then_inc(scattered[g], 16)

            def gather(g):
                pool.wait_ge(ys_out[g], 16 * 3)
                for n in range(g * GT, (g + 1) * GT):
                    gp.indirect_dma_start(y_tok[:, n, :], None, sorted_out[g],
                                          bass.IndirectOffsetOnAxis(place_i[:, n:n + 1], 0)).then_inc(y_in[g], 16)

            scatter(0)
            mix(1)
            gather(0)
            scatter(1)
            gather(1)


def toeplitz(taps):
    n = taps.shape[1]
    block = np.zeros((WIN, Q, P), taps.dtype)
    for i in range(Q):
        block[2 * Q + i - n + 1:2 * Q + i + 1, i, :] = taps.T
    return block.reshape(WIN, Q * P)


def laid_out(a):
    f = {k.replace("L0_attn_", "").replace("L0_ffn_", "f_"): np.asarray(v) for k, v in a.items()}
    z = np.float32
    wall = np.zeros((P, W_ALL), z)
    for at, name in ((W_Q, "Wq"), (W_K, "Wk"), (W_V, "Wv"), (W_O, "Wo")):
        wall[:, at:at + P] = f[name]
    wall[:, W_G:W_G + P] = f["Wg1"][:D]
    wall[:, W_OG:W_OG + 64] = f["Wog1"][:D]
    given = (0, 1, 3, 2)
    for h in range(H):
        wall[:, W_BR + h * Q] = f["Wb"][:, h]
        wall[:, W_BR + h * Q + 1] = f["Wres"][:, h]
        wall[:, W_G2 + h * Q:W_G2 + h * Q + 4] = f["Wg2"]
        wall[:64, W_OG2 + h * Q] = f["Wog2"][:, 0]
        for s in range(4):
            r = h * Q + 4 * s
            wall[r:r + 4, W_GS:W_GS + P] = f["Wg1"][D + 4 * given[s]:D + 4 * given[s] + 4]
        wall[h * Q + 4 * ST_O:h * Q + 4 * ST_O + 4, W_OGS:W_OGS + 64] = f["Wog1"][D:D + 4]
        wall[h * Q + 4 * ST_V:h * Q + 4 * ST_V + 4, W_OGS:W_OGS + 64] = f["Wog1"][D + 4:D + 8]
    vecs = np.zeros((P, V_ALL), z)
    for s, name in enumerate(("wv_conv", "wk_conv", "wq_conv")):
        vecs[:, V_CONV + 4 * s:V_CONV + 4 * s + 4] = f[name]
    vecs[:, V_BG1] = f["bg1"]
    vecs[:64, V_BOG1] = f["bog1"]
    vecs[:, V_BG2:V_BG2 + 4] = f["bg2"]
    vecs[:, V_TEMP] = f["logit_temp"][0]
    vecs[:, V_BOG2] = f["bog2"][0]
    vecs[:, V_BRES] = np.repeat(f["bres"], Q)
    vecs[:, V_STATIC] = np.repeat(f["conv_res_logit"], Q)
    vecs[:, V_NORM] = np.tile(f["norm_w"], H)
    fir_l, fir_s = toeplitz(f["fir_long"].reshape(P, 64)), toeplitz(f["fir_short"].reshape(P, 5))
    cst, lmask = shape_constants()
    return {
        "x": f["hidden_states"].reshape(N, D), "cst": cst, "lmask": lmask, "wall": wall, "vecs": vecs,
        "fir_l": fir_l, "fir_s": fir_s, "w1": f["f_W1"],
        "b1": f["f_b1"].reshape(NE, NF, P).transpose(0, 2, 1), "w2": f["f_W2"], "b2": f["f_b2"],
    }


def kernel(**inputs):
    import concourse.bacc as _bacc
    from concourse.bass_utils import run_bass_kernel_spmd as _run

    nc = _bacc.Bacc("TRN2", target_bir_lowering=False, num_devices=1)
    arrays, args = {}, []
    for name, a in laid_out(inputs).items():
        a = np.ascontiguousarray(a)
        arrays[f"in_{name}_dram"] = a
        args.append(nc.dram_tensor(f"in_{name}_dram", a.shape, mybir.dt.from_np(a.dtype), kind="ExternalInput").ap())
    for name in ("sorted_in", "sorted_out"):
        args.append([nc.dram_tensor(f"{name}{g}", (SLOTS * P, D), F32, kind="Internal").ap() for g in range(2)])
    args.append(nc.dram_tensor("out_0_dram", (N, D), F32, kind="ExternalOutput").ap())
    post_ln_block(nc, *args)
    r = _run(nc, [arrays], core_ids=[0])
    return r.results[0]["out_0_dram"].reshape(B, L, D)
```

```python
from contextlib import ExitStack

import numpy as np

import concourse.bass as bass
from concourse import mybir

F32 = mybir.dt.float32
I32 = mybir.dt.int32
BF16 = mybir.dt.bfloat16
ALU = mybir.AluOpType
ACT = mybir.ActivationFunctionType
AX = mybir.AxisListType

P = 128
B, L, D = 4, 512, 128
H = 4
Q = 32
C = L // Q
BC = B * C
TT = L // P
NT = B * TT
N = B * L
NE = 8
FF = 512
NF = FF // P
WIN = 3 * Q
EPS = 1e-5
L2_EPS = 1e-6
FLOOR = 0.02

C_ID, C_NSTRICT, C_UINCL, C_EYE, C_PAIR, C_STEP, C_VAL, C_LESS = 0, 128, 160, 192, 224, 256, 272, 304
C_FULL, C_BEFORE = C_LESS + P, C_LESS + P + NE
C_TOKEN = C_BEFORE + NE * NE
C_ALL = C_TOKEN + NT
W_Q, W_K, W_V, W_G, W_O, W_OG, W_BR, W_G2, W_OG2, W_GS, W_OGS = 0, 128, 256, 384, 512, 640, 704, 832, 960, 1088, 1216
W_ALL = W_OGS + 64
V_CONV, V_BG1, V_BOG1, V_BG2, V_TEMP, V_BOG2, V_BRES, V_STATIC, V_NORM, V_SHORT = 0, 12, 13, 14, 18, 19, 20, 21, 22, 23
KS = 5
V_ALL = V_SHORT + KS

G = 2
TAPS = [(0, 0), (0, 1), (0, 2), (0, 3), (1, 0), (1, 1), (2, 0), (2, 1), (1, 2), (1, 3), (2, 2), (2, 3)]
Q_SOURCE = 2
TAP_BANK = [4, 5, 6, 7, 4, 5, 6, 7, 4, 5, 6, 7]
GT = G * TT
SLOTS = (GT * P + NE * (P - 1)) // P
STEPS = 2 * SLOTS
ROW = D + 1
FIRST_SUMS = 18
SQUARES_AT = (4, 7, 10, 13)
SM_STEPS = 11
TURN_BANK = ((4, 5, 0, 1), (6, 7, 2, 3))
ROOT_AT, RANK_AT = 2, 7
PE_AT = (-1, 3, 11, 12, 17, 19, 27)
ACT_AT = (1, 1, 8, 10, 15, 17, 27)
DVE_AT = (1, 2, 5, 13, 15, 15, 17)
EARLY = 8
LEVELS = 4
ST_SHORT, ST_LONG, ST_V, ST_DELTA, ST_O = range(5)


def shape_constants():
    c = np.zeros((P, C_ALL), np.float32)
    i = np.arange(P)
    r, j = (i % Q)[:, None], np.arange(Q)[None, :]
    c[:, C_ID:C_ID + P] = np.eye(P)
    c[:, C_NSTRICT:C_NSTRICT + Q] = -(r > j).astype(np.float32)
    c[:, C_UINCL:C_UINCL + Q] = r <= j
    c[:, C_EYE:C_EYE + Q] = r == j
    c[:, C_PAIR:C_PAIR + Q] = (r // 2 == j // 2) & (r > j)
    c[:, C_STEP:C_STEP + 16] = np.arange(1, 17)
    c[:, C_VAL:C_VAL + 32] = np.arange(-16, 16)
    c[:, C_LESS:C_LESS + P] = i[:, None] < i[None, :]
    c[:, C_TOKEN:C_TOKEN + NT] = i[:, None] + P * np.arange(NT)[None, :]
    c[:, C_FULL:C_FULL + NE] = P * np.arange(NE) + 1
    c[:, C_BEFORE:C_BEFORE + NE * NE] = (np.arange(NE)[None, :] < np.arange(NE)[:, None]).reshape(1, NE * NE)
    m = np.zeros((P, LEVELS, Q), np.int32)
    for n in range(LEVELS):
        s = 2 << n
        m[:, n] = (r // (2 * s) == j // (2 * s)) & (r % (2 * s) >= s) & (j % (2 * s) < s)
    return c, m.reshape(P, LEVELS * Q)


def post_ln_block(nc, x, cst, lmask, wall, vecs, q_taps, fir_l, w1, b1, w2, b2, sorted_in, out):
    ctx = ExitStack()
    with ctx:
        def sb(name, shape, dt=F32):
            return ctx.enter_context(nc.sbuf_tensor(name, shape, dt))

        def sem(name):
            return ctx.enter_context(nc.semaphore(name))

        x_tok = sb("x_tok", [P, NT, ROW])
        xT = sb("xT", [P, N])
        qkT = sb("qkT", [P, 2, N])
        kT_raw = sb("kT_raw", [P, N])
        vT = sb("vT", [P, N])
        k_hc = sb("k_hc", [P, N])
        q_hc = sb("q_hc", [P, N])
        v_hc = sb("v_hc", [P, N])
        short = sb("short", [P, N])
        long = sb("long", [P, N])
        k_sq = sb("k_sq", [P, N])
        q_sq = sb("q_sq", [P, N])
        stats = sb("stats", [P, BC, Q])
        arena = sb("arena", [P, NE, N])
        cst_s = sb("cst_s", [P, C_ALL])
        lmask_s = sb("lmask_s", [P, LEVELS, Q], I32)
        w_s = sb("w_s", [P, W_ALL])
        v_s = sb("v_s", [P, V_ALL])
        gate_hc = sb("gate_hc", [P, BC, Q])
        beta = sb("beta", [P, BC])
        sgate = sb("sgate", [P, BC])
        norm = sb("norm", [P, 2, BC])
        nrm1 = sb("nrm1", [P, 2, BC])
        raw = sb("raw", [P, 5, 3, BC])
        m1 = sb("m1", [P, 5, BC])
        m2 = sb("m2", [P, 5, BC])
        prob = sb("prob", [P, BC, 4])
        prob2 = sb("prob2", [P, BC, 4])
        row1 = sb("row1", [P, BC])
        row2 = sb("row2", [P, BC])
        row3 = sb("row3", [P, BC])
        coef = sb("coef", [P, BC])
        tmpv = sb("tmpv", [P, 8])
        epsv = sb("epsv", [P, 2])
        r_s = sb("r_s", [P, 6, NT])
        ge = sb("ge", [P, GT, 16])
        eq = sb("eq", [P, GT, 32])
        me = sb("me", [P, G, GT + 1, NE], BF16)
        below = sb("below", [P, P], BF16)
        ones = sb("ones", [P, P], BF16)
        rank = sb("rank", [P, GT + 1, NE])
        cnt = sb("cnt", [P, 4, NE])
        place = sb("place", [P, NT])
        place_i = sb("place_i", [P, NT], I32)
        tile_e = sb("tile_e", [P, 3, SLOTS])
        tile_i = sb("tile_i", [P, G, 2, SLOTS], I32)
        zero = sb("zero", [P, ROW])
        token_i = sb("token_i", [P, G, SLOTS + 1], I32)
        fit = eq[:, :, :].rearrange("p a b -> p (a b)")[:, 0:SLOTS * NE].rearrange("p (j e) -> p j e", e=NE)
        chain = sb("chain", [P, B, Q])

        toep_flat = arena[:, 0:4, :].rearrange("p a n -> p (a n)")
        win_flat = arena[:, 4:8, :].rearrange("p a n -> p (a n)")
        toep = toep_flat[:, 0:Q * P]
        win = win_flat.rearrange("p (h n d) -> p h n d", h=H, n=BC)
        low = toep_flat[:, 0:N]
        lowT = toep_flat[:, N:2 * N]
        inv = toep_flat[:, 2 * N:3 * N]
        invT = toep_flat[:, 3 * N:4 * N]
        mid = win_flat[:, 0:N]
        attnT = win_flat[:, N:2 * N]
        state = win_flat[:, 2 * N:3 * N]
        shortT = state
        delta = win_flat[:, 3 * N:4 * N]
        nbm = k_sq[:, :]
        statsT = lowT
        hid = low
        o_hc = inv
        oT = invT
        mixA, mixB = mid, state
        x1 = x_tok[:, :, 0:D]
        bn6 = vT[:, 0:6 * NT].rearrange("p (n k) -> p n k", k=6)
        bn2 = vT[:, 6 * NT:8 * NT].rearrange("p (n k) -> p n k", k=2)
        zn6 = vT[:, 8 * NT:8 * NT + 12].rearrange("p (n k) -> p n k", k=6)
        zn2 = vT[:, 9 * NT:9 * NT + 4].rearrange("p (n k) -> p n k", k=2)
        z_dev = vT[:, 10 * NT:10 * NT + 4].rearrange("p (n k) -> p n k", k=2)
        zbuf = vT[:, N // 2:N // 2 + 2 * D].rearrange("p (k d) -> p k d", k=2)
        xs_half = arena[:, :, N // 2:N // 2 + 2 * ROW]
        xsT_half = arena[:, :, N // 2 + 2 * ROW:N // 2 + 2 * ROW + 2 * P]

        def sorted_tile(g, j):
            return kT_raw[:, j * ROW:j * ROW + D] if g == 0 else xs_half[:, j // 2, j % 2 * ROW:j % 2 * ROW + D]

        def sorted_T(g, j):
            return q_hc[:, j * P:(j + 1) * P] if g == 0 else xsT_half[:, j // 2, j % 2 * P:(j % 2 + 1) * P]

        wq_tap = long[:, 0:4 * P].rearrange("p (k d) -> p k d", k=4)
        q_tap = long[:, 4 * P:8 * P].rearrange("p (k d) -> p k d", k=4)

        hT = k_hc[:, :].rearrange("p (k f n) -> p k f n", k=4, f=NF)
        wbuf = qkT[:, :, :].rearrange("p s (a n) -> p (s a) n", a=4)
        bbuf = sb("bbuf", [P, 8, NF])
        b1tab = xT[:, 0:NE * NF].rearrange("p (e f) -> p e f", e=NE)
        with_b2 = long[:, 0:2 * D].rearrange("p (k d) -> p k d", k=2)
        b2in = long[:, 0:NE * D].rearrange("p (e d) -> p e d", e=NE)
        b2pair = short[:, 0:NE * D].rearrange("p (e d) -> p e d", e=NE)

        ps = ctx.enter_context(nc.psum_tensor("ps", [P, 8, 512], F32))

        def hc(t):
            return t.rearrange("p (b c d) -> p b c d", b=B, c=C)

        def over(ap, shape):
            return ap.to_broadcast(shape)

        ident = cst_s[:, C_ID:C_ID + P]
        uincl = cst_s[:, C_UINCL:C_UINCL + Q].unsqueeze(1)
        nstrict = cst_s[:, C_NSTRICT:C_NSTRICT + Q].unsqueeze(1)
        eye = cst_s[:, C_EYE:C_EYE + Q].unsqueeze(1)
        pair = cst_s[:, C_PAIR:C_PAIR + Q].unsqueeze(1)
        FULL = [P, C, Q]

        x_in = [sem(f"x_in{b}") for b in range(B)]
        w_in, c_in, lm_in, v_in, f_in, b2_in = (
            sem(n) for n in ("w_in", "c_in", "lm_in", "v_in", "f_in", "b2_in"))
        w_all, filled = sem("w_all"), sem("filled")
        scattered = [sem(f"scattered{g}") for g in range(2)]
        xs_in = [sem(f"xs_in{g}") for g in range(2)]
        zero_set, me_done, rank_psum, place_done = sem("zero_set"), sem("me_done"), sem("rank_psum"), sem("place_done")
        xs_psum, xs_done, wb_done = sem("xs_psum"), sem("xs_done"), sem("wb_done")
        pair_sum, bias_done = sem("pair_sum"), sem("bias_done")
        win_zero, win_in, win3_in = sem("win_zero"), sem("win_in"), sem("win3_in")
        eps_set, stats_zero = sem("eps_set"), sem("stats_zero")
        qt_in, wq_done = sem("qt_in"), sem("wq_done")
        xt_psum, xt_done = sem("xt_psum"), sem("xt_done")
        proj_psum, tap3_done, taps_done, silu_done, hc_done = (
            sem(n) for n in ("proj_psum", "tap3_done", "taps_done", "silu_done", "hc_done"))
        tap2_done, short_tap, short_done = sem("tap2_done"), sem("short_tap"), sem("short_done")
        br_psum, br_hc, beta_done, res_done, sgate_done = (
            sem(n) for n in ("br_psum", "br_hc", "beta_done", "res_done", "sgate_done"))
        sq_done, ssq_done, nrm_sqrt, nrm_done, kn_done, knT_done = (
            sem(n) for n in ("sq_done", "ssq_done", "nrm_sqrt", "nrm_done", "kn_done", "knT_done"))
        nbm_done = sem("nbm_done")
        fir_psum, fir_done = sem("fir_psum"), sem("fir_done")
        gram_psum, low_done, attn_done, lowT_done = (
            sem(n) for n in ("gram_psum", "low_done", "attn_done", "lowT_done"))
        pair_done, inv_done, invT_done, inv_beta_done = (
            sem(n) for n in ("pair_done", "inv_done", "invT_done", "inv_beta_done"))
        lx_psum, lx_done, xlx_psum = sem("lx_psum"), sem("lx_done"), sem("xlx_psum")
        k_state_psum, rhs_done, u_psum, u_done, state_psum, s_done, o_psum = (
            sem(n) for n in ("k_state_psum", "rhs_done", "u_psum", "u_done", "state_psum", "s_done", "o_psum"))
        pair_low = sem("pair_low")
        st_sq, st_red, st_small, st_m2, st_var, st_l2 = (
            sem(n) for n in ("st_sq", "st_red", "st_small", "st_m2", "st_var", "st_l2"))
        ws_scaled, wo_scaled = sem("ws_scaled"), sem("wo_scaled")
        soft_a, soft_b, soft_c = sem("soft_a"), sem("soft_b"), sem("soft_c")
        delta_done, stT_done, g_psum, g_done, lg_psum, lg_hc = (
            sem(n) for n in ("delta_done", "stT_done", "g_psum", "g_done", "lg_psum", "lg_hc"))
        softmax_done, softmax_exp = sem("softmax_done"), sem("softmax_exp")
        mix_d, mix_p = sem("mix_d"), sem("mix_p")
        og_sig, factor_part, og_sqrt = sem("og_sig"), sem("factor_part"), sem("og_sqrt")
        of_done, oT_done, wo_psum = sem("of_done"), sem("oT_done"), sem("wo_psum")
        norm_part, norm_moments, norm_root = sem("norm_part"), sem("norm_moments"), sem("norm_root")
        x1_done, hop_done, b2_done = sem("x1_done"), sem("hop_done"), sem("b2_done")
        h_psum, h_done, dn_psum, y_done = sem("h_psum"), sem("h_done"), sem("dn_psum"), sem("y_done")
        z_stats, z_moments, z_root, z_inverse, fin_done, out_done = (
            sem(n) for n in ("z_stats", "z_moments", "z_root", "z_inverse", "fin_done", "out_done"))
        numbers, token_done = sem("numbers"), sem("token_done")

        block = ctx.enter_context(nc.Block())

        def gram_bank(b, half):
            return b + (2 if b < G else 4) * half

        def expert(engine, g, k, j):
            return nc.values_load(tile_i[0:1, g, k, j], engines=(engine,), min_val=0, max_val=NE - 1,
                                  skip_runtime_bounds_check_because="the counts are cut to NE - 1")

        def taps(n):
            return sum(s != Q_SOURCE for s, b in TAPS[:n + 1])

        def lv(n, b):
            return (b // G) * G * LEVELS + G * n + b % G + 1

        def sc(c, b):
            return (b // G) * G * C + G * c + b % G + 1

        def sl(c, b):
            return (b // G) * G * (C - 1) + G * c + b % G + 1

        def gt(r, b):
            return (b // G) * 2 * G + r * G + b % G + 1

        def ivt(n, b):
            return (b // G) * G * (LEVELS + 1) + G * n + b % G + 1

        def red(g, r):
            return FIRST_SUMS + (2 * g + r) * 3 * G

        def buffer(i, g):
            return i % 8 if g == 0 else (i + 2) % 4

        def group(g):
            return range(g * G, (g + 1) * G)

        def window(h, k, g):
            bs = slice(g * G, (g + 1) * G)
            dst = win[k * Q:(k + 1) * Q, h, :, :].rearrange("p (b c) d -> p b (c d)", b=B)
            src = hc(v_hc[:, :])[h * Q:(h + 1) * Q, bs, 0:C - 2 + k, :].rearrange("p b c d -> p b (c d)")
            return dst[:, bs, (2 - k) * Q:C * Q], src

        @block.sync
        def _(sp):
            xv = x.rearrange("(n p) d -> p n d", p=P)
            sp.dma_start(cst_s[:, :], cst).then_inc(c_in, 16)
            for b in range(B):
                sp.dma_start(x_tok[:, b * TT:(b + 1) * TT, 0:D], xv[:, b * TT:(b + 1) * TT, :]).then_inc(x_in[b], 16)
                if b == 0:
                    sp.dma_start(w_s[:, :], wall).then_inc(w_in, 16)
                    sp.dma_start(v_s[:, :], vecs).then_inc(v_in, 16)
            sp.dma_start(q_tap.rearrange("p k d -> p (k d)"),
                         bass.AP(q_taps.tensor, 0, [[0, P], [1, 4 * P]])).then_inc(qt_in, 16)
            sp.dma_start(toep[0:WIN, :], fir_l).then_inc(f_in, 16)
            sp.dma_start(lmask_s[:, :, :].rearrange("p a b -> p (a b)"), lmask).then_inc(lm_in, 16)
            sp.wait_ge(win_zero, 1)
            for g in range(2):
                sp.wait_ge(hc_done, G * (g + 1))
                for h in range(H - 1):
                    for k in range(3):
                        dst, src = window(h, k, g)
                        sp.dma_start(dst, src).then_inc(win_in, 16)
            sp.wait_ge(zero_set, 1)
            for g in range(2):
                sp.dma_start(sorted_in[g].rearrange("(n p) d -> p n d", p=P),
                             zero[:, :].unsqueeze(1).to_broadcast([P, SLOTS, ROW])).then_inc(filled, 16)
            sp.wait_ge(x1_done, G)
            sp.wait_ge(mix_p, 3 * G)
            sp.dma_start(b2in, bass.AP(b2.tensor, 0, [[0, P], [D, NE], [1, D]])).then_inc(b2_in, 16)
            sp.dma_start(b1tab, b1.rearrange("e p c -> p e c")).then_inc(w_all, 16)
            for e in range(NE):
                sp.dma_start(arena[:, e, 0:FF], w1[e]).then_inc(w_all, 16)
                sp.dma_start(arena[:, e, FF:2 * FF].rearrange("p (c d) -> p c d", c=NF),
                             w2[e].rearrange("(c p) d -> p c d", p=P)).then_inc(w_all, 16)

            def moves(g, a, b):
                rows = sorted_in[g][a * P:b * P, :].rearrange("(n p) d -> p n d", p=P)
                if g == 0 or b - a == 1:
                    chip = kT_raw[:, a * ROW:b * ROW] if g == 0 else xs_half[:, a // 2, 0:ROW]
                    return [(chip.rearrange("p (n d) -> p n d", d=ROW), rows)]
                return [(xs_half[:, a // 2:b // 2, k * ROW:(k + 1) * ROW], rows[:, k:b - a:2, :]) for k in range(2)]

            for g in range(2):
                sp.wait_ge(scattered[g], 16 * GT)
                for a, b in ((0, SLOTS - 1), (SLOTS - 1, SLOTS)):
                    for chip, rows in moves(g, a, b):
                        sp.dma_start(chip, rows).then_inc(xs_in[g], 16)

        @block.tensor
        def _(pe):
            k4, q4 = hc(qkT[:, 0, :]), hc(qkT[:, 1, :])
            kn4, lowT4, inv4, invT4 = hc(k_hc[:, :]), hc(lowT), hc(inv), hc(invT)
            mid4, attn4, state4 = hc(mid), hc(attnT), hc(state)

            def per_head(dst, lhsT, rhs, start=True, stop=True):
                for h in range(H):
                    s = slice(h * Q, (h + 1) * Q)
                    mm = nc.tensor.matmul(dst[s], lhsT[s], rhs[s], start=start, stop=stop)
                return mm

            def project(n):
                s, b = TAPS[n]
                if s != Q_SOURCE:
                    w = (W_V, W_K)[s]
                    nc.tensor.matmul(ps[:, TAP_BANK[n], :], w_s[:, w:w + P], xT[:, b * L:(b + 1) * L],
                                     start=True, stop=True).then_inc(proj_psum, 1)
                    return
                pe.wait_ge(wq_done, 1)
                for k in range(4):
                    mm = nc.tensor.matmul(ps[:, TAP_BANK[n], k:L], wq_tap[:, k, :], xT[:, b * L:(b + 1) * L - k],
                                          start=(k == 0), stop=(k == 3))
                mm.then_inc(proj_psum, 1)

            pe.wait_ge(c_in, 16)
            def turn_x(b):
                pe.wait_ge(x_in[b], 16)
                for t in range(TT):
                    mm = nc.tensor.transpose(ps[:, b, t * P:(t + 1) * P], x1[:, b * TT + t, :], ident)
                mm.then_inc(xt_psum, 1)

            for b in range(B):
                if b == 0:
                    turn_x(0)
                elif b < B - 1:
                    turn_x(b + 1)
                pe.wait_ge(w_in, 16)
                pe.wait_ge(xt_done, b + 1)
                project(b)
                if b == 0:
                    turn_x(1)
            for b in range(B):
                nc.tensor.matmul(ps[:, b, :], w_s[:, W_BR:W_BR + P], xT[:, b * L:(b + 1) * L],
                                 start=True, stop=True).then_inc(br_psum, 1)
            for n in range(B, 3 * B):
                if TAPS[n - B][0] == Q_SOURCE:
                    pe.wait_ge(silu_done, n - B + 1)
                else:
                    pe.wait_ge(taps_done, taps(n - B))
                project(n)
            pe.wait_ge(f_in, 16)
            pe.wait_ge(win_in, 16 * 3 * 2 * (H - 1))
            pe.wait_ge(win3_in, 16 * 3 * 2)
            pe.wait_ge(br_hc, B)
            for m in range(4):
                for i in range(8):
                    for h in range(H):
                        ch = h * Q + m * 8 + i
                        mm = nc.tensor.matmul(ps[h * Q:(h + 1) * Q, m, i * BC:(i + 1) * BC],
                                              toep[0:WIN, ch:Q * P:P], win[0:WIN, h, :, ch % Q],
                                              start=True, stop=True)
                mm.then_inc(fir_psum, 1)
            pe.wait_ge(fir_done, 4)

            def gram(b):
                pe.wait_ge(knT_done, b + 1)
                for c in range(C):
                    mm = per_head(ps[:, gram_bank(b, c // 8), (c % 8) * 64:(c % 8) * 64 + 64], k4[:, b, c, :],
                                  qkT[:, :, (b * C + c) * Q:(b * C + c + 1) * Q])
                mm.then_inc(gram_psum, 1)

            def low_x(n, b):
                if n == 0:
                    pe.wait_ge(lowT_done, b + 1)
                    pe.wait_ge(pair_done, b + 1)
                    pe.wait_ge(attn_done, b + 1)
                else:
                    pe.wait_ge(inv_done, lv(n - 1, b))
                for c in range(C):
                    mm = per_head(ps[:, b, c * Q:(c + 1) * Q], lowT4[:, b, c, :], inv4[:, b, c, :])
                mm.then_inc(lx_psum, 1)

            def x_low_x(n, b):
                pe.wait_ge(lx_done, lv(n, b))
                pe.wait_ge(invT_done, ivt(n, b))
                for c in range(C):
                    mm = per_head(ps[:, 4 + b, c * Q:(c + 1) * Q], invT4[:, b, c, :], mid4[:, b, c, :])
                mm.then_inc(xlx_psum, 1)

            def outputs(c, b):
                for h in range(H):
                    s = slice(h * Q, (h + 1) * Q)
                    dst = ps[s, 4 + b, c * Q:(c + 1) * Q]
                    if c > 0:
                        nc.tensor.matmul(dst, q4[s, b, c, :], state4[s, b, c, :], start=True, stop=False)
                    mm = nc.tensor.matmul(dst, attn4[s, b, c, :], mid4[s, b, c, :], start=(c == 0), stop=True)
                if c == C - 1:
                    mm.then_inc(o_psum, 1)

            def scan_step(g, c):
                if c > 0:
                    for b in group(g):
                        pe.wait_ge(s_done, sl(c - 1, b))
                        per_head(ps[:, b, 0:Q], k4[:, b, c, :], state4[:, b, c, :]).then_inc(k_state_psum, 1)
                    outputs(c - 1, g * G)
                for b in group(g):
                    pe.wait_ge(rhs_done, sc(c, b))
                    per_head(ps[:, b, 64:64 + Q], invT4[:, b, c, :], chain[:, b, :]).then_inc(u_psum, 1)
                if c > 0:
                    outputs(c - 1, g * G + 1)
                for b in group(g):
                    pe.wait_ge(u_done, sc(c, b))
                    if c < C - 1:
                        per_head(ps[:, b, 128:128 + Q], kn4[:, b, c, :], mid4[:, b, c, :]).then_inc(state_psum, 1)
                if c == C - 1:
                    for b in group(g):
                        outputs(c, b)

            def gate_hidden(g, r):
                wide = (P, 64)[r]
                wx, wst = ((W_G, W_GS), (W_OG, W_OGS))[r]
                pe.wait_ge(ws_scaled, 1)
                for b in group(g):
                    pe.wait_ge(stT_done, gt(r, b))
                    nc.tensor.matmul(ps[0:wide, b, :], w_s[:, wx:wx + wide], xT[:, b * L:(b + 1) * L],
                                     start=True, stop=False)
                    nc.tensor.matmul(ps[0:wide, b, :], w_s[:, wst:wst + wide], statsT[:, b * L:(b + 1) * L],
                                     start=False, stop=True).then_inc(g_psum, 1)

            def gate_out(g, r):
                wide, w = ((P, W_G2), (64, W_OG2))[r]
                for b in group(g):
                    pe.wait_ge(g_done, gt(r, b))
                    if r == 0:
                        pe.wait_ge(delta_done, b + 1)
                    else:
                        pe.wait_ge(lg_hc, gt(0, b))
                    nc.tensor.matmul(ps[:, 4 + b, :], w_s[0:wide, w:w + P], hid[0:wide, b * L:(b + 1) * L],
                                     start=True, stop=True).then_inc(lg_psum, 1)

            def project_out(g):
                pe.wait_ge(wo_scaled, 1)
                for b in group(g):
                    pe.wait_ge(oT_done, b + 1)
                    for t in range(TT):
                        a = b * L + t * P
                        mm = nc.tensor.matmul(ps[:, b, t * P:(t + 1) * P], oT[:, a:a + P], w_s[:, W_O:W_O + P],
                                              start=True, stop=True)
                    mm.then_inc(wo_psum, 1)

            def ranks(g):
                out_ = ps[:, 4 + 2 * g, 0:(GT + 1) * NE]
                pe.wait_ge(me_done, g + 1)
                pe.wait_ge(numbers, 1)
                m_ = me[:, g, :, :].rearrange("p n e -> p (n e)")
                nc.tensor.matmul(out_, below[:, :], m_, start=True, stop=False)
                for k in range(1, GT + 1):
                    mm = nc.tensor.matmul(ps[:, 4 + 2 * g, k * NE:(GT + 1) * NE], ones[:, :],
                                          m_[:, 0:(GT + 1 - k) * NE], start=False, stop=(k == GT))
                mm.then_inc(rank_psum, 1)

            def turn_sorted(g):
                pe.wait_ge(xs_in[g], 16 * (2 + g))
                pe.wait_ge(place_done, g + 1)
                for j in range(SLOTS):
                    mm = nc.tensor.transpose(ps[:, TURN_BANK[g][j // 4], j % 4 * P:(j % 4 + 1) * P],
                                             sorted_tile(g, j), ident)
                    if j % 4 == 3 or j == SLOTS - 1:
                        mm.then_inc(xs_psum, 1)

            def up(u, i, tile, base, w):
                pe.wait_ge(wb_done, i + (base + 1))
                if base > 0 or i >= 2:
                    pe.wait_ge(h_done, i * 2 + 2 * (base - 1))
                for f in range(NF):
                    mm = nc.tensor.matmul(ps[:, u % 2, f * P:(f + 1) * P], wbuf[:, w, f * P:(f + 1) * P], tile,
                                          start=True, stop=True)
                mm.then_inc(h_psum, 1)

            def down(u, i, j, base):
                g = base // STEPS
                jj = slice(j, j + 1) if isinstance(j, int) else bass.ds(j, 1)
                pe.wait_ge(h_done, i * 2 + (2 * base + 1))
                if u % 2 == 0 and (base > 0 or i >= 4):
                    pe.wait_ge(y_done, j + (base // 2 - 1))
                e = expert(mybir.EngineType.PE, g, u % 2, jj)
                for f in range(NF):
                    if f == NF // 2:
                        pe.wait_ge(h_done, i * 2 + (2 * base + 2))
                    w_ = arena[:, bass.ds(e, 1), FF + f * P:FF + (f + 1) * P].rearrange("p a n -> p (a n)")
                    mm = nc.tensor.matmul(ps[:, 4 + u // 2, 0:P], hT[:, u, f, :], w_,
                                          start=(u % 2 == 0 and f == 0), stop=(u % 2 == 1 and f == NF - 1))
                mm.then_inc(dn_psum, 1)

            for b in group(0):
                gram(b)
            pe.wait_ge(taps_done, 2 * B)
            for n in range(LEVELS):
                for b in group(0):
                    low_x(n, b)
                for b in group(0):
                    x_low_x(n, b)
            for b in group(0):
                pe.wait_ge(inv_beta_done, b + 1)
            for c in range(C):
                scan_step(0, c)
            for b in group(1):
                gram(b)
            for n in range(LEVELS):
                for b in group(1):
                    low_x(n, b)
                if n == 0:
                    gate_hidden(0, 0)
                if n == 2:
                    gate_hidden(0, 1)
                if n == 3:
                    project_out(0)
                for b in group(1):
                    x_low_x(n, b)
                if n == 0:
                    gate_out(0, 0)
                if n == 2:
                    gate_out(0, 1)
            for b in group(1):
                pe.wait_ge(inv_beta_done, b + 1)
            for c in range(C):
                scan_step(1, c)
                if c == RANK_AT:
                    ranks(0)
            turn_sorted(0)
            stages = (lambda: gate_hidden(1, 0), lambda: gate_out(1, 0), lambda: gate_hidden(1, 1),
                      lambda: gate_out(1, 1), lambda: project_out(1), lambda: ranks(1),
                      lambda: turn_sorted(1))

            def between(j):
                for at, stage in zip(PE_AT, stages):
                    if at == j:
                        stage()

            between(-1)
            pe.wait_ge(xs_done, 4)
            for i in range(STEPS + 2):
                if i < STEPS:
                    up(i % 4, i, sorted_T(0, i // 2), 0, buffer(i, 0))
                else:
                    pe.wait_ge(xs_done, 8)
                    up(i % 4, i - STEPS, sorted_T(1, 0), STEPS, buffer(i - STEPS, 1))
                if i >= 2:
                    down((i - 2) % 4, i - 2, (i - 2) // 2, 0)
                between(i)
            with pe.Fori(0, (STEPS - 2) // 4) as r:
                for u in range(4):
                    down((u + 2) % 4, r * 4 + u, r * 2 + u // 2, STEPS)
                    k = (u + 2) // 2
                    x_ = xsT_half[:, bass.ds(r + k // 2, 1), k % 2 * P:(k % 2 + 1) * P]
                    up(u, r * 4 + (u + 2), x_.rearrange("p a n -> p (a n)"), STEPS, u)
            for u in range(2):
                down(u + 2, STEPS - 2 + u, SLOTS - 1, STEPS)

        @block.scalar
        def _(act):
            srcs = (vT[:, :], kT_raw[:, :], qkT[:, 1, :])
            def turned_x(b):
                act.wait_ge(xt_psum, b + 1)
                nc.scalar.copy(xT[:, b * L:(b + 1) * L], ps[:, b, :]).then_inc(xt_done, 1)

            def newest_tap(n):
                s, b = TAPS[n]
                if s == Q_SOURCE:
                    return
                act.wait_ge(proj_psum, n + 1)
                c = V_CONV + 4 * s + 3
                nc.scalar.activation(srcs[s][:, b * L:(b + 1) * L], ps[:, TAP_BANK[n], :], ACT.Copy,
                                     scale=v_s[:, c:c + 1]).then_inc(tap3_done, 1)

            def silu(n):
                s, b = TAPS[n]
                y = srcs[s][:, b * L:(b + 1) * L]
                if s == Q_SOURCE:
                    act.wait_ge(proj_psum, n + 1)
                else:
                    act.wait_ge(taps_done, taps(n))
                nc.scalar.activation(y, ps[:, TAP_BANK[n], :] if s == Q_SOURCE else y, ACT.Silu).then_inc(silu_done, 1)

            def norms(g):
                cs = slice(g * G * C, (g + 1) * G * C)
                act.wait_ge(ssq_done, 2 * G * (g + 1))
                nc.scalar.activation(nrm1[:, :, cs], norm[:, :, cs], ACT.Sqrt, bias=epsv[:, 0:1]).then_inc(nrm_sqrt, 1)

            turned_x(0)
            act.wait_ge(v_in, 16)
            for n in range(2 * B + 1):
                if n == 0:
                    newest_tap(0)
                    turned_x(1)
                if n + 2 < B:
                    turned_x(n + 2)
                if 1 <= n < 2 * B:
                    newest_tap(n)
                if n >= 1:
                    silu(n - 1)
            act.wait_ge(eps_set, 2)
            norms(0)
            for m in range(4):
                act.wait_ge(fir_psum, m + 1)
                dst = long[:, :].rearrange("p (n d) -> p d n", d=Q)[:, m * 8:m * 8 + 8, :]
                nc.scalar.copy(dst, ps[:, m, :].rearrange("p (d n) -> p d n", d=8)).then_inc(fir_done, 1)
            act.wait_ge(br_hc, B)
            nc.scalar.activation(beta[:, :], gate_hc[:, :, 0], ACT.Sigmoid).then_inc(beta_done, 1)
            nc.scalar.activation(row1[:, :], gate_hc[:, :, 1], ACT.Sigmoid,
                                 bias=v_s[:, V_BRES:V_BRES + 1]).then_inc(res_done, 1)
            nc.scalar.activation(tmpv[:, 3:4], v_s[:, V_STATIC:V_STATIC + 1], ACT.Sigmoid).then_inc(res_done, 1)
            for n in range(2 * B, 3 * B):
                newest_tap(n)
            for n in range(2 * B, 2 * B + 3):
                silu(n)
            nc.scalar.activation(tmpv[:, 0:1], v_s[:, V_TEMP:V_TEMP + 1], ACT.Abs).then_inc(soft_a, 1)
            act.wait_ge(soft_a, 1)
            nc.scalar.activation(tmpv[:, 1:2], tmpv[:, 0:1], ACT.Exp, scale=-1.0).then_inc(soft_a, 1)
            act.wait_ge(soft_a, 2)
            nc.scalar.activation(tmpv[:, 2:3], tmpv[:, 1:2], ACT.Ln, bias=1.0).then_inc(soft_a, 1)

            def low_x_out(n, b):
                act.wait_ge(lx_psum, lv(n, b))
                nc.scalar.copy(mid[:, b * L:(b + 1) * L], ps[:, b, :]).then_inc(lx_done, 1)

            def first_squares(k, g):
                if k:
                    act.wait_ge(st_red, 6 * (k - 1) + 3 * g + 3)
                if k == 2:
                    act.wait_ge(short_done, B)
                ls = slice(g * G * L, (g + 1) * G * L)
                nc.scalar.activation(delta[:, ls], (long, v_hc, short)[k][:, ls], ACT.Square).then_inc(st_sq, 1)

            def scan_out(g, c):
                for b in group(g):
                    act.wait_ge(u_psum, sc(c, b))
                    nc.scalar.copy(hc(mid)[:, b, c, :], ps[:, b, 64:64 + Q]).then_inc(u_done, 1)

            def gate_squares(g, r):
                for b in group(g):
                    if r == 0:
                        act.wait_ge(delta_done, b + 1)
                    else:
                        act.wait_ge(mix_d, 3 * G * g + 2 * G + b % G + 1)
                    nc.scalar.activation(q_sq[:, b * L:(b + 1) * L], (delta, o_hc)[r][:, b * L:(b + 1) * L],
                                         ACT.Square).then_inc(st_sq, 1)

            def gate_root(g, r):
                act.wait_ge(st_red, red(g, r) + 3 * G)
                cs, s = slice(g * G * C, (g + 1) * G * C), (ST_DELTA, ST_O)[r]
                nc.scalar.activation(stats[:, cs, 4 * s + 3], raw[:, s, 2, cs], ACT.Sqrt).then_inc(st_l2, 1)

            def gate_gelu(g, r):
                wide, col = ((P, V_BG1), (64, V_BOG1))[r]
                for b in group(g):
                    act.wait_ge(g_psum, gt(r, b))
                    if r == 1:
                        act.wait_ge(lg_psum, gt(0, b))
                    nc.scalar.activation(hid[0:wide, b * L:(b + 1) * L], ps[0:wide, b, :], ACT.Gelu,
                                         bias=v_s[0:wide, col:col + 1]).then_inc(g_done, 1)

            def soft_exp(g):
                cs = slice(g * G * C, (g + 1) * G * C)
                act.wait_ge(softmax_done, SM_STEPS * g + 3)
                nc.scalar.activation(prob2[:, cs, :], prob[:, cs, :], ACT.Exp).then_inc(softmax_exp, 1)

            def out_gate(g):
                cs = slice(g * G * C, (g + 1) * G * C)
                act.wait_ge(lg_hc, gt(1, (g + 1) * G - 1))
                nc.scalar.activation(row1[:, cs], gate_hc[:, cs, 0], ACT.Sigmoid,
                                     bias=v_s[:, V_BOG2:V_BOG2 + 1]).then_inc(og_sig, 1)
                act.wait_ge(factor_part, 4 * g + 2)
                nc.scalar.activation(row3[:, cs], row2[:, cs], ACT.Sqrt, bias=epsv[:, 1:2]).then_inc(og_sqrt, 1)

            def first_norm(g):
                t = slice(g * GT, (g + 1) * GT)
                act.wait_ge(norm_moments, G * (g + 1))
                nc.scalar.activation(r_s[:, 2, t], bn2[:, t, 1], ACT.Sqrt, bias=epsv[:, 1:2]).then_inc(norm_root, 1)

            def deviation(k, j, base):
                act.wait_ge(z_moments, j + (base // 2 + 1))
                nc.scalar.activation(z_dev[:, k, 0:1], zn2[:, k, 1:2], ACT.Sqrt, bias=epsv[:, 1:2]).then_inc(z_root, 1)

            def sorted_out_T(g):
                for k in range(4):
                    n = min(4, SLOTS - 4 * k) * P
                    act.wait_ge(xs_psum, 4 * g + k + 1)
                    if g == 0:
                        dst, src = q_hc[:, 4 * k * P:4 * k * P + n], ps[:, TURN_BANK[g][k], 0:n]
                        nc.scalar.copy(dst, src).then_inc(xs_done, 1)
                    elif n == 4 * P:
                        nc.scalar.copy(xsT_half[:, 2 * k:2 * k + 2, :],
                                       ps[:, TURN_BANK[g][k], :].rearrange("p (a n) -> p a n", a=2)).then_inc(xs_done, 1)
                    else:
                        nc.scalar.copy(xsT_half[:, 2 * k, :], ps[:, TURN_BANK[g][k], 0:2 * P])
                        nc.scalar.copy(xsT_half[:, 2 * k + 1, 0:P],
                                       ps[:, TURN_BANK[g][k], 2 * P:3 * P]).then_inc(xs_done, 1)

            def relus(u, i, base, w):
                act.wait_ge(h_psum, i + (base + 1))
                if base > 0 or i >= 4:
                    act.wait_ge(dn_psum, i + (base - 3))
                for f in range(NF):
                    a = nc.scalar.activation(hT[:, u, f, :], ps[:, u % 2, f * P:(f + 1) * P], ACT.Relu,
                                             bias=bbuf[:, w, f:f + 1])
                    if f % 2 == 1:
                        a.then_inc(h_done, 1)

            for n in range(LEVELS):
                for b in group(0):
                    low_x_out(n, b)
                if n == 0:
                    silu(2 * B + 3)
                if n == 1:
                    norms(1)
                if n == 2:
                    first_squares(0, 0)
                    first_squares(0, 1)
            for c in range(C):
                scan_out(0, c)
                if c in SQUARES_AT:
                    i = SQUARES_AT.index(c)
                    first_squares(1 + i // 2, i % 2)
            act.wait_ge(st_red, FIRST_SUMS)
            nc.scalar.activation(stats[:, :, 3:12:4].rearrange("p n s -> p s n"), raw[:, 0:3, 2, :],
                                 ACT.Sqrt).then_inc(st_l2, 1)
            gate_squares(0, 0)
            gate_root(0, 0)
            for n in range(LEVELS):
                for b in group(1):
                    low_x_out(n, b)
                if n == 0:
                    gate_gelu(0, 0)
                    soft_exp(0)
                if n == 1:
                    gate_squares(0, 1)
                    gate_root(0, 1)
                if n == 2:
                    gate_gelu(0, 1)
                    out_gate(0)
            for c in range(C):
                scan_out(1, c)
                if c == ROOT_AT:
                    first_norm(0)
            gate_squares(1, 0)
            sorted_out_T(0)
            gate_root(1, 0)
            stages = (lambda: gate_gelu(1, 0), lambda: soft_exp(1), lambda: (gate_squares(1, 1), gate_root(1, 1)),
                      lambda: gate_gelu(1, 1), lambda: out_gate(1), lambda: first_norm(1),
                      lambda: sorted_out_T(1))

            def between(j):
                for at, stage in zip(ACT_AT, stages):
                    if at == j:
                        stage()

            between(-1)
            for j in range(SLOTS):
                relus(2 * j % 4, 2 * j, 0, buffer(2 * j, 0))
                between(2 * j)
                relus((2 * j + 1) % 4, 2 * j + 1, 0, buffer(2 * j + 1, 0))
                if j >= 1:
                    deviation((j - 1) % 2, j - 1, 0)
                between(2 * j + 1)
            relus(2, 0, STEPS, buffer(0, 1))
            relus(3, 1, STEPS, buffer(1, 1))
            deviation((SLOTS - 1) % 2, SLOTS - 1, 0)
            with act.Fori(0, (SLOTS - 1) // 2) as r:
                for k in range(2):
                    for u in range(2):
                        relus(2 * k + u, r * 4 + (2 * k + 2 + u), STEPS, 2 * k + u)
                    deviation(1 - k, r * 2 + k, STEPS)
            deviation(SLOTS % 2, SLOTS - 1, STEPS)

        @block.vector
        def _(dve):
            V = nc.vector
            srcs = (vT[:, :], kT_raw[:, :], qkT[:, 1, :])
            hcs = (v_hc, k_hc, q_hc)
            st4, v4 = hc(state), hc(v_hc[:, :])
            T4 = [P, TT, D]
            softmax_steps, small_steps = [0], [0]

            def step(i):
                softmax_steps[0] += 1
                i.then_inc(softmax_done, 1)
                dve.wait_ge(softmax_done, softmax_steps[0])

            def hop(i):
                small_steps[0] += 1
                i.then_inc(hop_done, 1)
                dve.wait_ge(hop_done, small_steps[0])

            def chunks(g):
                return slice(g * G * C, (g + 1) * G * C)

            def older_taps(n):
                s, b = TAPS[n]
                if s == Q_SOURCE:
                    return
                dve.wait_ge(tap3_done, taps(n))
                for k in range(1, 4):
                    y = srcs[s][:, b * L + k:(b + 1) * L]
                    c = V_CONV + 4 * s + 3 - k
                    if k > 1:
                        dve.wait_ge(tap2_done, 2 * taps(n) + k - 3)
                    V.scalar_tensor_tensor(out=y, in0=ps[:, TAP_BANK[n], 0:L - k], scalar=v_s[:, c:c + 1], in1=y,
                                           op0=ALU.mult, op1=ALU.add).then_inc(taps_done if k == 3 else tap2_done, 1)

            def to_hc(n):
                s, b = TAPS[n]
                dve.wait_ge(silu_done, n + 1)
                V.transpose(hcs[s][:, b * L:(b + 1) * L], srcs[s][:, b * L:(b + 1) * L]).then_inc(hc_done, 1)

            def short_filter(g):
                bs = slice(g * G, (g + 1) * G)
                v_, y = (a.rearrange("p (b l) -> p b l", b=B)[:, bs, :] for a in (vT[:, :], shortT))
                tap = V_SHORT + KS - 1
                V.tensor_scalar(y, v_, v_s[:, tap:tap + 1], None, ALU.mult).then_inc(short_tap, 1)
                for k in range(1, KS):
                    dve.wait_ge(short_tap, g * KS + k)
                    V.scalar_tensor_tensor(out=y[:, :, k:L], in0=v_[:, :, 0:L - k], scalar=v_s[:, tap - k:tap - k + 1],
                                           in1=y[:, :, k:L], op0=ALU.mult, op1=ALU.add).then_inc(short_tap, 1)

            def short_hc():
                for b in range(B):
                    dve.wait_ge(short_tap, (b // G + 1) * KS)
                    V.transpose(short[:, b * L:(b + 1) * L], shortT[:, b * L:(b + 1) * L]).then_inc(short_done, 1)

            def norms(g):
                for n in range(B + 2 * G * g, B + 2 * G * (g + 1)):
                    s, b = TAPS[n]
                    dve.wait_ge(sq_done, n - B + 1)
                    V.tensor_reduce(norm[:, s - 1, b * C:(b + 1) * C], hc((k_sq, q_sq)[s - 1][:, :])[:, b, :, :], AX.X,
                                    ALU.add).then_inc(ssq_done, 1)

            def unit_k(g):
                dve.wait_ge(nrm_sqrt, g + 1)
                V.reciprocal(norm[:, :, chunks(g)], nrm1[:, :, chunks(g)]).then_inc(nrm_done, 1)
                dve.wait_ge(nrm_done, g + 1)
                for b in group(g):
                    k = hc(k_hc[:, :])[:, b, :, :]
                    V.tensor_tensor(k, k, over(norm[:, 0, b * C:(b + 1) * C].unsqueeze(2), FULL),
                                    ALU.mult).then_inc(kn_done, 1)
                    dve.wait_ge(kn_done, b + 1)
                    V.transpose(qkT[:, 0, b * L:(b + 1) * L], k_hc[:, b * L:(b + 1) * L]).then_inc(knT_done, 1)

            def triangles(b):
                dve.wait_ge(gram_psum, b + 1)
                dve.wait_ge(nbm_done, b + 1)
                for half in range(2):
                    gram = ps[:, gram_bank(b, half), :].rearrange("p (c x) -> p c x", x=2 * Q)
                    cs = slice(half * 8, half * 8 + 8)
                    V.tensor_tensor(hc(low)[:, b, cs, :], gram[:, :, 0:Q], hc(nbm)[:, b, cs, :],
                                    ALU.mult).then_inc(low_done, 1)
                dve.wait_ge(low_done, 2 * b + 2)
                V.transpose(lowT[:, b * L:(b + 1) * L], low[:, b * L:(b + 1) * L]).then_inc(lowT_done, 1)
                for half in range(2):
                    gram = ps[:, gram_bank(b, half), :].rearrange("p (c x) -> p c x", x=2 * Q)
                    cs = slice(half * 8, half * 8 + 8)
                    a = V.tensor_tensor(hc(attnT)[:, b, cs, :], gram[:, :, Q:2 * Q], over(uincl, [P, 8, Q]),
                                        ALU.mult)
                a.then_inc(attn_done, 1)

            def turn_pairs(g):
                for b in group(g):
                    dve.wait_ge(pair_done, b + 1)
                    V.transpose(invT[:, b * L:(b + 1) * L], inv[:, b * L:(b + 1) * L]).then_inc(invT_done, 1)

            def level(g, n):
                for b in group(g):
                    dve.wait_ge(xlx_psum, lv(n, b))
                    V.copy_predicated(hc(inv)[:, b, :, :], over(lmask_s[:, n, :].unsqueeze(1), FULL),
                                      ps[:, 4 + b, :].rearrange("p (c d) -> p c d", c=C)).then_inc(inv_done, 1)
                    dve.wait_ge(inv_done, lv(n, b))
                    V.transpose(invT[:, b * L:(b + 1) * L], inv[:, b * L:(b + 1) * L]).then_inc(invT_done, 1)
                    if n == LEVELS - 1:
                        dve.wait_ge(invT_done, ivt(n + 1, b))
                        t = hc(invT)[:, b, :, :]
                        V.tensor_tensor(t, t, over(beta[:, b * C:(b + 1) * C].unsqueeze(2), FULL),
                                        ALU.mult).then_inc(inv_beta_done, 1)

            def scan_rhs(g, c):
                for b in group(g):
                    if c == 0:
                        V.tensor_copy(chain[:, b, :], v4[:, b, c, :]).then_inc(rhs_done, 1)
                    else:
                        dve.wait_ge(k_state_psum, sl(c - 1, b))
                        V.tensor_tensor(chain[:, b, :], v4[:, b, c, :], ps[:, b, 0:Q],
                                        ALU.subtract).then_inc(rhs_done, 1)

            def scan_state(g, c):
                for b in group(g):
                    if c == C - 1:
                        continue
                    dve.wait_ge(state_psum, sl(c, b))
                    d_ = ps[:, b, 128:128 + Q]
                    if c == 0:
                        V.tensor_copy(st4[:, b, 1, :], d_).then_inc(s_done, 1)
                    else:
                        dve.wait_ge(s_done, sl(c - 1, b))
                        V.tensor_tensor(st4[:, b, c + 1, :], st4[:, b, c, :], d_, ALU.add).then_inc(s_done, 1)

            def sum_of(src, s, r, cs):
                V.tensor_reduce(raw[:, s, r, cs], src.rearrange("p (n d) -> p n d", d=Q)[:, cs, :], AX.X, ALU.add,
                                apply_absolute_value=(r == 1)).then_inc(st_red, 1)

            def first_sum(i):
                k, g, r = i // 6, i % 6 // 3, i % 3
                if r == 2:
                    dve.wait_ge(st_sq, 2 * k + g + 1)
                sum_of(delta if r == 2 else (long, v_hc, short)[k][:, :], (ST_LONG, ST_V, ST_SHORT)[k], r, chunks(g))

            def sums(src, squares, s, b0, b1, count):
                cs = slice(b0 * C, b1 * C)
                sum_of(src, s, 0, cs)
                sum_of(src, s, 1, cs)
                dve.wait_ge(st_sq, count)
                sum_of(squares, s, 2, cs)

            def small_stats(s0, s1, cs, k):
                slot = stats[:, cs, 4 * s0:4 * s1].rearrange("p n (s k) -> p k s n", k=4)
                V.tensor_scalar(slot[:, 0], raw[:, s0:s1, 0, cs], 1.0 / Q, None, ALU.mult).then_inc(st_small, 1)
                V.tensor_scalar(slot[:, 2], raw[:, s0:s1, 1, cs], 1.0 / Q, None, ALU.mult).then_inc(st_small, 1)
                V.tensor_scalar(m1[:, s0:s1, cs], raw[:, s0:s1, 0, cs], 1.0 / Q, None, ALU.mult).then_inc(st_small, 1)
                dve.wait_ge(st_small, 3 * k + 3)
                V.tensor_tensor(m2[:, s0:s1, cs], m1[:, s0:s1, cs], m1[:, s0:s1, cs], ALU.mult).then_inc(st_m2, 1)
                dve.wait_ge(st_m2, k + 1)
                for s in range(s0, s1):
                    V.scalar_tensor_tensor(out=stats[:, cs, 4 * s + 1], in0=raw[:, s, 2, cs], scalar=1.0 / Q,
                                           in1=m2[:, s, cs], op0=ALU.mult, op1=ALU.subtract).then_inc(st_var, 1)

            def scan_result(g):
                for b in group(g):
                    dve.wait_ge(o_psum, b + 1)
                    V.tensor_tensor(hc(delta)[:, b, :, :], ps[:, 4 + b, :].rearrange("p (c d) -> p c d", c=C),
                                    over(norm[:, 1, b * C:(b + 1) * C].unsqueeze(2), FULL),
                                    ALU.mult).then_inc(delta_done, 1)

            def gate_stats(g, r):
                s, src = ((ST_DELTA, delta), (ST_O, o_hc))[r]
                for b in group(g):
                    if r == 0:
                        dve.wait_ge(delta_done, b + 1)
                    else:
                        dve.wait_ge(mix_d, 3 * G * g + 2 * G + b % G + 1)
                    sums(src, q_sq[:, :], s, b, b + 1, 6 + gt(r, b))
                dve.wait_ge(st_red, red(g, r) + 3 * G)
                small_stats(s, s + 1, chunks(g), 1 + 2 * g + r)
                dve.wait_ge(st_var, 4 + 2 * g + r)
                dve.wait_ge(st_l2, 2 + 2 * g + r)
                for b in group(g):
                    if r == 1:
                        dve.wait_ge(g_psum, gt(0, b))
                    V.transpose(statsT[:, b * L:(b + 1) * L], stats[:, b * C:(b + 1) * C, :].rearrange(
                        "p a b -> p (a b)")).then_inc(stT_done, 1)

            def logits_hc(g, r):
                for b in group(g):
                    dve.wait_ge(lg_psum, gt(r, b))
                    V.transpose(gate_hc[:, b * C:(b + 1) * C, :].rearrange("p a b -> p (a b)"),
                                ps[:, 4 + b, :]).then_inc(lg_hc, 1)

            def softmax(g):
                logits_hc(g, 0)
                cs, n = chunks(g), G * C
                W4 = [P, n, 4]
                dve.wait_ge(lg_hc, gt(0, (g + 1) * G - 1))
                dve.wait_ge(soft_c, 1)
                step(V.tensor_tensor(prob2[:, cs, :], gate_hc[:, cs, 0:4],
                                     over(v_s[:, V_BG2:V_BG2 + 4].unsqueeze(1), W4), ALU.add))
                step(V.tensor_reduce(row1[:, cs], prob2[:, cs, :], AX.X, ALU.max))
                V.tensor_tensor(prob2[:, cs, :], prob2[:, cs, :], over(row1[:, cs].unsqueeze(2), W4),
                                ALU.subtract).then_inc(soft_c, 1)
                dve.wait_ge(soft_c, 2 + g)
                step(V.tensor_scalar(prob[:, cs, :], prob2[:, cs, :], tmpv[:, 5:6], None, ALU.mult))
                dve.wait_ge(softmax_exp, g + 1)
                step(V.tensor_reduce(row1[:, cs], prob2[:, cs, :], AX.X, ALU.add))
                step(V.reciprocal(row2[:, cs], row1[:, cs]))
                step(V.tensor_tensor(prob[:, cs, :], prob2[:, cs, :], over(row2[:, cs].unsqueeze(2), W4), ALU.mult))
                step(V.tensor_scalar(prob2[:, cs, :], prob[:, cs, :], FLOOR, None, ALU.max))
                step(V.tensor_reduce(row1[:, cs], prob2[:, cs, :], AX.X, ALU.add))
                step(V.reciprocal(row2[:, cs], row1[:, cs]))
                step(V.tensor_tensor(prob[:, cs, :], prob2[:, cs, :], over(row2[:, cs].unsqueeze(2), W4), ALU.mult))
                step(V.tensor_tensor(coef[:, cs], prob[:, cs, 0], sgate[:, cs], ALU.add))

            def mix(g):
                for b in group(g):
                    cs, ls = slice(b * C, (b + 1) * C), slice(b * L, (b + 1) * L)
                    V.tensor_tensor(hc(o_hc)[:, b, :, :], hc(short[:, :])[:, b, :, :],
                                    over(coef[:, cs].unsqueeze(2), FULL), ALU.mult).then_inc(mix_d, 1)
                    V.tensor_tensor(hc(delta)[:, b, :, :], hc(delta)[:, b, :, :],
                                    over(prob[:, cs, 2].unsqueeze(2), FULL), ALU.mult).then_inc(soft_b, 1)
                    dve.wait_ge(mix_d, 3 * G * g + 2 * (b % G) + 1)
                    dve.wait_ge(soft_b, b + 2)
                    V.tensor_tensor(o_hc[:, ls], o_hc[:, ls], delta[:, ls], ALU.add).then_inc(mix_d, 1)
                for b in group(g):
                    ls = slice(b * L, (b + 1) * L)
                    dve.wait_ge(mix_d, 3 * G * g + 2 * G)
                    dve.wait_ge(mix_p, 3 * (b + 1))
                    V.tensor_tensor(o_hc[:, ls], o_hc[:, ls], mixA[:, ls], ALU.add).then_inc(mix_d, 1)

            def factor(g):
                logits_hc(g, 1)
                cs = chunks(g)
                dve.wait_ge(og_sig, g + 1)
                V.tensor_tensor(row3[:, cs], row1[:, cs], row1[:, cs], ALU.mult).then_inc(factor_part, 1)
                dve.wait_ge(factor_part, 4 * g + 1)
                V.scalar_tensor_tensor(out=row2[:, cs], in0=raw[:, ST_O, 2, cs], scalar=1.0 / Q, in1=row3[:, cs],
                                       op0=ALU.mult, op1=ALU.mult).then_inc(factor_part, 1)
                dve.wait_ge(og_sqrt, g + 1)
                V.reciprocal(row2[:, cs], row3[:, cs]).then_inc(factor_part, 1)
                dve.wait_ge(factor_part, 4 * g + 3)
                V.tensor_tensor(coef[:, cs], row1[:, cs], row2[:, cs], ALU.mult).then_inc(factor_part, 1)
                dve.wait_ge(factor_part, 4 * g + 4)
                for b in group(g):
                    o = hc(o_hc)[:, b, :, :]
                    V.tensor_tensor(o, o, over(coef[:, b * C:(b + 1) * C].unsqueeze(2), FULL),
                                    ALU.mult).then_inc(of_done, 1)
                    dve.wait_ge(of_done, b + 1)
                    V.transpose(oT[:, b * L:(b + 1) * L], o_hc[:, b * L:(b + 1) * L]).then_inc(oT_done, 1)

            def norm_add(g):
                for b in group(g):
                    tb = slice(b * TT, (b + 1) * TT)
                    dve.wait_ge(wo_psum, b + 1)
                    V.tensor_tensor(x1[:, tb, :], x1[:, tb, :], ps[:, b, :].rearrange("p (n d) -> p n d", n=TT),
                                    ALU.add).then_inc(norm_part, 1)

            def norm_stats(g):
                for b in group(g):
                    dve.wait_ge(norm_part, 2 * G * g + b % G + 1)
                    for n in range(b * TT, (b + 1) * TT):
                        a = V.bn_stats(bn6[:, n, :], x1[:, n, :])
                    a.then_inc(norm_part, 1)

            def norm_aggregate(g):
                for b in group(g):
                    dve.wait_ge(norm_part, 2 * G * g + G + b % G + 1)
                    for n in range(b * TT, (b + 1) * TT):
                        a = V.bn_aggr(bn2[:, n, :], bn6[:, n, :])
                    a.then_inc(norm_moments, 1)

            def norm_scale(b):
                g = b // G
                t = slice(g * GT, (g + 1) * GT)
                if b % G == 0:
                    dve.wait_ge(norm_root, g + 1)
                    hop(V.reciprocal(r_s[:, 3, t], r_s[:, 2, t]))
                for n in range(b * TT, (b + 1) * TT):
                    a = V.tensor_scalar(x1[:, n, :], x1[:, n, :], bn2[:, n, 0:1], r_s[:, 3, n:n + 1], ALU.subtract,
                                        ALU.mult)
                a.then_inc(x1_done, 1)

            def first_norm(g):
                norm_add(g)
                norm_stats(g)
                norm_aggregate(g)
                for b in group(g):
                    norm_scale(b)

            def sum_cut(g):
                t, n = slice(g * GT, (g + 1) * GT), GT
                dve.wait_ge(x1_done, (g + 1) * G)
                hop(V.tensor_tensor(r_s[:, 0, t], x1[:, t, 0], x1[:, t, 1], ALU.add))
                hop(V.tensor_scalar(r_s[:, 1, t], r_s[:, 0, t], -1.0, None, ALU.mult))
                hop(V.tensor_tensor(r_s[:, 2, t], r_s[:, 0, t], r_s[:, 1, t], ALU.max))
                hop(V.tensor_tensor(ge[:, :, :], over(r_s[:, 2, t].unsqueeze(2), [P, n, 16]),
                                    over(cst_s[:, C_STEP:C_STEP + 16].unsqueeze(1), [P, n, 16]), ALU.is_ge))
                hop(V.tensor_reduce(r_s[:, 3, t], ge[:, :, :], AX.X, ALU.add))

            def first_experts(g):
                t, n = slice(g * GT, (g + 1) * GT), GT
                hop(V.tensor_scalar(r_s[:, 4, t], r_s[:, 0, t], 0.0, 2.0, ALU.is_ge, ALU.mult))
                hop(V.tensor_scalar(r_s[:, 5, t], r_s[:, 4, t], -1.0, None, ALU.add))
                hop(V.tensor_tensor(r_s[:, 4, t], r_s[:, 3, t], r_s[:, 5, t], ALU.mult))
                hop(V.tensor_tensor(eq[:, :, :], over(r_s[:, 4, t].unsqueeze(2), [P, n, 32]),
                                    over(cst_s[:, C_VAL:C_VAL + 32].unsqueeze(1), [P, n, 32]), ALU.is_equal))
                with nc.allow_low_precision(reason="the sums are zero or one"):
                    V.tensor_reduce(me[:, g, 0:GT, :], eq[:, :, :].rearrange("p n (g e) -> p n e g", e=NE), AX.X,
                                    ALU.add).then_inc(me_done, 1)

            def tile_counts(g):
                EE = [P, NE, NE]
                dve.wait_ge(rank_psum, g + 1)
                hop(V.tensor_copy(rank[:, :, :].rearrange("p n e -> p (n e)"), ps[:, 4 + 2 * g, 0:(GT + 1) * NE]))
                hop(V.tensor_tensor(fit[:, 0:NE, :], over(rank[:, GT, :].unsqueeze(2), EE),
                                    over(cst_s[:, C_FULL:C_FULL + NE].unsqueeze(1), EE), ALU.is_ge))
                hop(V.tensor_reduce(cnt[:, 0, :], fit[:, 0:NE, :], AX.X, ALU.add))
                hop(V.tensor_tensor(fit[:, 0:NE, :], over(cnt[:, 0, :].unsqueeze(1), EE),
                                    cst_s[:, C_BEFORE:C_BEFORE + NE * NE].rearrange("p (a b) -> p a b", a=NE), ALU.mult))
                hop(V.tensor_reduce(cnt[:, 1, :], fit[:, 0:NE, :], AX.X, ALU.add))

            def places(g):
                t = slice(g * GT, (g + 1) * GT)
                hop(V.scalar_tensor_tensor(out=rank[:, 0:GT, :], in0=over(cnt[:, 1, :].unsqueeze(1), [P, GT, NE]),
                                           scalar=float(P), in1=rank[:, 0:GT, :], op0=ALU.mult, op1=ALU.add))
                hop(V.tensor_tensor(rank[:, 0:GT, :], rank[:, 0:GT, :], me[:, g, 0:GT, :], ALU.mult))
                hop(V.tensor_reduce(place[:, t], rank[:, 0:GT, :], AX.X, ALU.add))
                V.tensor_copy(place_i[:, t], place[:, t]).then_inc(place_done, 1)

            def tile_experts(g):
                SE = [P, SLOTS, NE]
                hop(V.tensor_tensor(cnt[:, 2, :], cnt[:, 1, :], cnt[:, 0, :], ALU.add))
                hop(V.scalar_tensor_tensor(out=fit[:, :, :],
                                           in0=over(cst_s[:, C_STEP:C_STEP + SLOTS].unsqueeze(2), SE), scalar=-1.0,
                                           in1=over(cnt[:, 2, :].unsqueeze(1), SE), op0=ALU.add, op1=ALU.is_ge))
                hop(V.tensor_reduce(tile_e[:, 0, :], fit[:, :, :], AX.X, ALU.add))
                hop(V.tensor_scalar(tile_e[:, 0, :], tile_e[:, 0, :], NE - 1.0, None, ALU.min))
                hop(V.tensor_scalar(tile_e[:, 1, :], tile_e[:, 0, :], NE - 1.0, float(-NE), ALU.is_ge, ALU.mult))
                hop(V.scalar_tensor_tensor(out=tile_e[:, 2, :], in0=tile_e[:, 0, :], scalar=1.0, in1=tile_e[:, 1, :],
                                           op0=ALU.add, op1=ALU.add))
                hop(V.tensor_copy(tile_i[:, g, :, :], tile_e[:, 0:3:2, :]))

            def fetch(g, u, i, j, base):
                for k in range(2):
                    if g == 1:
                        dve.wait_ge(h_done, i * 2 + 2 * (base - 3 + k))
                    elif i >= 8:
                        dve.wait_ge(h_done, 2 * (i + k - 7))
                    e = expert(mybir.EngineType.DVE, g, k, j)
                    if k == 0:
                        first = e
                    V.tensor_copy(wbuf[:, u + k, :], arena[:, bass.ds(e, 1), 0:FF].rearrange("p a n -> p (a n)"))
                    V.tensor_copy(bbuf[:, u + k, :], b1tab[:, bass.ds(e, 1), :].rearrange("p a f -> p (a f)")
                                  ).then_inc(wb_done, 1)
                return first

            def with_bias(u, e, tile):
                V.tensor_tensor(with_b2[:, u // 2, :], tile, b2pair[:, bass.ds(e, 1), :].rearrange("p a d -> p (a d)"),
                                ALU.add).then_inc(bias_done, 1)

            def take(u, j, base, ahead=None):
                k = u // 2
                dve.wait_ge(dn_psum, j * 2 + (base + 2))
                dve.wait_ge(bias_done, j + (base // 2 + 1))
                V.scalar_tensor_tensor(out=zbuf[:, k, :], in0=ps[:, 4 + k, 0:P], scalar=0.5, in1=with_b2[:, k, :],
                                       op0=ALU.mult, op1=ALU.add).then_inc(y_done, 1)
                dve.wait_ge(y_done, j + (base // 2 + 1))
                V.bn_stats(zn6[:, k, :], zbuf[:, k, :]).then_inc(z_stats, 1)
                dve.wait_ge(z_stats, j + (base // 2 + 1))
                if ahead:
                    with_bias(u, *ahead)
                V.bn_aggr(zn2[:, k, :], zn6[:, k, :]).then_inc(z_moments, 1)

            def finish(k, j, y, base):
                dve.wait_ge(z_root, j + (base // 2 + 1))
                V.reciprocal(z_dev[:, k, 1:2], z_dev[:, k, 0:1]).then_inc(z_inverse, 1)
                dve.wait_ge(z_inverse, j + (base // 2 + 1))
                V.tensor_scalar(y, zbuf[:, k, :], zn2[:, k, 0:1], z_dev[:, k, 1:2], ALU.subtract,
                                ALU.mult).then_inc(fin_done, 1)

            dve.wait_ge(w_in, 16)
            dve.wait_ge(qt_in, 16)
            V.tensor_tensor(wq_tap, over(w_s[:, W_Q:W_Q + P].unsqueeze(1), [P, 4, P]), q_tap,
                            ALU.mult).then_inc(wq_done, 1)
            dve.wait_ge(v_in, 16)
            for n in range(2 * B):
                older_taps(n)
                if n >= 2:
                    to_hc(n - 2)
                if n == B + 1:
                    for i in range(B):
                        dve.wait_ge(br_psum, i + 1)
                        V.transpose(gate_hc[:, i * C:(i + 1) * C, :].rearrange("p a b -> p (a b)"),
                                    ps[:, i, :]).then_inc(br_hc, 1)
            to_hc(2 * B - 2)
            to_hc(2 * B - 1)
            norms(0)
            unit_k(0)
            older_taps(2 * B)
            older_taps(2 * B + 1)
            dve.wait_ge(fir_psum, 4)
            triangles(0)
            triangles(1)
            turn_pairs(0)
            to_hc(2 * B)
            to_hc(2 * B + 1)
            to_hc(2 * B + 2)
            to_hc(2 * B + 3)
            dve.wait_ge(soft_a, 3)
            V.tensor_scalar(tmpv[:, 4:5], v_s[:, V_TEMP:V_TEMP + 1], 0.0, tmpv[:, 2:3], ALU.max,
                            ALU.add).then_inc(soft_b, 1)
            dve.wait_ge(soft_b, 1)
            V.reciprocal(tmpv[:, 5:6], tmpv[:, 4:5]).then_inc(soft_c, 1)
            dve.wait_ge(res_done, 2)
            V.tensor_scalar(sgate[:, :], row1[:, :], tmpv[:, 3:4], None, ALU.mult).then_inc(sgate_done, 1)
            dve.wait_ge(lm_in, 16)
            for n in range(LEVELS):
                level(0, n)
                if n == 0:
                    norms(1)
                    short_filter(0)
                if n == 1:
                    short_filter(1)
                if n == 2:
                    short_hc()
                    unit_k(1)
            dve.wait_ge(short_done, B)
            for c in range(C):
                scan_rhs(0, c)
                first_sum(c)
                scan_state(0, c)
            first_sum(C)
            first_sum(C + 1)
            dve.wait_ge(st_red, FIRST_SUMS)
            dve.wait_ge(stats_zero, 1)
            small_stats(0, 3, slice(0, BC), 0)
            scan_result(0)
            triangles(2)
            triangles(3)
            turn_pairs(1)
            gate_stats(0, 0)
            level(1, 0)
            softmax(0)
            mix(0)
            level(1, 1)
            gate_stats(0, 1)
            level(1, 2)
            factor(0)
            level(1, 3)
            dve.wait_ge(zero_set, 1)
            for c in range(C):
                scan_rhs(1, c)
                if c == 0:
                    norm_add(0)
                if c == 1:
                    norm_stats(0)
                if c == ROOT_AT:
                    norm_aggregate(0)
                if c == ROOT_AT + 2:
                    norm_scale(0)
                if c == ROOT_AT + 3:
                    norm_scale(1)
                if c == RANK_AT - 1:
                    sum_cut(0)
                if c == RANK_AT:
                    first_experts(0)
                if c == RANK_AT + 1:
                    tile_counts(0)
                if c == RANK_AT + 2:
                    places(0)
                if c == RANK_AT + 3:
                    tile_experts(0)
                scan_state(1, c)
            scan_result(1)
            gate_stats(1, 0)
            dve.wait_ge(w_all, 16 * (2 * NE + 1))
            dve.wait_ge(b2_done, 1)
            stages = (lambda: softmax(1), lambda: mix(1), lambda: gate_stats(1, 1), lambda: factor(1),
                      lambda: first_norm(1), lambda: (sum_cut(1), first_experts(1)),
                      lambda: (tile_counts(1), places(1), tile_experts(1)))

            def between(j):
                for at, stage in zip(DVE_AT, stages):
                    if at == j:
                        stage()

            dve.wait_ge(xs_in[0], 16 * 2)
            for j in range(2):
                with_bias(2 * j, fetch(0, 2 * j, 2 * j, slice(j, j + 1), 0), sorted_tile(0, j))
            for j in range(2, 4):
                fetch(0, 2 * j, 2 * j, slice(j, j + 1), 0)
            between(-1)

            def tile(g, j):
                u, ahead = (2 * j + 2 * g) % 4, None
                if g == 0 and j + 4 < SLOTS:
                    fetch(0, buffer(2 * j + 8, 0), 2 * j + 8, slice(j + 4, j + 5), 0)
                if g == 0 or j + 2 < SLOTS:
                    g_, j_ = (g, j + 2) if j + 2 < SLOTS else (1, j + 2 - SLOTS)
                    if g_ == 1:
                        e = fetch(1, u, 2 * j_, slice(j_, j_ + 1), STEPS)
                    else:
                        e = expert(mybir.EngineType.DVE, 0, 0, slice(j_, j_ + 1))
                    ahead = e, sorted_tile(g_, j_)
                if j >= 1:
                    finish((j - 1 + g) % 2, j - 1, sorted_tile(g, j - 1), g * STEPS)
                elif g == 1:
                    finish((SLOTS - 1) % 2, SLOTS - 1, sorted_tile(0, SLOTS - 1), 0)
                if g == 0:
                    between(2 * j)
                    if j + 2 == SLOTS:
                        dve.wait_ge(xs_in[1], 16 * 3)
                take(u, j, g * STEPS, ahead)

            for j in range(SLOTS):
                tile(0, j)
                between(2 * j + 1)
            tile(1, 0)

            def tile_of(row, k):
                return xs_half[:, bass.ds(row, 1), k * ROW:k * ROW + D].rearrange("p a d -> p (a d)")

            with dve.Fori(0, (SLOTS - 3) // 2) as r:
                for k in range(2):
                    u = 2 * k
                    e = fetch(1, u, r * 4 + (2 * k + 6), bass.ds(r * 2 + (k + 3), 1), STEPS)
                    finish(1 - k, r * 2 + k, tile_of(r, k), STEPS)
                    take(u, r * 2 + (k + 1), STEPS, (e, tile_of(r + (k + 1), 1 - k)))
            for j in range(SLOTS - 2, SLOTS):
                tile(1, j)
            finish(SLOTS % 2, SLOTS - 1, sorted_tile(1, SLOTS - 1), STEPS)

        @block.gpsimd
        def _(pool):
            gp = nc.gpsimd
            w5 = win[:, :, :, :].rearrange("p h (b c) d -> p h b (c d)", b=B)
            for h in range(H):
                z = gp.memset(w5[:, h, :, 0:2 * Q], 0.0)
            z.then_inc(win_zero, 1)
            gp.memset(zero[:, 0:D], 0.0)
            gp.memset(zero[:, D:ROW], float(N))
            gp.memset(ones[:, :], 1.0)
            gp.memset(me[:, :, :, :], 0.0).then_inc(zero_set, 1)
            gp.memset(epsv[:, 0:1], L2_EPS).then_inc(eps_set, 1)
            gp.memset(epsv[:, 1:2], EPS).then_inc(eps_set, 1)
            pool.wait_ge(w_in, 16)
            pool.wait_ge(v_in, 16)
            gp.tensor_scalar(w_s[:, W_GS:W_ALL], w_s[:, W_GS:W_ALL], 1.0 / H, None, ALU.mult).then_inc(ws_scaled, 1)
            gp.tensor_scalar(w_s[:, W_O:W_O + P], w_s[:, W_O:W_O + P], v_s[:, V_NORM:V_NORM + 1], None,
                             ALU.mult).then_inc(wo_scaled, 1)

            def squares(n):
                s, b = TAPS[n]
                src = (k_hc, q_hc)[s - 1][:, b * L:(b + 1) * L]
                pool.wait_ge(hc_done, n + 1)
                gp.tensor_tensor((k_sq, q_sq)[s - 1][:, b * L:(b + 1) * L], src, src, ALU.mult).then_inc(sq_done, 1)

            def beta_masks(g):
                pool.wait_ge(ssq_done, 2 * G * (g + 1))
                for b in group(g):
                    gp.tensor_tensor(hc(nbm)[:, b, :, :], over(nstrict, FULL),
                                     over(beta[:, b * C:(b + 1) * C].unsqueeze(2), FULL), ALU.mult).then_inc(nbm_done, 1)

            def pairs(g):
                for b in group(g):
                    pool.wait_ge(low_done, 2 * b + 2)
                    x_ = hc(inv)[:, b, :, :]
                    gp.tensor_tensor(x_, hc(low)[:, b, :, :], over(pair, FULL), ALU.mult).then_inc(pair_low, 1)
                    pool.wait_ge(pair_low, b + 1)
                    gp.tensor_tensor(x_, x_, over(eye, FULL), ALU.add).then_inc(pair_done, 1)

            def mix(g):
                pool.wait_ge(softmax_done, SM_STEPS * g + SM_STEPS - 1)
                pool.wait_ge(o_psum, (g + 1) * G)
                for b in group(g):
                    cs, ls = slice(b * C, (b + 1) * C), slice(b * L, (b + 1) * L)
                    gp.tensor_tensor(hc(mixA)[:, b, :, :], hc(v_hc[:, :])[:, b, :, :],
                                     over(prob[:, cs, 3].unsqueeze(2), FULL), ALU.mult).then_inc(mix_p, 1)
                    gp.tensor_tensor(hc(mixB)[:, b, :, :], hc(long[:, :])[:, b, :, :],
                                     over(prob[:, cs, 1].unsqueeze(2), FULL), ALU.mult).then_inc(mix_p, 1)
                    pool.wait_ge(mix_p, 3 * b + 2)
                    gp.tensor_tensor(mixA[:, ls], mixA[:, ls], mixB[:, ls], ALU.add).then_inc(mix_p, 1)

            pool.wait_ge(win_zero, 1)
            for g in range(2):
                pool.wait_ge(hc_done, G * (g + 1))
                for k in range(3):
                    dst, src = window(H - 1, k, g)
                    gp.dma_start(dst, src).then_inc(win3_in, 16)
            for n in range(B, 2 * B):
                squares(n)
            gp.memset(stats[:, :, :], 0.0).then_inc(stats_zero, 1)
            pool.wait_ge(c_in, 16)
            gp.tensor_copy(below[:, :], cst_s[:, C_LESS:C_LESS + P])
            gp.tensor_copy(x_tok[:, :, D], cst_s[:, C_TOKEN:C_TOKEN + NT]).then_inc(numbers, 1)
            pool.wait_ge(beta_done, 1)
            beta_masks(0)
            pairs(0)
            for n in range(2 * B, 3 * B):
                squares(n)
            beta_masks(1)
            pairs(1)
            mix(0)
            pool.wait_ge(b2_in, 16)
            gp.tensor_tensor(b2pair[:, 0:NE - 1, :], b2in[:, 0:NE - 1, :], b2in[:, 1:NE, :], ALU.add)
            gp.tensor_tensor(b2pair[:, NE - 1, :], b2in[:, NE - 1, :], b2in[:, 0, :], ALU.add).then_inc(pair_sum, 1)
            pool.wait_ge(pair_sum, 1)
            gp.tensor_scalar(b2pair, b2pair, 0.5, None, ALU.mult).then_inc(b2_done, 1)

            def scatter(g):
                pool.wait_ge(numbers, 1)
                pool.wait_ge(place_done, g + 1)
                pool.wait_ge(filled, 32)
                for n in range(g * GT, (g + 1) * GT):
                    gp.indirect_dma_start(sorted_in[g], bass.IndirectOffsetOnAxis(place_i[:, n:n + 1], 0),
                                          x_tok[:, n, :], None).then_inc(scattered[g], 16)

            def numbers_in(g):
                pool.wait_ge(xs_in[g], 16 * (2 + g))
                if g == 0:
                    src = kT_raw[:, 0:SLOTS * ROW].rearrange("p (n d) -> p n d", d=ROW)
                    gp.tensor_copy(token_i[:, g, 0:SLOTS], src[:, :, D]).then_inc(token_done, 1)
                else:
                    rows = SLOTS // 2
                    for k in range(2):
                        gp.tensor_copy(token_i[:, g, k:2 * rows:2], xs_half[:, 0:rows, k * ROW + D])
                    gp.tensor_copy(token_i[:, g, SLOTS - 1:SLOTS], xs_half[:, rows, D:ROW]).then_inc(token_done, 1)
                pool.wait_ge(token_done, g + 1)

            def results_out(g, j0, j1):
                for j in range(j0, j1):
                    pool.wait_ge(fin_done, g * SLOTS + j + 1)
                    gp.indirect_dma_start(out, bass.IndirectOffsetOnAxis(token_i[:, g, j:j + 1], 0),
                                          sorted_tile(g, j), None,
                                          bounds_check=N - 1, oob_is_err=False).then_inc(out_done, 16)

            scatter(0)
            numbers_in(0)
            mix(1)
            results_out(0, 0, EARLY)
            scatter(1)
            results_out(0, EARLY, SLOTS)
            numbers_in(1)
            results_out(1, 0, SLOTS)
            pool.wait_ge(out_done, 16 * 2 * SLOTS)


def toeplitz(taps):
    n = taps.shape[1]
    block = np.zeros((WIN, Q, P), taps.dtype)
    for i in range(Q):
        block[2 * Q + i - n + 1:2 * Q + i + 1, i, :] = taps.T
    return block.reshape(WIN, Q * P)


def laid_out(a):
    f = {k.replace("L0_attn_", "").replace("L0_ffn_", "f_"): np.asarray(v) for k, v in a.items()}
    z = np.float32
    wall = np.zeros((P, W_ALL), z)
    for at, name in ((W_Q, "Wq"), (W_K, "Wk"), (W_V, "Wv"), (W_O, "Wo")):
        wall[:, at:at + P] = f[name]
    wall[:, W_G:W_G + P] = f["Wg1"][:D]
    wall[:, W_OG:W_OG + 64] = f["Wog1"][:D]
    given = (0, 1, 3, 2)
    for h in range(H):
        wall[:, W_BR + h * Q] = f["Wb"][:, h]
        wall[:, W_BR + h * Q + 1] = f["Wres"][:, h]
        wall[:, W_G2 + h * Q:W_G2 + h * Q + 4] = f["Wg2"]
        wall[:64, W_OG2 + h * Q] = f["Wog2"][:, 0]
        for s in range(4):
            r = h * Q + 4 * s
            wall[r:r + 4, W_GS:W_GS + P] = f["Wg1"][D + 4 * given[s]:D + 4 * given[s] + 4]
        wall[h * Q + 4 * ST_O:h * Q + 4 * ST_O + 4, W_OGS:W_OGS + 64] = f["Wog1"][D:D + 4]
        wall[h * Q + 4 * ST_V:h * Q + 4 * ST_V + 4, W_OGS:W_OGS + 64] = f["Wog1"][D + 4:D + 8]
    vecs = np.zeros((P, V_ALL), z)
    for s, name in enumerate(("wv_conv", "wk_conv")):
        vecs[:, V_CONV + 4 * s:V_CONV + 4 * s + 4] = f[name]
    vecs[:, V_BG1] = f["bg1"]
    vecs[:64, V_BOG1] = f["bog1"]
    vecs[:, V_BG2:V_BG2 + 4] = f["bg2"]
    vecs[:, V_TEMP] = f["logit_temp"][0]
    vecs[:, V_BOG2] = f["bog2"][0]
    vecs[:, V_BRES] = np.repeat(f["bres"], Q)
    vecs[:, V_STATIC] = np.repeat(f["conv_res_logit"], Q)
    vecs[:, V_NORM] = np.tile(f["norm_w"], H)
    vecs[:, V_SHORT:V_SHORT + KS] = f["fir_short"].reshape(P, KS)
    fir_l = toeplitz(f["fir_long"].reshape(P, 64))
    cst, lmask = shape_constants()
    return {
        "x": f["hidden_states"].reshape(N, D), "cst": cst, "lmask": lmask, "wall": wall, "vecs": vecs,
        "q_taps": f["wq_conv"].reshape(P, 4)[:, ::-1].T,
        "fir_l": fir_l, "w1": f["f_W1"],
        "b1": f["f_b1"].reshape(NE, NF, P).transpose(0, 2, 1), "w2": f["f_W2"], "b2": f["f_b2"],
    }


def kernel(**inputs):
    import concourse.bacc as _bacc
    from concourse.bass_utils import run_bass_kernel_spmd as _run

    nc = _bacc.Bacc("TRN2", target_bir_lowering=False, num_devices=1)
    arrays, args = {}, []
    for name, a in laid_out(inputs).items():
        a = np.ascontiguousarray(a)
        arrays[f"in_{name}_dram"] = a
        args.append(nc.dram_tensor(f"in_{name}_dram", a.shape, mybir.dt.from_np(a.dtype), kind="ExternalInput").ap())
    args.append([nc.dram_tensor(f"sorted_in{g}", (SLOTS * P, ROW), F32, kind="Internal").ap() for g in range(2)])
    args.append(nc.dram_tensor("out_0_dram", (N, D), F32, kind="ExternalOutput").ap())
    post_ln_block(nc, *args)
    r = _run(nc, [arrays], core_ids=[0])
    return r.results[0]["out_0_dram"].reshape(B, L, D)
```
